# Optimizing a Trainium2 kernel written in Bass

```python
import numpy as np
import jax
import jax.numpy as jnp

def _softmax(x, axis=-1):
    return jax.nn.softmax(x, axis=axis)

def _gelu(x):
    return jax.nn.gelu(x, approximate=True)

def _silu(x):
    return jax.nn.silu(x)

def _sigmoid(x):
    return jax.nn.sigmoid(x)

def _layernorm(x, axis=-1, eps=1e-05):
    m = jnp.mean(x, axis=axis, keepdims=True)
    v = jnp.var(x, axis=axis, keepdims=True)
    return (x - m) / jnp.sqrt(v + eps)

def _scatter_add(tgt, idx, src, axis=0):
    return tgt.at[idx].add(src)

def _segment_sum(src, seg, n):
    return jax.ops.segment_sum(src, seg, n)
kernel_name = 'mk_xattn_ffn_d4_seqx_r8_213d5e'

def setup_inputs(seed: int=0):
    np.random.seed(seed)
    _w = jnp.asarray

    def _rec_inputs():
        import jax
        import jax.numpy as jnp
        _rk = jax.random.key(seed)
        x = -0.0002928 + 1 * jax.random.normal(jax.random.fold_in(_rk, 1), (32, 64, 128), jnp.float32)
        _lenS = 64 - jax.random.randint(jax.random.fold_in(_rk, 7), (32,), 0, max(1, 64 // 4) + 1, jnp.int32)
        _lenS2 = 64 - jax.random.randint(jax.random.fold_in(_rk, 8), (32,), 0, max(1, 64 // 4) + 1, jnp.int32)
        _ctx_1024P = jax.random.normal(jax.random.fold_in(_rk, 11), (32, 16, 128), jnp.float32)
        _ctx_1024c = jax.random.dirichlet(jax.random.fold_in(_rk, 511), 0.3 * jnp.ones((16,), jnp.float32), (32, 64))
        _ctx_1024t = jnp.einsum('bsk,bkd->bsd', _ctx_1024c, _ctx_1024P)
        _ctx_1024t = _ctx_1024t * jax.lax.rsqrt(jnp.mean(jnp.square(_ctx_1024t)) + 1e-12) * 0.953939
        ctx_1024 = -1.39393e-06 + 0.999914 * (_ctx_1024t + 0.3 * jax.random.normal(jax.random.fold_in(_rk, 611), (32, 64, 128), jnp.float32))
        _validS = jnp.arange(64)[None, :] < _lenS[:, None]
        _validS2 = jnp.arange(64)[None, :] < _lenS2[:, None]
        _causal = jnp.tril(jnp.ones((64, 64), dtype=bool))
        mask_SxS2_ff0 = jnp.where(jnp.ones((64, 64), dtype=bool), 0.0, -1000000000.0).astype(jnp.float32)
        return (x, ctx_1024, mask_SxS2_ff0)
    x, ctx_1024, mask_SxS2_ff0 = _rec_inputs()

    def _L0_xattn_setup():
        import jax, jax.numpy as jnp
        import numpy as np
        B, M, N = (2, 256, 256)
        K, P, Q, D = (16, 128, 128, 64)
        Pp, Qp, Dp = (P, Q, D)
        key = jax.random.key(seed)
        ks = jax.random.split(key, 10)
        s = 0.02
        return {'y_q': jax.random.normal(ks[0], (B, N, Qp), jnp.float32), 'x_kv': jax.random.normal(ks[1], (B, M, Pp), jnp.float32), 'mask': jnp.zeros((M, N), jnp.float32), 'Lx': jax.random.normal(ks[2], (K, Pp, Dp), jnp.float32) * s, 'Ly': jax.random.normal(ks[3], (K, Qp, Dp), jnp.float32) * s, 'Lo': jax.random.normal(ks[4], (1, K, 1, Dp), jnp.float32) * s, 'Tx': jax.random.normal(ks[5], (K, P, D), jnp.float32) * s, 'Ty': jax.random.normal(ks[6], (K, Q, D), jnp.float32) * s, 'To0': jax.random.normal(ks[7], (1, K, 1, D), jnp.float32) * s, 'To1': jax.random.normal(ks[8], (1, 1, Q), jnp.float32) * s}
    _L0_xattn_all = _L0_xattn_setup()
    _L0_xattn_in = {k: v for k, v in _L0_xattn_all.items() if k in ('Lx', 'Ly', 'Lo', 'Tx', 'Ty', 'To0', 'To1')}
    del _L0_xattn_all

    def _L0_ffn_setup():
        import jax, jax.numpy as jnp
        import numpy as np
        DIM = 128
        DEPTH = 6
        HEADS = 16
        DIM_HEAD = 64
        WINDOW = 32
        INNER = HEADS * DIM_HEAD
        DIM_INNER = int(DIM * 4 * 2 / 3)
        QK_SCALE = 8.0

        def shift_tokens(t):
            a, s = jnp.split(t, 2, -1)
            s = jnp.pad(s, ((0, 0), (1, 0), (0, 0)))[:, :-1]
            return jnp.concatenate([a, s], -1)

        def l2norm(t):
            return t / jnp.maximum(jnp.linalg.norm(t, axis=-1, keepdims=True), 1e-12)

        def rotate_half(x):
            x1, x2 = jnp.split(x, 2, -1)
            return jnp.concatenate([-x2, x1], -1)

        def rotary_tables(n):
            half = jnp.arange(0, DIM_HEAD, 2, dtype=jnp.float32)
            inv_freq = 1.0 / 10000.0 ** (half / DIM_HEAD)
            t = jnp.arange(n, dtype=jnp.float32)
            freqs = t[:, None] * inv_freq[None, :]
            freqs = jnp.concatenate([freqs, freqs], -1)
            base_scale = (half + 0.4 * DIM_HEAD) / (1.4 * DIM_HEAD)
            power = (t - n // 2) / (WINDOW // 2)
            scale = base_scale[None, :] ** power[:, None]
            scale = jnp.concatenate([scale, scale], -1)
            return (freqs, scale)

        def local_attention(q, k, v):
            b, h, n, d = q.shape
            w = WINDOW
            nw = n // w
            bq = q.reshape(b, h, nw, w, d)
            bk = k.reshape(b, h, nw, w, d)
            bv = v.reshape(b, h, nw, w, d)

            def look(t):
                p = jnp.pad(t, ((0, 0), (0, 0), (1, 0), (0, 0), (0, 0)))
                return jnp.concatenate([p[:, :, :nw], p[:, :, 1:]], axis=3)
            bk2, bv2 = (look(bk), look(bv))
            seq = jnp.arange(n).reshape(nw, w)
            seq_p = jnp.pad(seq, ((1, 0), (0, 0)), constant_values=-1)
            jt = jnp.concatenate([seq_p[:nw], seq_p[1:]], axis=1)
            it = seq[:, :, None]
            jb = jt[:, None, :]
            mask = (it < jb) | (it > jb + w) | (jb == -1)
            sim = jnp.einsum('bhwie,bhwje->bhwij', bq, bk2) * QK_SCALE
            sim = jnp.where(mask, -jnp.finfo(sim.dtype).max, sim)
            attn = jax.nn.softmax(sim, -1)
            out = jnp.einsum('bhwij,bhwje->bhwie', attn, bv2)
            return out.reshape(b, h, n, d)

        def attn_layer(x, Wqkv, qs, ksc, Wo):
            b, n, _ = x.shape
            qkv = x @ Wqkv
            q, k, v = jnp.split(qkv, 3, -1)
            sh = lambda t: t.reshape(b, n, HEADS, DIM_HEAD).transpose(0, 2, 1, 3)
            q, k, v = (sh(q), sh(k), sh(v))
            q = l2norm(q) * qs
            k = l2norm(k) * ksc
            freqs, scale = rotary_tables(n)
            cos, sin = (jnp.cos(freqs), jnp.sin(freqs))
            q = q * cos * scale + rotate_half(q) * sin * scale
            inv = 1.0 / scale
            k = k * cos * inv + rotate_half(k) * sin * inv
            out = local_attention(q, k, v)
            out = out.transpose(0, 2, 1, 3).reshape(b, n, INNER)
            return out @ Wo

        def ffn_layer(x, g, bln, W1, b1, W2, b2):
            mu = x.mean(-1, keepdims=True)
            var = ((x - mu) ** 2).mean(-1, keepdims=True)
            xn = (x - mu) / jnp.sqrt(var + 1e-05) * g + bln
            hg = xn @ W1 + b1
            a, gate = jnp.split(hg, 2, -1)
            return a * jax.nn.gelu(gate, approximate=False) @ W2 + b2
        key = jax.random.key(seed)
        ks = jax.random.split(key, 8)
        B, N = (2, 256)
        init = lambda k, shape: jax.random.normal(k, shape, jnp.float32) * 0.02
        return {'x': jax.random.normal(ks[0], (B, N, DIM), jnp.float32), 'Wqkv': init(ks[1], (DEPTH, DIM, 3 * INNER)), 'q_scale': jnp.ones((DEPTH, DIM_HEAD), jnp.float32), 'k_scale': jnp.ones((DEPTH, DIM_HEAD), jnp.float32), 'Wo': init(ks[2], (DEPTH, INNER, DIM)), 'ln_g': jnp.ones((DEPTH, DIM), jnp.float32), 'ln_b': jnp.zeros((DEPTH, DIM), jnp.float32), 'W1': init(ks[3], (DEPTH, DIM, 2 * DIM_INNER)), 'b1': jnp.zeros((DEPTH, 2 * DIM_INNER), jnp.float32), 'W2': init(ks[4], (DEPTH, DIM_INNER, DIM)), 'b2': jnp.zeros((DEPTH, DIM), jnp.float32)}
    _L0_ffn_all = _L0_ffn_setup()
    _L0_ffn_in = {k: v for k, v in _L0_ffn_all.items() if k in ('Wqkv', 'q_scale', 'k_scale', 'Wo', 'ln_g', 'ln_b', 'W1', 'b1', 'W2', 'b2')}
    del _L0_ffn_all

    def _L1_xattn_setup():
        import jax, jax.numpy as jnp
        import numpy as np
        import math
        D_MODEL = 128
        N_HEAD = 16

        def _split_heads(x, n_head):
            B, S, D = x.shape
            return x.reshape(B, S, n_head, D // n_head).transpose(0, 2, 1, 3)
        key = jax.random.key(seed)
        ks = jax.random.split(key, 11)
        B, S, D = (2, 256, D_MODEL)
        s = 1.0 / math.sqrt(D)
        return {'q': jax.random.normal(ks[0], (B, S, D), dtype=jnp.float32), 'k': jax.random.normal(ks[1], (B, S, D), dtype=jnp.float32), 'v': jax.random.normal(ks[2], (B, S, D), dtype=jnp.float32), 'w_q': jax.random.normal(ks[3], (D, D), dtype=jnp.float32) * s, 'b_q': jnp.zeros((D,), dtype=jnp.float32), 'w_k': jax.random.normal(ks[4], (D, D), dtype=jnp.float32) * s, 'b_k': jnp.zeros((D,), dtype=jnp.float32), 'w_v': jax.random.normal(ks[5], (D, D), dtype=jnp.float32) * s, 'b_v': jnp.zeros((D,), dtype=jnp.float32), 'w_out': jax.random.normal(ks[6], (D, D), dtype=jnp.float32) * s, 'b_out': jnp.zeros((D,), dtype=jnp.float32)}
    _L1_xattn_all = _L1_xattn_setup()
    _L1_xattn_in = {k: v for k, v in _L1_xattn_all.items() if k in ('w_q', 'b_q', 'w_k', 'b_k', 'w_v', 'b_v', 'w_out', 'b_out')}
    del _L1_xattn_all

    def _L1_ffn_setup():
        import jax, jax.numpy as jnp
        import numpy as np
        FP8_MAX = 448.0
        FP8 = jnp.float8_e4m3fn
        key = jax.random.key(seed)
        kx, kw, kb = jax.random.split(key, 3)
        B, S, D_in, D_out = (4, 1024, 128, 128)
        x = jax.random.normal(kx, (B, S, D_in), dtype=jnp.float32)
        w = jax.random.normal(kw, (D_out, D_in), dtype=jnp.float32) * 0.02
        weight_scale = jnp.maximum(jnp.max(jnp.abs(w)), 1e-12) / FP8_MAX
        weight = (w / weight_scale).astype(FP8)
        bias = jax.random.normal(kb, (D_out,), dtype=jnp.float32) * 0.01
        return {'x': x, 'weight': weight, 'weight_scale': weight_scale, 'bias': bias}
    _L1_ffn_all = _L1_ffn_setup()
    _L1_ffn_in = {k: v for k, v in _L1_ffn_all.items() if k in ('weight', 'weight_scale', 'bias')}
    del _L1_ffn_all

    def _L2_xattn_setup():
        import jax, jax.numpy as jnp
        import numpy as np
        E = 128
        H = 16
        D = E // H

        def _split_heads(x):
            B, S, _ = x.shape
            return x.reshape(B, S, H, D).transpose(0, 2, 1, 3)
        key = jax.random.key(seed)
        ks = jax.random.split(key, 8)
        B, S = (4, 256)
        scale = 1.0 / np.sqrt(E)
        return {'Q': jax.random.normal(ks[0], (B, S, E), jnp.float32), 'K': jax.random.normal(ks[1], (B, S, E), jnp.float32), 'V': jax.random.normal(ks[2], (B, S, E), jnp.float32), 'Wq': jax.random.normal(ks[3], (E, E), jnp.float32) * scale, 'Wk': jax.random.normal(ks[4], (E, E), jnp.float32) * scale, 'Wv': jax.random.normal(ks[5], (E, E), jnp.float32) * scale, 'Wo': jax.random.normal(ks[6], (E, E), jnp.float32) * scale, 'bo': jax.random.normal(ks[7], (E,), jnp.float32) * 0.01}
    _L2_xattn_all = _L2_xattn_setup()
    _L2_xattn_in = {k: v for k, v in _L2_xattn_all.items() if k in ('Wq', 'Wk', 'Wv', 'Wo', 'bo')}
    del _L2_xattn_all

    def _L2_ffn_setup():
        import jax, jax.numpy as jnp
        import numpy as np
        import math
        N_EMBD = 128
        HIDDEN = 4 * N_EMBD
        N_EXPERTS = 8
        TOP_K = 2
        B, T = (4, 256)

        def new_gelu(x):
            c = math.sqrt(2.0 / math.pi)
            return 0.5 * x * (1.0 + jnp.tanh(c * (x + 0.044715 * x * x * x)))

        def _moe_forward(x, Wfc_s, bfc_s, Wproj_s, bproj_s, Wr, Wfc, bfc, Wproj, bproj):
            Bb, Tt, C = x.shape
            xf = x.reshape(Bb * Tt, C)
            N = Bb * Tt
            shared = new_gelu(xf @ Wfc_s + bfc_s) @ Wproj_s + bproj_s
            logits = xf @ Wr
            probs = jax.nn.softmax(logits, axis=-1)
            topk_p, topk_i = jax.lax.top_k(probs, TOP_K)
            topk_p = topk_p / jnp.sum(topk_p, axis=-1, keepdims=True)
            gate = jnp.zeros((N, N_EXPERTS), dtype=xf.dtype)
            gate = gate.at[jnp.arange(N)[:, None], topk_i].add(topk_p)
            routed = jnp.zeros_like(xf)
            for e in range(N_EXPERTS):
                h = new_gelu(xf @ Wfc[e] + bfc[e]) @ Wproj[e] + bproj[e]
                routed = routed + h * gate[:, e:e + 1]
            return (shared + routed).reshape(Bb, Tt, C)
        key = jax.random.key(seed)
        ks = jax.random.split(key, 10)
        s = 0.02
        return {'x': jax.random.normal(ks[0], (B, T, N_EMBD), dtype=jnp.float32), 'Wfc_s': jax.random.normal(ks[1], (N_EMBD, HIDDEN), dtype=jnp.float32) * s, 'bfc_s': jnp.zeros((HIDDEN,), dtype=jnp.float32), 'Wproj_s': jax.random.normal(ks[2], (HIDDEN, N_EMBD), dtype=jnp.float32) * s, 'bproj_s': jnp.zeros((N_EMBD,), dtype=jnp.float32), 'Wr': jax.random.normal(ks[3], (N_EMBD, N_EXPERTS), dtype=jnp.float32) * s, 'Wfc': jax.random.normal(ks[4], (N_EXPERTS, N_EMBD, HIDDEN), dtype=jnp.float32) * s, 'bfc': jnp.zeros((N_EXPERTS, HIDDEN), dtype=jnp.float32), 'Wproj': jax.random.normal(ks[5], (N_EXPERTS, HIDDEN, N_EMBD), dtype=jnp.float32) * s, 'bproj': jnp.zeros((N_EXPERTS, N_EMBD), dtype=jnp.float32)}
    _L2_ffn_all = _L2_ffn_setup()
    _L2_ffn_in = {k: v for k, v in _L2_ffn_all.items() if k in ('Wfc_s', 'bfc_s', 'Wproj_s', 'bproj_s', 'Wr', 'Wfc', 'bfc', 'Wproj', 'bproj')}
    del _L2_ffn_all

    def _L3_xattn_setup():
        import jax, jax.numpy as jnp
        import numpy as np
        EMBED_DIM = 128
        NUM_HEADS = 16
        HEAD_DIM = EMBED_DIM // NUM_HEADS
        SCALE = 1.0 / np.sqrt(HEAD_DIM)

        def _quant_linear(x, w, b):
            s = jnp.max(jnp.abs(w)) / 127.0
            w_dq = jnp.clip(jnp.round(w / s), -128.0, 127.0) * s
            return jnp.einsum('bse,oe->bso', x, w_dq) + b
        key = jax.random.key(seed)
        ks = jax.random.split(key, 7)
        B, S, E = (2, 256, EMBED_DIM)
        return {'query': jax.random.normal(ks[0], (B, S, E), dtype=jnp.float32), 'key': jax.random.normal(ks[1], (B, S, E), dtype=jnp.float32), 'value': jax.random.normal(ks[2], (B, S, E), dtype=jnp.float32), 'Wq': jax.random.normal(ks[3], (E, E), dtype=jnp.float32) * 0.02, 'bq': jnp.zeros((E,), dtype=jnp.float32), 'Wk': jax.random.normal(ks[4], (E, E), dtype=jnp.float32) * 0.02, 'bk': jnp.zeros((E,), dtype=jnp.float32), 'Wv': jax.random.normal(ks[5], (E, E), dtype=jnp.float32) * 0.02, 'bv': jnp.zeros((E,), dtype=jnp.float32), 'Wo': jax.random.normal(ks[6], (E, E), dtype=jnp.float32) * 0.02, 'bo': jnp.zeros((E,), dtype=jnp.float32)}
    _L3_xattn_all = _L3_xattn_setup()
    _L3_xattn_in = {k: v for k, v in _L3_xattn_all.items() if k in ('Wq', 'bq', 'Wk', 'bk', 'Wv', 'bv', 'Wo', 'bo')}
    del _L3_xattn_all

    def _L3_ffn_setup():
        import jax, jax.numpy as jnp
        import numpy as np
        EPS = 1e-12

        def _l2norm(v):
            n = jnp.sqrt(jnp.sum(v * v, axis=-1, keepdims=True))
            return v / jnp.maximum(n, EPS)
        key = jax.random.key(seed)
        ks = jax.random.split(key, 6)
        B, S, D, F, E = (2, 256, 128, 512, 8)
        std = 0.02
        return {'x': jax.random.normal(ks[0], (B, S, D), jnp.float32), 'Wp': jax.random.normal(ks[1], (D, D), jnp.float32) * (1.0 / np.sqrt(D)), 'sim_matrix': jax.random.normal(ks[2], (E, D), jnp.float32) * std, 'temperature': jnp.asarray(1.0, jnp.float32), 'W1': jax.random.normal(ks[3], (E, D, F), jnp.float32) * (1.0 / np.sqrt(D)), 'b1': jnp.zeros((E, F), jnp.float32), 'W2': jax.random.normal(ks[4], (E, F, D), jnp.float32) * (1.0 / np.sqrt(F)), 'b2': jnp.zeros((E, D), jnp.float32)}
    _L3_ffn_all = _L3_ffn_setup()
    _L3_ffn_in = {k: v for k, v in _L3_ffn_all.items() if k in ('Wp', 'sim_matrix', 'temperature', 'W1', 'b1', 'W2', 'b2')}
    del _L3_ffn_all
    return {'x': x, 'ctx_1024': ctx_1024, 'mask_SxS2_ff0': mask_SxS2_ff0, 'L0_xattn_Lx': _L0_xattn_in['Lx'], 'L0_xattn_Ly': _L0_xattn_in['Ly'], 'L0_xattn_Lo': _L0_xattn_in['Lo'], 'L0_xattn_Tx': _L0_xattn_in['Tx'], 'L0_xattn_Ty': _L0_xattn_in['Ty'], 'L0_xattn_To0': _L0_xattn_in['To0'], 'L0_xattn_To1': _L0_xattn_in['To1'], 'L0_ffn_Wqkv': _L0_ffn_in['Wqkv'], 'L0_ffn_q_scale': _L0_ffn_in['q_scale'], 'L0_ffn_k_scale': _L0_ffn_in['k_scale'], 'L0_ffn_Wo': _L0_ffn_in['Wo'], 'L0_ffn_ln_g': _L0_ffn_in['ln_g'], 'L0_ffn_ln_b': _L0_ffn_in['ln_b'], 'L0_ffn_W1': _L0_ffn_in['W1'], 'L0_ffn_b1': _L0_ffn_in['b1'], 'L0_ffn_W2': _L0_ffn_in['W2'], 'L0_ffn_b2': _L0_ffn_in['b2'], 'L1_xattn_w_q': _L1_xattn_in['w_q'], 'L1_xattn_b_q': _L1_xattn_in['b_q'], 'L1_xattn_w_k': _L1_xattn_in['w_k'], 'L1_xattn_b_k': _L1_xattn_in['b_k'], 'L1_xattn_w_v': _L1_xattn_in['w_v'], 'L1_xattn_b_v': _L1_xattn_in['b_v'], 'L1_xattn_w_out': _L1_xattn_in['w_out'], 'L1_xattn_b_out': _L1_xattn_in['b_out'], 'L1_ffn_weight': _L1_ffn_in['weight'], 'L1_ffn_weight_scale': _L1_ffn_in['weight_scale'], 'L1_ffn_bias': _L1_ffn_in['bias'], 'L2_xattn_Wq': _L2_xattn_in['Wq'], 'L2_xattn_Wk': _L2_xattn_in['Wk'], 'L2_xattn_Wv': _L2_xattn_in['Wv'], 'L2_xattn_Wo': _L2_xattn_in['Wo'], 'L2_xattn_bo': _L2_xattn_in['bo'], 'L2_ffn_Wfc_s': _L2_ffn_in['Wfc_s'], 'L2_ffn_bfc_s': _L2_ffn_in['bfc_s'], 'L2_ffn_Wproj_s': _L2_ffn_in['Wproj_s'], 'L2_ffn_bproj_s': _L2_ffn_in['bproj_s'], 'L2_ffn_Wr': _L2_ffn_in['Wr'], 'L2_ffn_Wfc': _L2_ffn_in['Wfc'], 'L2_ffn_bfc': _L2_ffn_in['bfc'], 'L2_ffn_Wproj': _L2_ffn_in['Wproj'], 'L2_ffn_bproj': _L2_ffn_in['bproj'], 'L3_xattn_Wq': _L3_xattn_in['Wq'], 'L3_xattn_bq': _L3_xattn_in['bq'], 'L3_xattn_Wk': _L3_xattn_in['Wk'], 'L3_xattn_bk': _L3_xattn_in['bk'], 'L3_xattn_Wv': _L3_xattn_in['Wv'], 'L3_xattn_bv': _L3_xattn_in['bv'], 'L3_xattn_Wo': _L3_xattn_in['Wo'], 'L3_xattn_bo': _L3_xattn_in['bo'], 'L3_ffn_Wp': _L3_ffn_in['Wp'], 'L3_ffn_sim_matrix': _L3_ffn_in['sim_matrix'], 'L3_ffn_temperature': _L3_ffn_in['temperature'], 'L3_ffn_W1': _L3_ffn_in['W1'], 'L3_ffn_b1': _L3_ffn_in['b1'], 'L3_ffn_W2': _L3_ffn_in['W2'], 'L3_ffn_b2': _L3_ffn_in['b2']}

def reference(x, ctx_1024, mask_SxS2_ff0, L0_xattn_Lx, L0_xattn_Ly, L0_xattn_Lo, L0_xattn_Tx, L0_xattn_Ty, L0_xattn_To0, L0_xattn_To1, L0_ffn_Wqkv, L0_ffn_q_scale, L0_ffn_k_scale, L0_ffn_Wo, L0_ffn_ln_g, L0_ffn_ln_b, L0_ffn_W1, L0_ffn_b1, L0_ffn_W2, L0_ffn_b2, L1_xattn_w_q, L1_xattn_b_q, L1_xattn_w_k, L1_xattn_b_k, L1_xattn_w_v, L1_xattn_b_v, L1_xattn_w_out, L1_xattn_b_out, L1_ffn_weight, L1_ffn_weight_scale, L1_ffn_bias, L2_xattn_Wq, L2_xattn_Wk, L2_xattn_Wv, L2_xattn_Wo, L2_xattn_bo, L2_ffn_Wfc_s, L2_ffn_bfc_s, L2_ffn_Wproj_s, L2_ffn_bproj_s, L2_ffn_Wr, L2_ffn_Wfc, L2_ffn_bfc, L2_ffn_Wproj, L2_ffn_bproj, L3_xattn_Wq, L3_xattn_bq, L3_xattn_Wk, L3_xattn_bk, L3_xattn_Wv, L3_xattn_bv, L3_xattn_Wo, L3_xattn_bo, L3_ffn_Wp, L3_ffn_sim_matrix, L3_ffn_temperature, L3_ffn_W1, L3_ffn_b1, L3_ffn_W2, L3_ffn_b2):
    import jax
    import jax.numpy as jnp

    def _L0_xattn_ref(y_q, x_kv, mask, Lx, Ly, Lo, Tx, Ty, To0, To1):
        import jax, jax.numpy as jnp
        import numpy as np
        B, M, N = (2, 256, 256)
        K, P, Q, D = (16, 128, 128, 64)
        Pp, Qp, Dp = (P, Q, D)
        temp = jnp.sqrt(jnp.asarray(Dp, y_q.dtype))
        q = jnp.einsum('bnq,kqd->bknd', y_q, Ly) + Lo
        scores = jnp.einsum('bknd,bmp,kpd->bkmn', q, x_kv, Lx)
        scores = scores + mask[None, None, :, :]
        a = jax.nn.softmax(scores / temp, axis=-2)
        xt = jnp.einsum('bmp,kpd->bkmd', x_kv, Tx) + To0
        out = jnp.einsum('bkmn,bkmd,kqd->bnq', a, xt, Ty) + To1
        return out

    def _L0_ffn_ref(x, Wqkv, q_scale, k_scale, Wo, ln_g, ln_b, W1, b1, W2, b2):
        import jax, jax.numpy as jnp
        import numpy as np
        DIM = 128
        DEPTH = 6
        HEADS = 16
        DIM_HEAD = 64
        WINDOW = 32
        INNER = HEADS * DIM_HEAD
        DIM_INNER = int(DIM * 4 * 2 / 3)
        QK_SCALE = 8.0

        def shift_tokens(t):
            a, s = jnp.split(t, 2, -1)
            s = jnp.pad(s, ((0, 0), (1, 0), (0, 0)))[:, :-1]
            return jnp.concatenate([a, s], -1)

        def l2norm(t):
            return t / jnp.maximum(jnp.linalg.norm(t, axis=-1, keepdims=True), 1e-12)

        def rotate_half(x):
            x1, x2 = jnp.split(x, 2, -1)
            return jnp.concatenate([-x2, x1], -1)

        def rotary_tables(n):
            half = jnp.arange(0, DIM_HEAD, 2, dtype=jnp.float32)
            inv_freq = 1.0 / 10000.0 ** (half / DIM_HEAD)
            t = jnp.arange(n, dtype=jnp.float32)
            freqs = t[:, None] * inv_freq[None, :]
            freqs = jnp.concatenate([freqs, freqs], -1)
            base_scale = (half + 0.4 * DIM_HEAD) / (1.4 * DIM_HEAD)
            power = (t - n // 2) / (WINDOW // 2)
            scale = base_scale[None, :] ** power[:, None]
            scale = jnp.concatenate([scale, scale], -1)
            return (freqs, scale)

        def local_attention(q, k, v):
            b, h, n, d = q.shape
            w = WINDOW
            nw = n // w
            bq = q.reshape(b, h, nw, w, d)
            bk = k.reshape(b, h, nw, w, d)
            bv = v.reshape(b, h, nw, w, d)

            def look(t):
                p = jnp.pad(t, ((0, 0), (0, 0), (1, 0), (0, 0), (0, 0)))
                return jnp.concatenate([p[:, :, :nw], p[:, :, 1:]], axis=3)
            bk2, bv2 = (look(bk), look(bv))
            seq = jnp.arange(n).reshape(nw, w)
            seq_p = jnp.pad(seq, ((1, 0), (0, 0)), constant_values=-1)
            jt = jnp.concatenate([seq_p[:nw], seq_p[1:]], axis=1)
            it = seq[:, :, None]
            jb = jt[:, None, :]
            mask = (it < jb) | (it > jb + w) | (jb == -1)
            sim = jnp.einsum('bhwie,bhwje->bhwij', bq, bk2) * QK_SCALE
            sim = jnp.where(mask, -jnp.finfo(sim.dtype).max, sim)
            attn = jax.nn.softmax(sim, -1)
            out = jnp.einsum('bhwij,bhwje->bhwie', attn, bv2)
            return out.reshape(b, h, n, d)

        def attn_layer(x, Wqkv, qs, ksc, Wo):
            b, n, _ = x.shape
            qkv = x @ Wqkv
            q, k, v = jnp.split(qkv, 3, -1)
            sh = lambda t: t.reshape(b, n, HEADS, DIM_HEAD).transpose(0, 2, 1, 3)
            q, k, v = (sh(q), sh(k), sh(v))
            q = l2norm(q) * qs
            k = l2norm(k) * ksc
            freqs, scale = rotary_tables(n)
            cos, sin = (jnp.cos(freqs), jnp.sin(freqs))
            q = q * cos * scale + rotate_half(q) * sin * scale
            inv = 1.0 / scale
            k = k * cos * inv + rotate_half(k) * sin * inv
            out = local_attention(q, k, v)
            out = out.transpose(0, 2, 1, 3).reshape(b, n, INNER)
            return out @ Wo

        def ffn_layer(x, g, bln, W1, b1, W2, b2):
            mu = x.mean(-1, keepdims=True)
            var = ((x - mu) ** 2).mean(-1, keepdims=True)
            xn = (x - mu) / jnp.sqrt(var + 1e-05) * g + bln
            hg = xn @ W1 + b1
            a, gate = jnp.split(hg, 2, -1)
            return a * jax.nn.gelu(gate, approximate=False) @ W2 + b2
        for i in range(DEPTH):
            x = attn_layer(shift_tokens(x), Wqkv[i], q_scale[i], k_scale[i], Wo[i]) + x
            x = ffn_layer(shift_tokens(x), ln_g[i], ln_b[i], W1[i], b1[i], W2[i], b2[i]) + x
        return x

    def _L1_xattn_ref(q, k, v, w_q, b_q, w_k, b_k, w_v, b_v, w_out, b_out):
        import jax, jax.numpy as jnp
        import numpy as np
        import math
        D_MODEL = 128
        N_HEAD = 16

        def _split_heads(x, n_head):
            B, S, D = x.shape
            return x.reshape(B, S, n_head, D // n_head).transpose(0, 2, 1, 3)
        qh = _split_heads(q @ w_q + b_q, N_HEAD)
        kh = _split_heads(k @ w_k + b_k, N_HEAD)
        vh = _split_heads(v @ w_v + b_v, N_HEAD)
        d_k = qh.shape[-1]
        scores = jnp.einsum('bhqd,bhkd->bhqk', qh, kh) / jnp.sqrt(jnp.float32(d_k))
        attn = jax.nn.softmax(scores, axis=-1)
        context = jnp.einsum('bhqk,bhkd->bhqd', attn, vh)
        B, H, S, dk = context.shape
        context = context.transpose(0, 2, 1, 3).reshape(B, S, H * dk)
        return context @ w_out + b_out

    def _L1_ffn_ref(x, weight, weight_scale, bias):
        import jax, jax.numpy as jnp
        import numpy as np
        FP8_MAX = 448.0
        FP8 = jnp.float8_e4m3fn
        amax = jnp.max(jnp.abs(x), axis=-1, keepdims=True)
        x_scale = jnp.maximum(amax, 1e-12) / FP8_MAX
        qinput = (x / x_scale).astype(FP8)
        A = qinput.astype(x.dtype) * x_scale
        Bm = weight.astype(x.dtype) * weight_scale
        out = jnp.einsum('bsk,nk->bsn', A, Bm) + bias
        return out.astype(x.dtype)

    def _L2_xattn_ref(Q, K, V, Wq, Wk, Wv, Wo, bo):
        import jax, jax.numpy as jnp
        import numpy as np
        E = 128
        H = 16
        D = E // H

        def _split_heads(x):
            B, S, _ = x.shape
            return x.reshape(B, S, H, D).transpose(0, 2, 1, 3)
        q = _split_heads(Q @ Wq.T)
        k = _split_heads(K @ Wk.T)
        v = _split_heads(V @ Wv.T)
        scores = jnp.einsum('bhqd,bhkd->bhqk', q, k)
        attn = jax.nn.softmax(scores, axis=-1)
        out = jnp.einsum('bhqk,bhkd->bhqd', attn, v)
        B, _, Sq, _ = out.shape
        out = out.transpose(0, 2, 1, 3).reshape(B, Sq, E)
        return out @ Wo.T + bo

    def _L2_ffn_ref(x, Wfc_s, bfc_s, Wproj_s, bproj_s, Wr, Wfc, bfc, Wproj, bproj):
        import jax, jax.numpy as jnp
        import numpy as np
        import math
        N_EMBD = 128
        HIDDEN = 4 * N_EMBD
        N_EXPERTS = 8
        TOP_K = 2
        B, T = (4, 256)

        def new_gelu(x):
            c = math.sqrt(2.0 / math.pi)
            return 0.5 * x * (1.0 + jnp.tanh(c * (x + 0.044715 * x * x * x)))

        def _moe_forward(x, Wfc_s, bfc_s, Wproj_s, bproj_s, Wr, Wfc, bfc, Wproj, bproj):
            Bb, Tt, C = x.shape
            xf = x.reshape(Bb * Tt, C)
            N = Bb * Tt
            shared = new_gelu(xf @ Wfc_s + bfc_s) @ Wproj_s + bproj_s
            logits = xf @ Wr
            probs = jax.nn.softmax(logits, axis=-1)
            topk_p, topk_i = jax.lax.top_k(probs, TOP_K)
            topk_p = topk_p / jnp.sum(topk_p, axis=-1, keepdims=True)
            gate = jnp.zeros((N, N_EXPERTS), dtype=xf.dtype)
            gate = gate.at[jnp.arange(N)[:, None], topk_i].add(topk_p)
            routed = jnp.zeros_like(xf)
            for e in range(N_EXPERTS):
                h = new_gelu(xf @ Wfc[e] + bfc[e]) @ Wproj[e] + bproj[e]
                routed = routed + h * gate[:, e:e + 1]
            return (shared + routed).reshape(Bb, Tt, C)
        return _moe_forward(x, Wfc_s, bfc_s, Wproj_s, bproj_s, Wr, Wfc, bfc, Wproj, bproj)

    def _L3_xattn_ref(query, key, value, Wq, bq, Wk, bk, Wv, bv, Wo, bo):
        import jax, jax.numpy as jnp
        import numpy as np
        EMBED_DIM = 128
        NUM_HEADS = 16
        HEAD_DIM = EMBED_DIM // NUM_HEADS
        SCALE = 1.0 / np.sqrt(HEAD_DIM)

        def _quant_linear(x, w, b):
            s = jnp.max(jnp.abs(w)) / 127.0
            w_dq = jnp.clip(jnp.round(w / s), -128.0, 127.0) * s
            return jnp.einsum('bse,oe->bso', x, w_dq) + b
        B, S, E = query.shape
        H, D = (NUM_HEADS, HEAD_DIM)
        Q = _quant_linear(query, Wq, bq).reshape(B, S, H, D).transpose(0, 2, 1, 3)
        K = _quant_linear(key, Wk, bk).reshape(B, S, H, D).transpose(0, 2, 1, 3)
        V = _quant_linear(value, Wv, bv).reshape(B, S, H, D).transpose(0, 2, 1, 3)
        scores = jnp.einsum('bhqd,bhkd->bhqk', Q, K) * SCALE
        attn = jax.nn.softmax(scores, axis=-1)
        out = jnp.einsum('bhqk,bhkd->bhqd', attn, V)
        out = out.transpose(0, 2, 1, 3).reshape(B, S, E)
        return _quant_linear(out, Wo, bo)

    def _L3_ffn_ref(x, Wp, sim_matrix, temperature, W1, b1, W2, b2):
        import jax, jax.numpy as jnp
        import numpy as np
        EPS = 1e-12

        def _l2norm(v):
            n = jnp.sqrt(jnp.sum(v * v, axis=-1, keepdims=True))
            return v / jnp.maximum(n, EPS)
        E = sim_matrix.shape[0]
        top_k = 2
        proj = jnp.einsum('bsd,ed->bse', x, Wp)
        pn = _l2norm(proj)
        sn = _l2norm(sim_matrix)
        gate_scores = jnp.einsum('bsd,ed->bse', pn, sn) / temperature
        top_v, top_i = jax.lax.top_k(gate_scores, top_k)
        gate_probs = jax.nn.softmax(top_v, axis=-1)
        comb = jnp.sum(jax.nn.one_hot(top_i, E, dtype=x.dtype) * gate_probs[..., None], axis=-2)
        h = jax.nn.gelu(jnp.einsum('bsd,edf->ebsf', x, W1) + b1[:, None, None, :], approximate=False)
        eo = jnp.einsum('ebsf,efd->ebsd', h, W2) + b2[:, None, None, :]
        out = jnp.einsum('ebsd,bse->bsd', eo, comb)
        return out
    x = x + _L0_xattn_ref(_layernorm(x, axis=-1), ctx_1024, mask_SxS2_ff0, L0_xattn_Lx, L0_xattn_Ly, L0_xattn_Lo, L0_xattn_Tx, L0_xattn_Ty, L0_xattn_To0, L0_xattn_To1)
    x = x + _L0_ffn_ref(_layernorm(x, axis=-1), L0_ffn_Wqkv, L0_ffn_q_scale, L0_ffn_k_scale, L0_ffn_Wo, L0_ffn_ln_g, L0_ffn_ln_b, L0_ffn_W1, L0_ffn_b1, L0_ffn_W2, L0_ffn_b2)
    x = x + _L1_xattn_ref(_layernorm(x, axis=-1), ctx_1024, ctx_1024, L1_xattn_w_q, L1_xattn_b_q, L1_xattn_w_k, L1_xattn_b_k, L1_xattn_w_v, L1_xattn_b_v, L1_xattn_w_out, L1_xattn_b_out)
    x = x + _L1_ffn_ref(_layernorm(x, axis=-1), L1_ffn_weight, L1_ffn_weight_scale, L1_ffn_bias)
    x = x + _L2_xattn_ref(_layernorm(x, axis=-1), ctx_1024, ctx_1024, L2_xattn_Wq, L2_xattn_Wk, L2_xattn_Wv, L2_xattn_Wo, L2_xattn_bo)
    x = x + _L2_ffn_ref(_layernorm(x, axis=-1), L2_ffn_Wfc_s, L2_ffn_bfc_s, L2_ffn_Wproj_s, L2_ffn_bproj_s, L2_ffn_Wr, L2_ffn_Wfc, L2_ffn_bfc, L2_ffn_Wproj, L2_ffn_bproj)
    x = x + _L3_xattn_ref(_layernorm(x, axis=-1), ctx_1024, ctx_1024, L3_xattn_Wq, L3_xattn_bq, L3_xattn_Wk, L3_xattn_bk, L3_xattn_Wv, L3_xattn_bv, L3_xattn_Wo, L3_xattn_bo)
    x = x + _L3_ffn_ref(_layernorm(x, axis=-1), L3_ffn_Wp, L3_ffn_sim_matrix, L3_ffn_temperature, L3_ffn_W1, L3_ffn_b1, L3_ffn_W2, L3_ffn_b2)
    return x

_drawn_inputs = setup_inputs


def setup_inputs(seed=0):
    import zlib

    import numpy as np

    out = dict(_drawn_inputs(seed))
    spreads = {'mask_SxS2_ff0': (0.0, 2.0),
     'L0_ffn_q_scale': (1.0, 0.6),
     'L0_ffn_k_scale': (1.0, 0.6),
     'L0_ffn_ln_g': (1.0, 0.6),
     'L0_ffn_ln_b': (0.0, 0.8),
     'L0_ffn_b1': (0.0, 0.38),
     'L0_ffn_b2': (0.0, 0.1),
     'L1_xattn_b_q': (0.0, 0.361),
     'L1_xattn_b_k': (0.0, 2.0),
     'L1_xattn_b_v': (0.0, 0.1),
     'L1_xattn_b_out': (0.0, 0.1),
     'L2_ffn_bfc_s': (0.0, 0.324),
     'L2_ffn_bproj_s': (0.0, 0.1),
     'L2_ffn_bfc': (0.0, 0.443),
     'L2_ffn_bproj': (0.0, 0.1),
     'L3_xattn_bq': (0.0, 2.0),
     'L3_xattn_bk': (0.0, 2.0),
     'L3_xattn_bv': (0.0, 0.31),
     'L3_xattn_bo': (0.0, 0.1),
     'L3_ffn_b1': (0.0, 0.395),
     'L3_ffn_b2': (0.0, 0.1)}
    factors = {'L0_xattn_Lx': 5.932,
     'L0_xattn_Ly': 7.148,
     'L0_xattn_Lo': 21.389,
     'L1_ffn_bias': 4.862,
     'L2_xattn_bo': 3.959,
     'L3_xattn_Wq': 8.0,
     'L3_xattn_Wk': 8.0}
    for name, (base, spread) in spreads.items():
        noise = np.random.default_rng([zlib.crc32(name.encode()), seed]).standard_normal(out[name].shape)
        drawn = base * np.exp(spread * noise) if base else spread * noise
        out[name] = jnp.asarray(drawn.astype(out[name].dtype))
    for name, factor in factors.items():
        out[name] = (out[name] * factor).astype(out[name].dtype)
    return out
```

```python
from contextlib import ExitStack

import numpy as np

import concourse.bass as bass
from concourse import mybir

F32 = mybir.dt.float32
BF16 = mybir.dt.bfloat16
ALU = mybir.AluOpType
ACT = mybir.ActivationFunctionType
AX = mybir.AxisListType

P = 128
SEQ = 64
TILES = 16
HEADS, HD = 16, 64
PAIRS = HEADS // 2
DEPTH = 6
WINDOW = 32
EPS = 1e-5
HID = 341
CHUNKS = [(0, 128), (128, 128), (256, 85)]
PHANTOM = 2



class Names:
    pass


def build(nc, a, out):
    ctx = ExitStack()
    with ctx:
        def sb(name, shape, dt=F32):
            return ctx.enter_context(nc.sbuf_tensor(name, shape, dt))

        def pb(name, shape, dt=F32):
            return ctx.enter_context(nc.psum_tensor(name, shape, dt))

        k = Names()
        primed = []

        def sem(name, first=0):
            s = ctx.enter_context(nc.semaphore(name))
            if first:
                primed.append((s, first))
            return s

        k.x = sb("x_all", [P, TILES, P])
        k.y = sb("y_all", [P, TILES, P])
        k.ident = sb("ident", [P, P])
        k.shift = sb("shift", [P, P])
        k.ones = sb("ones", [1, P])
        k.onescol = sb("onescol", [P, 1])
        k.power = sb("power", [P, HEADS])
        k.eps = sb("eps", [P, HEADS])
        k.ctxT = sb("ctxT", [P, 2, P])
        k.stats = sb("stats", [P, 2, 6])
        k.mv = sb("mv", [P, 2, 2])
        k.rstd = sb("rstd", [P, 2, 1])
        k.normed = sb("normed", [P, 2, P])
        k.xT = sb("xT", [P, 2, P])
        k.qT = sb("qT", [P, 2, PAIRS, P])
        k.kT = sb("kT", [P, 2, PAIRS, P])
        k.v2 = sb("v2", [P, 2, 2, 512])
        k.logit = sb("logit", [P, 2, HEADS, SEQ])
        k.prob = sb("prob", [P, 2, HEADS, SEQ])
        k.probT = sb("probT", [P, PAIRS, P])
        k.oT = sb("oT", [P, PAIRS, P])
        k.top = sb("top", [P, 2, HEADS])
        k.den = sb("den", [P, 2, HEADS])
        k.rden = sb("rden", [P, 2, HEADS])
        k.w0 = pb("w0", [P, 1024])
        k.w1 = pb("w1", [P, 1024])
        k.w2 = pb("w2", [P, 1024])
        k.pt = pb("pt", [P, 512])
        k.py = pb("py", [P, 512])

        k.m_fc = sb("m_fc", [P, 9, 512])
        k.a_ly, k.a_lx, k.a_tx, k.a_ty = (k.m_fc[:, 2 * i:2 * i + 2, :].rearrange("p a n -> p (a n)")
                                          for i in range(4))
        k.a_tx = k.a_tx.rearrange("p (a n) -> p a n", a=2)
        k.a_ty = k.a_ty.rearrange("p (h n) -> p h n", h=PAIRS)
        k.a_lo = sb("a_lo", [P, PAIRS])
        k.a_to0 = sb("a_to0", [P, PAIRS])
        k.a_to1 = sb("a_to1", [1, P])
        k.a_mask = sb("a_mask", [P, SEQ])

        k.b_wqkv = sb("b_wqkv", [P, 3072])
        k.b_wo = sb("b_wo", [P, PAIRS, P])
        k.b_scales = sb("b_scales", [P, 4 * HD])
        k.rope = sb("rope", [P, 4 * HD])
        k.rot = sb("rot", [P, 4, HD])
        k.band = sb("band", [P, SEQ])
        k.ytile = sb("ytile", [P, 2, P])
        k.sT = sb("sT", [P, 2, P])
        k.straight = sb("straight", [P, 2, HEADS, HD])
        k.turned = sb("turned", [P, 2, HEADS, HD])
        k.sq = sb("sq", [P, 2, HEADS, HD])
        k.norm2 = sb("norm2", [P, 2, HEADS])
        k.rnorm = sb("rnorm", [P, 2, HEADS])
        k.c_w1 = sb("c_w1", [P, 2 * HID])
        k.c_w2 = sb("c_w2", [P, 3, P])
        k.c_cols = sb("c_cols", [P, 8])
        k.c_b2 = sb("c_b2", [1, P])
        k.xs = sb("xs", [P, 2, 4, P])
        k.xnT = sb("xnT", [P, 2, 512])
        k.gate = sb("gate", [P, 3, 512])
        k.hid = sb("hid", [P, 3, 512])
        k.stats4 = sb("stats4", [P, TILES, 6])
        k.mv4 = sb("mv4", [P, TILES, 2])
        k.rstd4 = sb("rstd4", [P, TILES])

        k.s_w = sb("s_w", [P, 3, 4, P])
        k.s_cols = sb("s_cols", [P, 3, 3])
        k.s_bo = sb("s_bo", [1, 3, P])
        k.member = sb("member", [P, 8])
        k.s_qT = sb("s_qT", [P, 2, P])
        k.s_v = sb("s_v", [P, 2, 2, PAIRS, 2, 8])
        k.s_rows = sb("s_rows", [P, P])
        k.s_oT = sb("s_oT", [P, P])
        k.wmax = sb("wmax", [P, 4])
        k.wmaxT = sb("wmaxT", [4, 1])
        k.wdiag = sb("wdiag", [4, 4])
        k.ones4 = sb("ones4", [4, P])
        k.wstep = sb("wstep", [P, 4])
        k.wrstep = sb("wrstep", [P, 4])

        k.ident16 = sb("ident16", [P, P], BF16)
        k.f_bytes = sb("f_bytes", [P, P], mybir.dt.uint8)
        k.f_w = sb("f_w", [P, P], BF16)
        k.f_ws = sb("f_ws", [P, 1])
        k.f_bias = sb("f_bias", [P, P])
        k.f_scale = sb("f_scale", [P, TILES])
        k.f_rscale = sb("f_rscale", [P, TILES])
        k.m_proj = sb("m_proj", [P, 9, 4, P])
        k.m_bfc = sb("m_bfc", [P, 9, 4])
        k.m_brow = sb("m_brow", [9, P])
        k.m_wr = sb("m_wr", [P, 8])
        k.m_wp = sb("m_wp", [P, P])
        k.m_sim = sb("m_sim", [8, P])
        k.m_simsq = sb("m_simsq", [8, P])
        k.m_simn = sb("m_simn", [8, 1])
        k.m_temp = sb("m_temp", [P, 1])
        k.m_rtemp = sb("m_rtemp", [P, 1])
        k.m_tri = sb("m_tri", [P, SEQ])
        k.m_norm2 = sb("m_norm2", [P, TILES])
        k.m_logit = sb("m_logit", [P, TILES, 8])
        k.m_exp = sb("m_exp", [P, TILES, 8])
        k.m_rank = sb("m_rank", [P, TILES, 8])
        k.m_top = sb("m_top", [P, TILES])
        k.m_gate = sb("m_gate", [P, TILES, 9])
        wide = (lambda b: b[:, :, :, :].rearrange("p a h n -> p (a h n)"))
        k.s_k8 = wide(k.straight).rearrange("p (s j n) -> p s j n", s=2, j=8)
        k.m_scaled = wide(k.xs).rearrange("p (s j n) -> p s j n", s=2, j=4)
        k.f_int, k.f_mag = (wide(k.sq)[:, i * P:(i + 1) * P].bitcast(mybir.dt.int32) for i in range(2))
        k.f_val, k.f_low = (wide(k.sq)[:, i * P:(i + 1) * P] for i in range(2, 4))
        k.f_q, k.f_qT = (k.prob[:, i, :, :].rearrange("p h n -> p (h n)").bitcast(BF16)
                         .rearrange("p (t n) -> p t n", n=P) for i in range(2))
        k.m_xT = k.qT[:, :, :, :].rearrange("p a h n -> p (a h n)").rearrange("p (q n) -> p q n", q=4)
        k.m_projT = k.kT[:, :, :, :].rearrange("p a h n -> p (a h n)")
        k.m_sq = k.logit[:, :, :, :].rearrange("p a h n -> p (a h n)")
        k.m_greater = k.sq[:, 0, :, :].rearrange("p h n -> p (h n)").rearrange("p (t m) -> p t m", t=TILES)
        k.m_equal = k.sq[:, 1, :, :].rearrange("p h n -> p (h n)").rearrange("p (t m) -> p t m", t=TILES)
        k.m_gateT = k.v2[0:9, :, :, :].rearrange("p a b n -> p (a b n)")
        k.m_hid = [b[:, :, :, :].rearrange("p a h n -> p (a h n)").rearrange("p (c n) -> p c n", c=4)
                   for b in (k.straight, k.turned)]

        k.loaded = sem("loaded")
        k.stored = sem("stored")
        k.consts = sem("consts")
        k.powers = sem("powers")
        k.primed = sem("primed")
        k.xT_psum = sem("xT_psum", PHANTOM)
        k.xT_ready = sem("xT_ready", PHANTOM)
        k.q_psum = sem("q_psum", PHANTOM)
        k.k_psum = sem("k_psum", PHANTOM)
        k.v_psum = sem("v_psum", PHANTOM)
        k.qT_ready = sem("qT_ready", PHANTOM)
        k.kT_ready = sem("kT_ready", PHANTOM)
        k.v_ready = sem("v_ready", PHANTOM)
        k.s_psum = sem("s_psum", PHANTOM)
        k.masked = sem("masked", PHANTOM)
        k.top_ready = sem("top_ready", PHANTOM)
        k.shifted = sem("shifted", PHANTOM)
        k.exp_ready = sem("exp_ready", PHANTOM)
        k.den_ready = sem("den_ready", PHANTOM)
        k.rden_ready = sem("rden_ready", PHANTOM)
        k.prob_ready = sem("prob_ready", PHANTOM)
        k.pT_psum = sem("pT_psum", PHANTOM)
        k.pT_ready = sem("pT_ready", PHANTOM)
        k.o_psum = sem("o_psum", PHANTOM)
        k.oT_ready = sem("oT_ready", PHANTOM)
        k.y_psum = sem("y_psum", PHANTOM)
        k.updated = sem("updated", PHANTOM)
        k.ctx_loaded = [sem("ctx_even"), sem("ctx_odd")]

        k.norm = Names()
        k.norm.stat = sem("norm_stat", PHANTOM)
        k.norm.mv = sem("norm_mv", PHANTOM)
        k.norm.eps = sem("norm_eps", PHANTOM)
        k.norm.rstd = sem("norm_rstd", PHANTOM)
        k.norm.normed = sem("norm_normed", PHANTOM)
        k.all_stat = sem("all_stat")
        k.all_mv = sem("all_mv")
        k.all_eps = sem("all_eps")
        k.all_rstd = sem("all_rstd")
        k.all_normed = sem("all_normed")
        B = PHANTOM + TILES
        k.b_loaded = sem("b_loaded")
        k.rot_ready = sem("rot_ready")
        k.y_copied = sem("y_copied", B)
        k.half_shifted = sem("half_shifted", B)
        k.q_squared = sem("q_squared", B)
        k.k_squared = sem("k_squared", B)
        k.q_turned = sem("q_turned", B)
        k.k_turned = sem("k_turned", B)
        k.q_norm2 = sem("q_norm2", B)
        k.k_norm2 = sem("k_norm2", B)
        k.q_floor = sem("q_floor", B)
        k.k_floor = sem("k_floor", B)
        k.q_rnorm = sem("q_rnorm", B)
        k.k_rnorm = sem("k_rnorm", B)
        k.q_added = sem("q_added", B)
        k.k_added = sem("k_added", B)
        k.q_final = sem("q_final", B)
        k.k_final = sem("k_final", B)
        k.qT_psum = sem("qT_psum", B)
        k.kT_psum = sem("kT_psum", B)
        k.c_loaded = sem("c_loaded")
        k.sh_psum = sem("sh_psum", PHANTOM)
        k.xs_low = sem("xs_low", PHANTOM)
        k.xs_high = sem("xs_high", PHANTOM)
        k.quad_stat = sem("quad_stat", PHANTOM)
        k.quad_mv = sem("quad_mv", PHANTOM)
        k.quad_eps = sem("quad_eps", PHANTOM)
        k.quad_rstd = sem("quad_rstd", PHANTOM)
        k.quad_normed = sem("quad_normed", PHANTOM)
        k.quad_turned = sem("quad_turned", PHANTOM)
        k.xnT_ready = sem("xnT_ready", PHANTOM)
        k.hid_psum = sem("hid_psum", 3 * PHANTOM)
        k.gated = sem("gated", 3 * PHANTOM)
        k.hid_ready = sem("hid_ready", 3 * PHANTOM)
        k.out_psum = sem("out_psum", PHANTOM)
        k.y_done = sem("y_done", PHANTOM)
        k.d = Names()
        k.d.xT_psum = sem("small_xT_psum", PHANTOM)
        k.d.xT_ready = sem("small_xT_ready", PHANTOM)
        k.d.q_psum = sem("small_q_psum", PHANTOM)
        k.d.k_psum = sem("small_k_psum", PHANTOM)
        k.d.v_psum = sem("small_v_psum", PHANTOM)
        k.d.q_ready = sem("small_q_ready", PHANTOM)
        k.d.k8_ready = sem("small_k8_ready", PHANTOM)
        k.d.v_ready = sem("small_v_ready", PHANTOM)
        k.d.s_psum = sem("small_s_psum", PHANTOM)
        k.d.top = sem("small_top", PHANTOM)
        k.d.shifted = sem("small_shifted", PHANTOM)
        k.d.exp = sem("small_exp", PHANTOM)
        k.d.den = sem("small_den", PHANTOM)
        k.d.rden = sem("small_rden", PHANTOM)
        k.d.pT_psum = sem("small_pT_psum", PHANTOM)
        k.d.pT_ready = sem("small_pT_ready", PHANTOM)
        k.d.o_psum = sem("small_o_psum", PHANTOM)
        k.d.rows = sem("small_rows", PHANTOM)
        k.d.o_turned = sem("small_o_turned", PHANTOM)
        k.d.oT_ready = sem("small_oT_ready", PHANTOM)
        k.d.y_psum = sem("small_y_psum", PHANTOM)
        k.d.updated = sem("small_updated", PHANTOM)
        k.quant = Names()
        k.quant.wmax = sem("quant_wmax")
        k.quant.turned = sem("quant_turned")
        k.quant.diag = sem("quant_diag")
        k.quant.spread = sem("quant_spread")
        k.quant.done = sem("quant_done")
        k.f = Names()
        k.f.weight = sem("fp8_weight")
        k.f.quantised = sem("fp8_quantised")
        k.f.turned = sem("fp8_turned")
        k.f.qT = sem("fp8_qT")
        k.f.product = sem("fp8_product")
        k.f.done = sem("fp8_done")
        k.e = []
        for n in (2, 3):
            e = Names()
            e.loaded = sem(f"experts{n}_loaded")
            e.xnT = sem(f"experts{n}_xnT")
            e.turned = sem(f"experts{n}_turned")
            e.logits = sem(f"experts{n}_logits")
            e.below = sem(f"experts{n}_below")
            e.exp = sem(f"experts{n}_exp")
            e.gates = sem(f"experts{n}_gates")
            e.gate_turned = sem(f"experts{n}_gate_turned")
            e.gateT = sem(f"experts{n}_gateT")
            e.bias_psum = sem(f"experts{n}_bias_psum")
            e.done = sem(f"experts{n}_done")
            e.first = PHANTOM if n == 2 else PHANTOM + 9 * QUADS
            k.e.append(e)
        e.projT = sem("experts3_projT")
        e.squares = sem("experts3_squares")
        e.sim_norm2 = sem("experts3_sim_norm2")
        e.sim_floor = sem("experts3_sim_floor")
        e.sim_rnorm = sem("experts3_sim_rnorm")
        e.sim_scaled = sem("experts3_sim_scaled")
        e.sim_turned = sem("experts3_sim_turned")
        e.sim_T = sem("experts3_sim_T")
        e.norm2 = sem("experts3_norm2")
        e.floor = sem("experts3_floor")
        e.rnorm = sem("experts3_rnorm")
        e.cooled = sem("experts3_cooled")
        e.raw = sem("experts3_raw")
        hid_psum, hid_ready = (sem(name, 4 * PHANTOM) for name in ("experts_hid_psum", "experts_hid_ready"))
        out_psum, scaled, added = (sem("experts_" + name, PHANTOM) for name in ("out_psum", "scaled", "added"))
        for e in k.e:
            e.hid_psum, e.hid_ready, e.out_psum, e.scaled, e.added = hid_psum, hid_ready, out_psum, scaled, added
        k.vector_link, k.links = sem("vector_link"), 0
        k.x_done = sem("x_done")

        block = ctx.enter_context(nc.Block())

        @block.sync
        def _(sp):
            sync_program(nc, sp, k, a, out)

        @block.tensor
        def _(pe):
            tensor_program(nc, pe, k)

        @block.scalar
        def _(act):
            scalar_program(nc, act, k)

        @block.vector
        def _(dve):
            vector_program(nc, dve, k)

        @block.gpsimd
        def _(pool):
            for s, first in primed:
                pool.sem_inc(s, first)
            gpsimd_program(nc, pool, k)


def steps(eng, first, step):
    with eng.Fori(1, TILES - 2, 2) as t:
        step(first + t, 1, t)
        step(first + t + 1, 0, t + 1)
    step(first + (TILES - 1), 1, TILES - 1)


def tile(ap, t):
    return ap[:, t, :] if isinstance(t, int) else ap[:, bass.ds(t, 1), :].rearrange("p a n -> p (a n)")



def cross0_tensor(pe, k, first):
    def front(T, s):
        pe.wait_ge(k.norm.normed, T + 1)
        pe.wait_ge(k.xT_ready, T)
        pe.transpose(k.pt[:, 0:P], k.normed[:, s, :], k.ident[:, :]).then_inc(k.xT_psum, 1)
        pe.wait_ge(k.xT_ready, T + 1)
        pe.wait_ge(k.oT_ready, T - 1)
        for h in range(PAIRS):
            mm = pe.matmul(k.w0[:, h * P:(h + 1) * P], k.a_ly[:, h * P:(h + 1) * P], k.xT[:, s, :],
                           start=True, stop=True)
        mm.then_inc(k.q_psum, 1)
        pe.wait_ge(k.ctx_loaded[s], 8 * (T - s - first) + 16)
        pe.wait_ge(k.masked, T)
        for h in range(PAIRS):
            mm = pe.matmul(k.w1[:, h * P:(h + 1) * P], k.a_lx[:, h * P:(h + 1) * P], k.ctxT[:, s, :],
                           start=True, stop=True)
        mm.then_inc(k.k_psum, 1)
        pe.wait_ge(k.pT_ready, T - 1)
        for b in range(2):
            for p in range(2):
                mm = pe.matmul(k.w2[64 * p:64 * p + 64, 512 * b:512 * b + 512],
                               k.ctxT[:, s, 64 * b:64 * b + 64], k.a_tx[:, p, :], start=True, stop=True)
        mm.then_inc(k.v_psum, 1)

    def step(T, s, t):
        front(T, s)
        attend_tail_tensor(pe, k, T - 1, 1 - s, k.a_ty, k.a_to1, k.qT_ready)
        wait_apart(pe, k, k.qT_ready, T + 1)
        pe.wait_ge(k.kT_ready, T + 1)
        scores_tensor(pe, k, s)

    front(first, 0)
    pe.wait_ge(k.qT_ready, first + 1)
    pe.wait_ge(k.kT_ready, first + 1)
    scores_tensor(pe, k, 0)
    steps(pe, first, step)
    attend_tail_tensor(pe, k, first + TILES - 1, 1, k.a_ty, k.a_to1, k.qT_ready, ahead=0)


def wait_apart(eng, k, s, value):
    if not isinstance(value, int):
        eng.to_reg(value)
    eng.wait_ge(k.consts, 5)
    eng.wait_ge(s, value)


def link(dve, k, instruction):
    k.links += 1
    instruction.then_inc(k.vector_link, 1)
    dve.wait_ge(k.vector_link, k.links)


def scores_tensor(pe, k, s):
    for h in range(PAIRS):
        for p in range(2):
            for b in range(2):
                r = slice(64 * p, 64 * p + 64)
                c = slice(64 * b, 64 * b + 64)
                mm = pe.matmul(k.w1[c, 512 * p + 64 * h:512 * p + 64 * h + 64], k.qT[r, s, h, c],
                               k.kT[r, s, h, c], start=True, stop=True)
    mm.then_inc(k.s_psum, 1)


def attend_tail_tensor(pe, k, T, s, w_out, b_out, w0_free, ahead=1):
    pe.wait_ge(k.prob_ready, T + 1)
    pe.wait_ge(k.v_ready, T + 1 + ahead)
    for h in range(PAIRS):
        mm = pe.transpose(k.w2[:, h * P:(h + 1) * P], k.prob[:, s, 2 * h:2 * h + 2, :].rearrange("p a m -> p (a m)"), k.ident[:, :])
    mm.then_inc(k.pT_psum, 1)
    wait_apart(pe, k, k.pT_ready, T + 1)
    pe.wait_ge(w0_free, T + 1 + ahead)
    for n in range(PAIRS):
        for p in range(2):
            h = (n + 4 * p) % PAIRS
            for b in range(2):
                r = slice(64 * p, 64 * p + 64)
                mm = pe.matmul(k.w0[r, h * P + 64 * b:h * P + 64 * b + 64], k.v2[r, s, b, 64 * h:64 * h + 64],
                               k.probT[r, h, 64 * b:64 * b + 64], start=True, stop=True)
    mm.then_inc(k.o_psum, 1)
    pe.wait_ge(k.oT_ready, T + 1)
    pe.wait_ge(k.updated, T)
    for h in range(PAIRS):
        mm = pe.matmul(k.py[:, 0:P], k.oT[:, h, :], w_out[:, h, :],
                       start=(h == 0), stop=(b_out is None and h == PAIRS - 1))
    if b_out is not None:
        mm = pe.matmul(k.py[:, 0:P], k.ones[0:1, :], b_out[0:1, :], start=False, stop=True)
    mm.then_inc(k.y_psum, 1)


def cross0_scalar(act, k, first):
    def front(T, s):
        act.wait_ge(k.xT_psum, T + 1)
        act.copy(k.xT[:, s, :], k.pt[:, 0:P]).then_inc(k.xT_ready, 1)

    def fill(T, s):
        act.wait_ge(k.k_psum, T + 1)
        act.copy(k.kT[:, s, :, :], k.w1[:, :]).then_inc(k.kT_ready, 1)
        act.wait_ge(k.v_psum, T + 1)
        act.copy(k.v2[:, s, :, :], k.w2[:, :]).then_inc(k.v_ready, 1)

    def step(T, s, t):
        front(T, s)
        exp_scalar(act, k, T - 1, 1 - s, 0.125)
        fill(T, s)
        probT_scalar(act, k, T - 1)

    front(first, 0)
    fill(first, 0)
    steps(act, first, step)
    exp_scalar(act, k, first + TILES - 1, 1, 0.125)
    probT_scalar(act, k, first + TILES - 1)


def exp_scalar(act, k, T, s, scale):
    act.wait_ge(k.shifted, T + 1)
    act.activation(k.prob[:, s, :, :], k.logit[:, s, :, :], ACT.Exp, scale=scale).then_inc(k.exp_ready, 1)


def probT_scalar(act, k, T):
    act.wait_ge(k.pT_psum, T + 1)
    act.wait_ge(k.o_psum, T)
    act.copy(k.probT[:, :, :], k.w2[:, :]).then_inc(k.pT_ready, 1)


def softmax_shift_vector(dve, k, T, s, mask):
    dve.wait_ge(k.s_psum, T + 1)
    flat = k.logit[:, s, :, :]
    dve.tensor_tensor(flat.rearrange("p (h a) m -> p a h m", a=2),
                      k.w1[:, :].rearrange("p (a h m) -> p a h m", a=2, m=SEQ),
                      mask[:, None, None, :].broadcast_to([P, 2, PAIRS, SEQ]), ALU.add).then_inc(k.masked, 1)
    dve.wait_ge(k.masked, T + 1)
    dve.tensor_reduce(k.top[:, s, :], flat, AX.X, ALU.max).then_inc(k.top_ready, 1)
    dve.wait_ge(k.top_ready, T + 1)
    dve.tensor_tensor(flat, flat, k.top[:, s, :, None].broadcast_to([P, HEADS, SEQ]),
                      ALU.subtract).then_inc(k.shifted, 1)


def softmax_sum_vector(dve, k, T, s):
    dve.wait_ge(k.exp_ready, T + 1)
    dve.tensor_reduce(k.den[:, s, :], k.prob[:, s, :, :], AX.X,
                      ALU.add).then_inc(k.den_ready, 1)
    dve.wait_ge(k.den_ready, T + 1)
    dve.reciprocal(k.rden[:, s, :], k.den[:, s, :]).then_inc(k.rden_ready, 1)


def softmax_scale_gpsimd(pool, k, T, s):
    pool.wait_ge(k.rden_ready, T + 1)
    flat = k.prob[:, s, :, :]
    pool.tensor_tensor(flat, flat, k.rden[:, s, :, None].broadcast_to([P, HEADS, SEQ]),
                       ALU.mult).then_inc(k.prob_ready, 1)


def stats_vector(dve, k, n, T, s, rows):
    dve.bn_stats(k.stats[:, s, :], rows).then_inc(n.stat, 1)
    wait_apart(dve, k, n.stat, T + 1)
    dve.bn_aggr(k.mv[:, s, :], k.stats[:, s, :]).then_inc(n.mv, 1)


def normalise_vector(dve, k, n, T, s, rows, to):
    dve.wait_ge(n.rstd, T + 1)
    return dve.tensor_scalar(to, rows, k.mv[:, s, 0:1], k.rstd[:, s, :], ALU.subtract, ALU.mult)


def rstd_gpsimd(pool, k, n, T, s):
    pool.wait_ge(n.mv, T + 1)
    pool.tensor_tensor(k.rstd[:, s, :], k.mv[:, s, 1:2], k.eps[:, 0:1], ALU.add).then_inc(n.eps, 1)
    pool.wait_ge(n.eps, T + 1)
    pool.tensor_tensor(k.rstd[:, s, :], k.rstd[:, s, :], k.power[:, 0:1], ALU.pow).then_inc(n.rstd, 1)


def cross0_vector(dve, k, first):
    def norm(T, s, t):
        rows = tile(k.x, t)
        stats_vector(dve, k, k.norm, T, s, rows)
        dve.wait_ge(k.xT_psum, T - 1)
        normalise_vector(dve, k, k.norm, T, s, rows, k.normed[:, s, :]).then_inc(k.norm.normed, 1)

    def q_bias(T, s):
        dve.wait_ge(k.q_psum, T + 1)
        dve.tensor_tensor(k.qT[:, s, :, :], k.w0[:, :].rearrange("p (h n) -> p h n", n=P),
                          k.a_lo[:, :, None].broadcast_to([P, PAIRS, P]), ALU.add).then_inc(k.qT_ready, 1)

    def tail(T, t):
        dve.wait_ge(k.o_psum, T + 1)
        dve.wait_ge(k.y_psum, T)
        dve.tensor_tensor(k.oT[:, :, :], k.w0[:, :].rearrange("p (h n) -> p h n", n=P),
                          k.a_to0[:, :, None].broadcast_to([P, PAIRS, P]), ALU.add).then_inc(k.oT_ready, 1)
        dve.wait_ge(k.y_psum, T + 1)
        dve.tensor_tensor(tile(k.x, t), tile(k.x, t), k.py[:, 0:P], ALU.add).then_inc(k.updated, 1)

    def step(T, s, t):
        norm(T, s, t)
        softmax_shift_vector(dve, k, T - 1, 1 - s, k.a_mask)
        q_bias(T, s)
        softmax_sum_vector(dve, k, T - 1, 1 - s)
        tail(T - 1, t - 1)

    norm(first, 0, 0)
    q_bias(first, 0)
    steps(dve, first, step)
    last = first + TILES - 1
    softmax_shift_vector(dve, k, last, 1, k.a_mask)
    softmax_sum_vector(dve, k, last, 1)
    tail(last, TILES - 1)


def cross0_gpsimd(pool, k, first):
    def step(T, s, t):
        rstd_gpsimd(pool, k, k.norm, T, s)
        softmax_scale_gpsimd(pool, k, T - 1, 1 - s)

    rstd_gpsimd(pool, k, k.norm, first, 0)
    steps(pool, first, step)
    softmax_scale_gpsimd(pool, k, first + TILES - 1, 1)



def fresh_vector(dve, k, n):
    with dve.Fori(0, TILES) as t:
        dve.bn_stats(tile(k.stats4, t), tile(k.x, t)).then_inc(k.all_stat, 1)
    dve.wait_ge(k.all_stat, n * TILES)
    for t in range(TILES):
        agg = dve.bn_aggr(k.mv4[:, t, :], k.stats4[:, t, :])
    agg.then_inc(k.all_mv, 1)
    dve.wait_ge(k.all_rstd, n)
    for t in range(TILES):
        last = dve.tensor_scalar(k.y[:, t, :], k.x[:, t, :], k.mv4[:, t, 0:1], k.rstd4[:, t:t + 1],
                                 ALU.subtract, ALU.mult)
    last.then_inc(k.all_normed, 1)


def fresh_gpsimd(pool, k, n):
    pool.wait_ge(k.all_mv, n)
    pool.tensor_tensor(k.rstd4[:, :], k.mv4[:, :, 1], k.eps[:, 0:1].broadcast_to([P, TILES]),
                       ALU.add).then_inc(k.all_eps, 1)
    pool.wait_ge(k.all_eps, n)
    pool.tensor_tensor(k.rstd4[:, :], k.rstd4[:, :], k.power[:, 0:1].broadcast_to([P, TILES]),
                       ALU.pow).then_inc(k.all_rstd, 1)



def local_tensor(pe, k, first):
    def front(T, s):
        pe.wait_ge(k.y_copied, T + 1)
        pe.wait_ge(k.half_shifted, T)
        pe.transpose(k.pt[:, 0:P], k.ytile[:, s, :], k.ident[:, :]).then_inc(k.xT_psum, 1)
        pe.wait_ge(k.half_shifted, T + 1)
        pe.wait_ge(k.oT_ready, T - 1)
        for c in range(2):
            mm = pe.matmul(k.w0[:, 512 * c:512 * c + 512], k.sT[:, s, :], k.b_wqkv[:, 512 * c:512 * c + 512],
                           start=True, stop=True)
        mm.then_inc(k.q_psum, 1)
        pe.wait_ge(k.masked, T)
        for c in range(2):
            mm = pe.matmul(k.w1[:, 512 * c:512 * c + 512], k.sT[:, s, :],
                           k.b_wqkv[:, 1024 + 512 * c:1536 + 512 * c], start=True, stop=True)
        mm.then_inc(k.k_psum, 1)
        pe.wait_ge(k.kT_ready, T)
        for b in range(2):
            for p in range(2):
                mm = pe.matmul(k.w2[64 * p:64 * p + 64, 512 * b:512 * b + 512],
                               k.sT[:, s, 64 * b:64 * b + 64], k.b_wqkv[:, 2048 + 512 * p:2560 + 512 * p],
                               start=True, stop=True)
        mm.then_inc(k.v_psum, 1)

    def turn(T, s):
        pe.wait_ge(k.q_final, T + 1)
        pe.wait_ge(k.k_turned, T + 1)
        pe.wait_ge(k.k_squared, T + 1)
        for h in range(PAIRS):
            mm = pe.transpose(k.w1[:, h * P:(h + 1) * P],
                              k.straight[:, 0, 2 * h:2 * h + 2, :].rearrange("p a d -> p (a d)"), k.ident[:, :])
        mm.then_inc(k.qT_psum, 1)
        pe.wait_ge(k.k_final, T + 1)
        pe.wait_ge(k.v_ready, T + 1)
        pe.wait_ge(k.pT_ready, T)
        for h in range(PAIRS):
            mm = pe.transpose(k.w2[:, h * P:(h + 1) * P],
                              k.straight[:, 1, 2 * h:2 * h + 2, :].rearrange("p a d -> p (a d)"), k.ident[:, :])
        mm.then_inc(k.kT_psum, 1)
        wait_apart(pe, k, k.qT_ready, T + 1)
        pe.wait_ge(k.kT_ready, T + 1)
        scores_tensor(pe, k, s)

    def step(T, s, t):
        front(T, s)
        local_w0_free(T + 1)
        attend_tail_tensor(pe, k, T - 1, 1 - s, k.b_wo, None, k.q_turned)
        turn(T, s)

    def local_w0_free(value):
        pe.wait_ge(k.q_squared, value)

    pe.wait_ge(k.b_loaded, B_LOADS * (first - PHANTOM))
    front(first, 0)
    turn(first, 0)
    steps(pe, first, step)
    attend_tail_tensor(pe, k, first + (TILES - 1), 1, k.b_wo, None, k.q_turned, ahead=0)


def local_scalar(act, k, first):
    def front(T, s):
        act.wait_ge(k.xT_psum, T + 1)
        act.wait_ge(k.v_psum, T - 1)
        act.copy(k.sT[0:64, s, :], k.pt[0:64, 0:P])
        act.copy(k.sT[64:P, s, :].rearrange("p (b n) -> p b n", b=2)[:, :, 1:SEQ],
                 k.pt[64:P, 0:P].rearrange("p (b n) -> p b n", b=2)[:, :, 0:SEQ - 1]).then_inc(k.half_shifted, 1)

    def fill(T, s):
        act.wait_ge(k.q_psum, T + 1)
        act.wait_ge(k.q_norm2, T)
        act.activation(k.sq[:, 0, :, :], k.w0[:, :], ACT.Square).then_inc(k.q_squared, 1)
        act.wait_ge(k.k_psum, T + 1)
        act.wait_ge(k.k_norm2, T)
        act.activation(k.sq[:, 1, :, :], k.w1[:, :], ACT.Square).then_inc(k.k_squared, 1)
        act.wait_ge(k.v_psum, T + 1)
        act.copy(k.v2[:, s, :, :], k.w2[:, :]).then_inc(k.v_ready, 1)

    def tail(T):
        probT_scalar(act, k, T)
        act.wait_ge(k.o_psum, T + 1)
        act.wait_ge(k.y_psum, T)
        act.copy(k.oT[:, :, :], k.w0[:, :]).then_inc(k.oT_ready, 1)

    def turned(T, s):
        act.wait_ge(k.qT_psum, T + 1)
        act.copy(k.qT[:, s, :, :], k.w1[:, :]).then_inc(k.qT_ready, 1)
        act.wait_ge(k.kT_psum, T + 1)
        act.copy(k.kT[:, s, :, :], k.w2[:, :]).then_inc(k.kT_ready, 1)

    def step(T, s, t):
        front(T, s)
        exp_scalar(act, k, T - 1, 1 - s, 8.0)
        fill(T, s)
        tail(T - 1)
        turned(T, s)

    front(first, 0)
    fill(first, 0)
    turned(first, 0)
    steps(act, first, step)
    last = first + (TILES - 1)
    exp_scalar(act, k, last, 1, 8.0)
    tail(last)


def local_vector(dve, k, first):
    def rotate(T, i, w, turned, squared, norm2):
        dve.wait_ge(squared, T + 1)
        dve.wait_ge(k.qT_psum if i == 0 else k.kT_psum, T)
        heads = w[:, :].rearrange("p (h d) -> p h d", d=HD)
        dve.tensor_tensor(k.straight[:, i, :, :], heads,
                          k.rot[:, 2 * i, None, :].broadcast_to([P, HEADS, HD]), ALU.mult)
        half = HD // 2
        for to, of in ((slice(0, half), slice(half, HD)), (slice(half, HD), slice(0, half))):
            last = dve.tensor_tensor(k.turned[:, i, :, to], heads[:, :, of],
                                     k.rot[:, 2 * i + 1, None, to].broadcast_to([P, HEADS, half]), ALU.mult)
        last.then_inc(turned, 1)
        dve.tensor_reduce(k.norm2[:, i, :], k.sq[:, i, :, :], AX.X, ALU.add).then_inc(norm2, 1)

    def q_rotate(T):
        rotate(T, 0, k.w0, k.q_turned, k.q_squared, k.q_norm2)

    def k_rotate(T):
        rotate(T, 1, k.w1, k.k_turned, k.k_squared, k.k_norm2)

    def tail(T, t):
        dve.wait_ge(k.y_psum, T + 1)
        dve.tensor_tensor(tile(k.y, t), tile(k.y, t), k.py[:, 0:P], ALU.add).then_inc(k.updated, 1)

    def step(T, s, t):
        softmax_shift_vector(dve, k, T - 1, 1 - s, k.band)
        q_rotate(T)
        softmax_sum_vector(dve, k, T - 1, 1 - s)
        k_rotate(T)
        tail(T - 1, t - 1)

    dve.wait_ge(k.b_loaded, B_LOADS * (first - PHANTOM))
    dve.tensor_tensor(k.rot[:, :, :].rearrange("p a d -> p (a d)"), k.rope[:, :], k.b_scales[:, :],
                      ALU.mult).then_inc(k.rot_ready, 1)
    dve.wait_ge(k.rot_ready, (first - PHANTOM) // TILES)
    q_rotate(first)
    k_rotate(first)
    steps(dve, first, step)
    last = first + (TILES - 1)
    softmax_shift_vector(dve, k, last, 1, k.band)
    softmax_sum_vector(dve, k, last, 1)
    tail(last, TILES - 1)


def local_gpsimd(pool, k, first, qfirst):
    def copy(T, s, t):
        wait_apart(pool, k, k.xT_psum, T - 1)
        pool.tensor_copy(k.ytile[:, s, :], tile(k.y, t)).then_inc(k.y_copied, 1)

    def finish(T, i, turned, norm2, floor, rnorm, added, final):
        wait_apart(pool, k, norm2, T + 1)
        pool.tensor_scalar(k.rnorm[:, i, :], k.norm2[:, i, :], 1e-24, None, ALU.max).then_inc(floor, 1)
        pool.wait_ge(floor, T + 1)
        pool.tensor_tensor(k.rnorm[:, i, :], k.rnorm[:, i, :], k.power[:, :], ALU.pow).then_inc(rnorm, 1)
        pool.wait_ge(turned, T + 1)
        pool.tensor_tensor(k.straight[:, i, :, :], k.straight[:, i, :, :], k.turned[:, i, :, :],
                           ALU.add).then_inc(added, 1)
        pool.wait_ge(added, T + 1)
        pool.wait_ge(rnorm, T + 1)
        pool.tensor_tensor(k.straight[:, i, :, :], k.straight[:, i, :, :],
                           k.rnorm[:, i, :, None].broadcast_to([P, HEADS, HD]), ALU.mult).then_inc(final, 1)

    def both(T):
        finish(T, 0, k.q_turned, k.q_norm2, k.q_floor, k.q_rnorm, k.q_added, k.q_final)
        finish(T, 1, k.k_turned, k.k_norm2, k.k_floor, k.k_rnorm, k.k_added, k.k_final)

    def step(T, s, t):
        copy(T, s, t)
        softmax_scale_gpsimd(pool, k, T - 1, 1 - s)
        both(T)

    pool.wait_ge(k.y_done, qfirst)
    copy(first, 0, 0)
    both(first)
    steps(pool, first, step)
    softmax_scale_gpsimd(pool, k, first + (TILES - 1), 1)



QUADS = TILES // 4


def gated_tensor(pe, k, first, qfirst):
    def front(Q, q, s):
        pe.wait_ge(k.xnT_ready, Q)
        pe.matmul(k.pt[:, 0:256].rearrange("p (j d) -> p j d", j=4), k.shift[:, :], k.y[:, 4 * q:4 * q + 4, 64:P],
                  start=True, stop=True).then_inc(k.sh_psum, 1)
        pe.wait_ge(k.quad_normed, Q + 1)
        pe.wait_ge(k.xs_high, Q + 1)
        for j in range(4):
            mm = pe.transpose(k.pt[:, j * P:(j + 1) * P], k.xs[:, s, j, :], k.ident[:, :])
        mm.then_inc(k.quad_turned, 1)

    def hidden(Q, s):
        pe.wait_ge(k.xnT_ready, Q + 1)
        for c, (at, n) in enumerate(CHUNKS):
            w = (k.w0, k.w1, k.w2)[c]
            pe.wait_ge(k.hid_ready, 3 * Q + (c - 2))
            pe.matmul(w[0:n, 0:512], k.c_w1[:, HID + at:HID + at + n], k.xnT[:, s, :], start=True, stop=True)
            pe.matmul(w[0:n, 512:1024], k.c_w1[:, at:at + n], k.xnT[:, s, :],
                      start=True, stop=True).then_inc(k.hid_psum, 1)

    def output(Q):
        pe.wait_ge(k.y_done, Q)
        pe.wait_ge(k.hid_ready, 3 * Q + 3)
        for j in range(4):
            for c, (at, n) in enumerate(CHUNKS):
                pe.matmul(k.py[:, j * P:(j + 1) * P], k.hid[0:n, c, j * P:(j + 1) * P], k.c_w2[0:n, c, :],
                          start=(c == 0), stop=False)
            mm = pe.matmul(k.py[:, j * P:(j + 1) * P], k.ones[0:1, :], k.c_b2[0:1, :], start=False, stop=True)
        mm.then_inc(k.out_psum, 1)

    pe.wait_ge(k.c_loaded, C_LOADS * (first - PHANTOM))
    pe.wait_ge(k.updated, first + TILES)
    front(qfirst, 0, 0)
    for q in range(QUADS):
        if q + 1 < QUADS:
            front(qfirst + (q + 1), q + 1, (q + 1) % 2)
        hidden(qfirst + q, q % 2)
        output(qfirst + q)


def gated_scalar(act, k, first, qfirst):
    def front(Q, q, s):
        act.wait_ge(k.quad_turned, Q - 1)
        act.copy(k.xs[:, s, :, 0:64], k.y[:, 4 * q:4 * q + 4, 0:64]).then_inc(k.xs_low, 1)
        act.wait_ge(k.sh_psum, Q + 1)
        act.copy(k.xs[:, s, :, 64:P], k.pt[:, 0:256].rearrange("p (j d) -> p j d", j=4)).then_inc(k.xs_high, 1)

    def gelu(Q):
        for c, (at, n) in enumerate(CHUNKS):
            act.wait_ge(k.hid_psum, 3 * Q + (c + 1))
            act.wait_ge(k.hid_ready, 3 * Q + (c - 2))
            act.activation(k.gate[0:n, c, :], (k.w0, k.w1, k.w2)[c][0:n, 0:512], ACT.Gelu,
                           bias=k.c_cols[0:n, 5 + c:6 + c]).then_inc(k.gated, 1)

    act.wait_ge(k.updated, first + TILES)
    act.wait_ge(k.c_loaded, C_LOADS * (first - PHANTOM))
    front(qfirst, 0, 0)
    for q in range(QUADS):
        if q + 1 < QUADS:
            front(qfirst + (q + 1), q + 1, (q + 1) % 2)
        gelu(qfirst + q)


def gated_vector(dve, k, first, qfirst):
    def front(Q, q, s):
        dve.wait_ge(k.xs_low, Q + 1)
        dve.wait_ge(k.xs_high, Q + 1)
        for j in range(4):
            last = dve.bn_stats(k.stats4[:, 4 * s + j, :], k.xs[:, s, j, :])
        last.then_inc(k.quad_stat, 1)
        wait_apart(dve, k, k.quad_stat, Q + 1)
        for j in range(4):
            last = dve.bn_aggr(k.mv4[:, 4 * s + j, :], k.stats4[:, 4 * s + j, :])
        last.then_inc(k.quad_mv, 1)
        dve.wait_ge(k.quad_rstd, Q + 1)
        for j in range(4):
            last = dve.tensor_scalar(k.xs[:, s, j, :], k.xs[:, s, j, :], k.mv4[:, 4 * s + j, 0:1],
                                     k.rstd4[:, 4 * s + j:4 * s + j + 1], ALU.subtract, ALU.mult)
        last.then_inc(k.quad_normed, 1)
        dve.wait_ge(k.quad_turned, Q + 1)
        dve.tensor_scalar(k.xnT[:, s, :], k.pt[:, :], k.c_cols[:, 0:1], k.c_cols[:, 1:2],
                          ALU.mult, ALU.add).then_inc(k.xnT_ready, 1)

    def hidden(Q):
        for c, (at, n) in enumerate(CHUNKS):
            dve.wait_ge(k.gated, 3 * Q + (c + 1))
            dve.wait_ge(k.out_psum, Q)
            dve.scalar_tensor_tensor(out=k.hid[0:n, c, :], in0=(k.w0, k.w1, k.w2)[c][0:n, 512:1024],
                                     scalar=k.c_cols[0:n, 2 + c:3 + c], in1=k.gate[0:n, c, :],
                                     op0=ALU.add, op1=ALU.mult).then_inc(k.hid_ready, 1)

    def output(Q, q):
        dve.wait_ge(k.out_psum, Q + 1)
        rows = k.y[:, 4 * q:4 * q + 4, :].rearrange("p j n -> p (j n)")
        dve.tensor_tensor(rows, rows, k.py[:, :], ALU.add).then_inc(k.y_done, 1)

    dve.wait_ge(k.c_loaded, C_LOADS * (first - PHANTOM))
    front(qfirst, 0, 0)
    for q in range(QUADS):
        if q + 1 < QUADS:
            front(qfirst + (q + 1), q + 1, (q + 1) % 2)
        hidden(qfirst + q)
        output(qfirst + q, q)


def gated_gpsimd(pool, k, first, qfirst):
    for q in range(QUADS):
        Q, s = qfirst + q, q % 2
        r = k.rstd4[:, 4 * s:4 * s + 4]
        pool.wait_ge(k.quad_mv, Q + 1)
        pool.tensor_tensor(r, k.mv4[:, 4 * s:4 * s + 4, 1], k.eps[:, 0:4], ALU.add).then_inc(k.quad_eps, 1)
        pool.wait_ge(k.quad_eps, Q + 1)
        pool.tensor_tensor(r, r, k.power[:, 0:4], ALU.pow).then_inc(k.quad_rstd, 1)



def small_tensor(pe, k, n):
    d, first = k.d, PHANTOM + TILES * n

    def front(T, s):
        pe.wait_ge(k.norm.normed, T + (TILES + 1))
        pe.wait_ge(d.v_ready, T)
        pe.transpose(k.pt[:, 0:P], k.normed[:, s, :], k.ident[:, :]).then_inc(d.xT_psum, 1)
        pe.wait_ge(k.ctx_loaded[s], 8 * (T - s - first) + (16 + 128 * (n + 1)))
        pe.wait_ge(d.oT_ready, T - 1)
        pe.matmul(k.w0[:, 512:512 + P], k.s_w[:, n, 1, :], k.ctxT[:, s, :], start=True, stop=True).then_inc(d.k_psum, 1)
        pe.wait_ge(d.xT_ready, T + 1)
        pe.wait_ge(d.rows, T - 1)
        pe.matmul(k.w0[:, 0:P], k.s_w[:, n, 0, :], k.xT[:, s, :], start=True, stop=True).then_inc(d.q_psum, 1)
        for p in range(2):
            for b in range(2):
                mm = pe.matmul(k.pt[64 * p:64 * p + 64, 64 * b:64 * b + 64], k.ctxT[:, s, 64 * b:64 * b + 64],
                               k.s_w[:, n, 2, 64 * p:64 * p + 64], start=True, stop=True)
        mm.then_inc(d.v_psum, 1)

    def scores(T, s):
        wait_apart(pe, k, d.q_ready, T + 1)
        pe.wait_ge(d.k8_ready, T + 1)
        pe.wait_ge(d.shifted, T)
        for b in range(2):
            for g in range(2):
                r = slice(64 * g, 64 * g + 64)
                mm = pe.matmul(k.w1[64 * b:64 * b + 64, 512 * g:512 * g + 512], k.s_qT[r, s, 64 * b:64 * b + 64],
                               k.s_k8[r, s, :, 64 * b:64 * b + 64], start=True, stop=True)
        mm.then_inc(d.s_psum, 1)

    def tail(T, s, ahead=1):
        pe.wait_ge(d.exp, T + 1)
        pe.wait_ge(d.pT_ready, T)
        for h in range(PAIRS):
            mm = pe.transpose(k.w2[:, h * P:(h + 1) * P],
                              k.prob[:, s, 2 * h:2 * h + 2, :].rearrange("p a m -> p (a m)"), k.ident[:, :])
        mm.then_inc(d.pT_psum, 1)
        wait_apart(pe, k, d.pT_ready, T + 1)
        pe.wait_ge(d.q_ready, T + 1 + ahead)
        for b in range(2):
            for h in range(PAIRS):
                mm = pe.matmul(k.w0[64 * b:64 * b + 64, 16 * h:16 * h + 16], k.probT[:, h, 64 * b:64 * b + 64],
                               k.s_v[:, s, b, h, :, :].rearrange("p a d -> p (a d)"), start=True, stop=True)
        mm.then_inc(d.o_psum, 1)
        pe.wait_ge(d.rows, T + 1)
        pe.wait_ge(d.k8_ready, T + 1 + ahead)
        pe.transpose(k.w0[:, 512:512 + P], k.s_rows[:, :], k.ident[:, :]).then_inc(d.o_turned, 1)
        pe.wait_ge(d.oT_ready, T + 1)
        pe.wait_ge(d.updated, T)
        pe.matmul(k.py[:, 0:P], k.s_oT[:, :], k.s_w[:, n, 3, :], start=True, stop=False)
        pe.matmul(k.py[:, 0:P], k.ones[0:1, :], k.s_bo[0:1, n, :], start=False, stop=True).then_inc(d.y_psum, 1)

    def step(T, s, t):
        front(T, s)
        tail(T - 1, 1 - s)
        scores(T, s)

    front(first, 0)
    scores(first, 0)
    steps(pe, first, step)
    tail(first + TILES - 1, 1, ahead=0)


def small_scalar(act, k, n, scale):
    d, first = k.d, PHANTOM + TILES * n

    def front(T, s):
        act.wait_ge(d.xT_psum, T + 1)
        act.copy(k.xT[:, s, :], k.pt[:, 0:P]).then_inc(d.xT_ready, 1)
        act.wait_ge(d.q_psum, T + 1)
        act.activation(k.s_qT[:, s, :], k.w0[:, 0:P], ACT.Identity, bias=k.s_cols[:, n, 0:1]).then_inc(d.q_ready, 1)
        act.wait_ge(d.v_psum, T + 1)
        for p in range(2):
            last = act.copy(k.s_v[64 * p:64 * p + 64, s, :, :, p, :],
                            k.pt[64 * p:64 * p + 64, 0:P].rearrange("p (b h d) -> p b h d", b=2, d=8))
        last.then_inc(d.v_ready, 1)

    def exp(T, s):
        act.wait_ge(d.shifted, T + 1)
        act.activation(k.prob[:, s, :, :], k.logit[:, s, :, :], ACT.Exp, scale=scale).then_inc(d.exp, 1)

    def tail(T):
        act.wait_ge(d.pT_psum, T + 1)
        act.wait_ge(d.o_psum, T)
        act.copy(k.probT[:, :, :], k.w2[:, :]).then_inc(d.pT_ready, 1)
        act.wait_ge(d.o_turned, T + 1)
        act.wait_ge(d.y_psum, T)
        act.activation(k.s_oT[:, :], k.w0[:, 512:512 + P], ACT.Identity,
                       bias=k.s_cols[:, n, 2:3]).then_inc(d.oT_ready, 1)

    def step(T, s, t):
        exp(T - 1, 1 - s)
        front(T, s)
        tail(T - 1)

    front(first, 0)
    steps(act, first, step)
    last = first + TILES - 1
    exp(last, 1)
    tail(last)


def small_vector(dve, k, n):
    d, first = k.d, PHANTOM + TILES * n

    def norm(T, s, t):
        rows = tile(k.x, t)
        stats_vector(dve, k, k.norm, T + TILES, s, rows)
        dve.wait_ge(d.xT_psum, T - 1)
        normalise_vector(dve, k, k.norm, T + TILES, s, rows, k.normed[:, s, :]).then_inc(k.norm.normed, 1)

    def keys(T, s):
        dve.wait_ge(d.k_psum, T + 1)
        dve.scalar_tensor_tensor(out=k.s_k8[:, s, :, :], in0=k.w0[:, None, 512:512 + P].broadcast_to([P, 8, P]),
                                 scalar=k.s_cols[:, n, 1:2], in1=k.member[:, :, None].broadcast_to([P, 8, P]),
                                 op0=ALU.add, op1=ALU.mult).then_inc(d.k8_ready, 1)

    def softmax(T, s):
        logits = k.w1[:, :].rearrange("p (h m) -> p h m", m=SEQ)
        dve.wait_ge(d.s_psum, T + 1)
        dve.tensor_reduce(k.top[:, s, :], logits, AX.X, ALU.max).then_inc(d.top, 1)
        dve.wait_ge(d.top, T + 1)
        dve.tensor_tensor(k.logit[:, s, :, :], logits, k.top[:, s, :, None].broadcast_to([P, HEADS, SEQ]),
                          ALU.subtract).then_inc(d.shifted, 1)

    def total(T, s):
        dve.wait_ge(d.exp, T + 1)
        dve.tensor_reduce(k.den[:, s, :], k.prob[:, s, :, :], AX.X, ALU.add).then_inc(d.den, 1)
        dve.wait_ge(d.den, T + 1)
        dve.reciprocal(k.rden[:, s, :], k.den[:, s, :]).then_inc(d.rden, 1)

    def tail(T, s, t):
        dve.wait_ge(d.o_psum, T + 1)
        dve.wait_ge(d.rden, T + 1)
        dve.wait_ge(d.o_turned, T)
        dve.tensor_tensor(k.s_rows[:, :].rearrange("p (h d) -> p h d", d=8),
                          k.w0[:, 0:P].rearrange("p (h d) -> p h d", d=8),
                          k.rden[:, s, :, None].broadcast_to([P, HEADS, 8]), ALU.mult).then_inc(d.rows, 1)
        dve.wait_ge(d.y_psum, T + 1)
        dve.tensor_tensor(tile(k.x, t), tile(k.x, t), k.py[:, 0:P], ALU.add).then_inc(d.updated, 1)

    def step(T, s, t):
        softmax(T - 1, 1 - s)
        norm(T, s, t)
        keys(T, s)
        total(T - 1, 1 - s)
        tail(T - 1, 1 - s, t - 1)

    norm(first, 0, 0)
    keys(first, 0)
    steps(dve, first, step)
    last = first + TILES - 1
    softmax(last, 1)
    total(last, 1)
    tail(last, 1, TILES - 1)


def small_gpsimd(pool, k, n):
    first = PHANTOM + TILES * n

    def step(T, s, t):
        rstd_gpsimd(pool, k, k.norm, T + TILES, s)

    step(first, 0, 0)
    steps(pool, first, step)



def quantise_vector(dve, k):
    q = k.quant
    w = k.s_w[:, 2, :, :]
    dve.tensor_reduce(k.wmax[:, :], w, AX.X, ALU.max, apply_absolute_value=True).then_inc(q.wmax, 1)
    dve.wait_ge(q.turned, 1)
    link(dve, k, dve.tensor_reduce(k.wmaxT[:, :], k.pt[0:4, 0:P], AX.X, ALU.max))
    dve.tensor_scalar(k.wdiag[:, :], k.ident[0:4, 0:4], k.wmaxT[:, 0:1], None, ALU.mult).then_inc(q.diag, 1)
    dve.wait_ge(q.spread, 1)
    link(dve, k, dve.tensor_scalar(k.wstep[:, :], k.pt[:, P:P + 4], 1.0 / 127.0, None, ALU.mult))
    link(dve, k, dve.reciprocal(k.wrstep[:, :], k.wstep[:, :]))
    wide = (lambda c: c[:, :, None].broadcast_to([P, 4, P]))
    link(dve, k, dve.tensor_tensor(w, w, wide(k.wrstep), ALU.mult))
    link(dve, k, dve.tensor_scalar(w, w, 12582912.0, 12582912.0, ALU.add, ALU.subtract))
    link(dve, k, dve.tensor_scalar(w, w, -128.0, 127.0, ALU.max, ALU.min))
    dve.tensor_tensor(w, w, wide(k.wstep), ALU.mult).then_inc(q.done, 1)


def quantise_tensor(pe, k):
    pe.wait_ge(k.quant.wmax, 1)
    pe.transpose(k.pt[0:4, 0:P], k.wmax[:, :], k.ident[:, :]).then_inc(k.quant.turned, 1)
    pe.wait_ge(k.quant.diag, 1)
    pe.matmul(k.pt[:, P:P + 4], k.ones4[:, :], k.wdiag[:, :], start=True, stop=True).then_inc(k.quant.spread, 1)
    pe.wait_ge(k.quant.done, 1)



def fp8_weight_vector(dve, k):
    integer = mybir.dt.int32
    link(dve, k, dve.tensor_copy(k.f_int[:, :], k.f_bytes[:, :]))
    link(dve, k, dve.tensor_scalar(k.f_mag[:, :], k.f_int[:, :], 127, None, ALU.bitwise_and))
    link(dve, k, dve.tensor_scalar(k.f_low[:, :], k.f_mag[:, :], 2.0 ** -9, 2.0 ** -6, ALU.mult, ALU.min))
    link(dve, k, dve.tensor_scalar(k.f_val[:, :].bitcast(integer), k.f_mag[:, :], 20, None, ALU.logical_shift_left))
    link(dve, k, dve.scalar_tensor_tensor(out=k.f_val[:, :], in0=k.f_val[:, :], scalar=2.0 ** 120,
                                          in1=k.f_low[:, :], op0=ALU.mult, op1=ALU.max))
    link(dve, k, dve.tensor_scalar(k.f_low[:, :], k.f_int[:, :], 128.0, -2.0, ALU.is_ge, ALU.mult))
    dve.scalar_tensor_tensor(out=k.f_w[:, :], in0=k.f_low[:, :], scalar=1.0, in1=k.f_val[:, :],
                             op0=ALU.add, op1=ALU.mult).then_inc(k.f.weight, 1)


def fp8_vector(dve, k):
    f = k.f
    y, words = k.y[:, :, :], k.logit[:, :, :, :].rearrange("p a h n -> p (a h n)").rearrange("p (t n) -> p t n", n=P)
    wide = (lambda c: c[:, :, None].broadcast_to([P, TILES, P]))
    dve.wait_ge(k.all_normed, 2)
    link(dve, k, dve.tensor_reduce(k.f_scale[:, :], y, AX.X, ALU.max, apply_absolute_value=True))
    link(dve, k, dve.tensor_scalar(k.f_scale[:, :], k.f_scale[:, :], 1e-12, 1.0 / 448.0, ALU.max, ALU.mult))
    link(dve, k, dve.reciprocal(k.f_rscale[:, :], k.f_scale[:, :]))
    link(dve, k, dve.tensor_tensor(y, y, wide(k.f_rscale), ALU.mult))
    link(dve, k, dve.tensor_scalar(words.bitcast(mybir.dt.int32), y.bitcast(mybir.dt.int32), 0x7F800000, None,
                                   ALU.bitwise_and))
    link(dve, k, dve.tensor_scalar(words, words, 2.0 ** -6, 1.5 * 2.0 ** 20, ALU.max, ALU.mult))
    link(dve, k, dve.tensor_tensor(y, y, words, ALU.add))
    dve.tensor_tensor(k.f_q[:, :, :], y, words, ALU.subtract).then_inc(f.quantised, 1)
    link(dve, k, dve.tensor_tensor(k.x[:, :, :], k.x[:, :, :], k.f_bias[:, None, :].broadcast_to([P, TILES, P]),
                                   ALU.add))
    link(dve, k, dve.tensor_scalar(k.f_scale[:, :], k.f_scale[:, :], k.f_ws[:, 0:1], None, ALU.mult))
    for t in range(TILES):
        w = k.w1 if t < 8 else k.w2
        if t % 8 == 0:
            dve.wait_ge(f.product, t // 8 + 1)
        last = dve.scalar_tensor_tensor(out=k.x[:, t, :], in0=w[:, (t % 8) * P:(t % 8 + 1) * P],
                                        scalar=k.f_scale[:, t:t + 1], in1=k.x[:, t, :], op0=ALU.mult, op1=ALU.add)
    last.then_inc(f.done, 1)
    dve.wait_ge(f.done, 1)


def fp8_tensor(pe, k):
    f, turned = k.f, k.w0[:, :].bitcast(BF16)
    pe.wait_ge(f.quantised, 1)
    pe.wait_ge(f.weight, 1)
    for t in range(TILES):
        mm = pe.transpose(turned[:, t * P:(t + 1) * P], k.f_q[:, t, :], k.ident16[:, :])
        if t % 8 == 7:
            mm.then_inc(f.turned, 1)
    for t in range(TILES):
        if t % 8 == 0:
            pe.wait_ge(f.qT, t // 8 + 1)
        w = k.w1 if t < 8 else k.w2
        mm = pe.matmul(w[:, (t % 8) * P:(t % 8 + 1) * P], k.f_qT[:, t, :], k.f_w[:, :], start=True, stop=True)
        if t % 8 == 7:
            mm.then_inc(f.product, 1)


def fp8_scalar(act, k):
    f, turned = k.f, k.w0[:, :].bitcast(BF16)
    for c in range(2):
        act.wait_ge(f.turned, c + 1)
        act.copy(k.f_qT[:, 8 * c:8 * c + 8, :], turned[:, 1024 * c:1024 * c + 1024]).then_inc(f.qT, 1)



def experts_prelude_tensor(pe, k, e, similar):
    for q in range(QUADS):
        if q == 0:
            pe.wait_ge(k.all_normed, 4 if similar else 3)
        else:
            pe.wait_ge(e.xnT, q)
        for j in range(4):
            mm = pe.transpose(k.pt[:, j * P:(j + 1) * P], k.y[:, 4 * q + j, :], k.ident[:, :])
        mm.then_inc(e.turned, 1)
        pe.wait_ge(e.xnT, q + 1)
        if similar:
            w = (k.w0, k.w1)[q // 2]
            pe.matmul(w[:, 512 * (q % 2):512 * (q % 2) + 512], k.m_wp[:, :], k.m_xT[:, q, :],
                      start=True, stop=True).then_inc(e.raw, 1)
        else:
            for j in range(4):
                t = 4 * q + j
                mm = pe.matmul(k.py[:, 8 * t:8 * t + 8], k.m_xT[:, q, j * P:(j + 1) * P], k.m_wr[:, :],
                               start=True, stop=True)
    if similar:
        pe.wait_ge(e.sim_scaled, 1)
        pe.transpose(k.pt[:, 0:8], k.m_sim[:, :], k.ident[0:8, 0:8]).then_inc(e.sim_turned, 1)
        pe.wait_ge(e.sim_T, 1)
        for t in range(TILES):
            if t % 4 == 0:
                pe.wait_ge(e.projT, t // 4 + 1)
                pe.wait_ge(e.squares, t // 4 + 1)
            pe.matmul(k.py[:, 8 * t:8 * t + 8], k.m_projT[:, t * P:(t + 1) * P], k.m_wr[:, :], start=True, stop=True)
            mm = pe.matmul(k.py[:, P + t:P + t + 1], k.m_sq[:, t * P:(t + 1) * P], k.onescol[:, :],
                           start=True, stop=True)
    mm.then_inc(e.logits, 1)


def experts_tensor(pe, k, e, ne):
    bank = (lambda i: k.w2[:, 512 * (i % 2):512 * (i % 2) + 512])

    def quad(q):
        G = (lambda i: q * ne + (e.first + i))

        def hidden(i):
            for c in range(4):
                w = (k.w0, k.w1)[c // 2]
                pe.wait_ge(e.hid_ready, 4 * G(i) + (c - 3))
                pe.matmul(w[:, 512 * (c % 2):512 * (c % 2) + 512], k.m_fc[:, i, c * P:(c + 1) * P],
                          k.m_xT[:, bass.ds(q, 1), :].rearrange("p a n -> p (a n)"),
                          start=True, stop=True).then_inc(e.hid_psum, 1)

        def output(i):
            pe.wait_ge(e.hid_ready, 4 * G(i) + 4)
            pe.wait_ge(e.scaled, slot_before(G(i), i, ne))
            for j in range(4):
                for c in range(4):
                    mm = pe.matmul(bank(i)[:, j * P:(j + 1) * P], k.m_hid[i % 2][:, c, j * P:(j + 1) * P],
                                   k.m_proj[:, i, c, :], start=(c == 0), stop=(c == 3))
            mm.then_inc(e.out_psum, 1)

        for i in range(ne):
            hidden(i)
            if i:
                output(i - 1)
        output(ne - 1)

    with pe.Fori(0, QUADS) as q:
        quad(q)


def slot_before(G, i, ne):
    return G if i == 0 and ne % 2 else G - 1


def experts_bias_tensor(pe, k, e, ne):
    pe.wait_ge(e.gates, 1)
    for t in range(TILES):
        w = k.w0 if t < 8 else k.w1
        mm = pe.transpose(w[0:ne, (t % 8) * P:(t % 8 + 1) * P], k.m_gate[:, t, 0:ne], k.ident[:, :])
        if t % 8 == 7:
            mm.then_inc(e.gate_turned, 1)
    for t in range(TILES):
        if t % 8 == 0:
            pe.wait_ge(e.gateT, t // 8 + 1)
            if t == 0:
                pe.wait_ge(e.scaled, e.first + ne * QUADS)
        w = k.w2 if t < 8 else k.w0
        mm = pe.matmul(w[:, (t % 8) * P:(t % 8 + 1) * P], k.m_gateT[0:ne, t * P:(t + 1) * P], k.m_brow[0:ne, :],
                       start=True, stop=True)
        if t % 8 == 7:
            mm.then_inc(e.bias_psum, 1)


def experts_scalar(act, k, e, ne, similar, gelu):
    for q in range(QUADS):
        act.wait_ge(e.turned, q + 1)
        act.copy(k.m_xT[:, q, :], k.pt[:, :]).then_inc(e.xnT, 1)
        if similar:
            w = (k.w0, k.w1)[q // 2][:, 512 * (q % 2):512 * (q % 2) + 512]
            act.wait_ge(e.raw, q + 1)
            act.copy(k.m_projT[:, 512 * q:512 * q + 512], w).then_inc(e.projT, 1)
            act.activation(k.m_sq[:, 512 * q:512 * q + 512], w, ACT.Square).then_inc(e.squares, 1)
    if similar:
        act.wait_ge(e.sim_turned, 1)
        act.copy(k.m_wr[:, :], k.pt[:, 0:8]).then_inc(e.sim_T, 1)
    act.wait_ge(e.below, 1)
    act.activation(k.m_exp[:, :, :], k.m_exp[:, :, :], ACT.Exp).then_inc(e.exp, 1)

    with act.Fori(0, QUADS) as q:
        for i in range(ne):
            G = q * ne + (e.first + i)
            for c in range(4):
                w = (k.w0, k.w1)[c // 2]
                act.wait_ge(e.hid_psum, 4 * G + (c + 1))
                if c == 0:
                    act.wait_ge(e.out_psum, slot_before(G, i, ne))
                act.activation(k.m_hid[i % 2][:, c, :], w[:, 512 * (c % 2):512 * (c % 2) + 512], gelu,
                               bias=k.m_bfc[:, i, c:c + 1]).then_inc(e.hid_ready, 1)
    for c in range(2):
        act.wait_ge(e.gate_turned, c + 1)
        act.copy(k.m_gateT[0:ne, 1024 * c:1024 * c + 1024], (k.w0, k.w1)[c][0:ne, :]).then_inc(e.gateT, 1)


def similar_vector(dve, k, e):
    dve.wait_ge(e.loaded, 16 * EXPERT3_LOADS)
    link(dve, k, dve.tensor_tensor(k.m_simsq[:, :], k.m_sim[:, :], k.m_sim[:, :], ALU.mult))
    dve.reciprocal(k.m_rtemp[:, :], k.m_temp[:, :]).then_inc(e.cooled, 1)
    dve.tensor_reduce(k.m_simn[:, :], k.m_simsq[:, :], AX.X, ALU.add).then_inc(e.sim_norm2, 1)
    dve.wait_ge(e.sim_rnorm, 1)
    dve.tensor_scalar(k.m_sim[:, :], k.m_sim[:, :], k.m_simn[:, 0:1], None, ALU.mult).then_inc(e.sim_scaled, 1)


def gates_vector(dve, k, e, similar):
    lg, wide = k.m_logit[:, :, :], [P, TILES, 8]
    dve.wait_ge(e.logits, 1)
    raw = k.py[:, 0:P].rearrange("p (t e) -> p t e", e=8)
    if similar:
        dve.tensor_copy(k.m_norm2[:, :], k.py[:, P:P + TILES]).then_inc(e.norm2, 1)
        dve.wait_ge(e.rnorm, 1)
        link(dve, k, dve.tensor_tensor(lg, raw, k.m_norm2[:, :, None].broadcast_to(wide), ALU.mult))
        dve.wait_ge(e.cooled, 1)
        link(dve, k, dve.tensor_scalar(lg, lg, k.m_rtemp[:, 0:1], None, ALU.mult))
    else:
        link(dve, k, dve.tensor_copy(lg, raw))
    link(dve, k, dve.tensor_reduce(k.m_top[:, :], lg, AX.X, ALU.max))
    dve.tensor_tensor(k.m_exp[:, :, :], lg, k.m_top[:, :, None].broadcast_to(wide), ALU.subtract).then_inc(e.below, 1)
    pairs = [P, TILES, 8, 8]
    split = (lambda b: b.rearrange("p t (e j) -> p t e j", e=8))
    link(dve, k, dve.tensor_tensor(split(k.m_greater), lg[:, :, None, :].broadcast_to(pairs), lg[:, :, :, None].broadcast_to(pairs),
                                   ALU.is_gt))
    link(dve, k, dve.tensor_tensor(split(k.m_equal), lg[:, :, None, :].broadcast_to(pairs), lg[:, :, :, None].broadcast_to(pairs),
                                   ALU.is_equal))
    link(dve, k, dve.tensor_tensor(k.m_equal, k.m_equal, k.m_tri[:, None, :].broadcast_to([P, TILES, SEQ]),
                                   ALU.mult))
    link(dve, k, dve.tensor_tensor(k.m_equal, k.m_equal, k.m_greater, ALU.add))
    link(dve, k, dve.tensor_reduce(k.m_rank[:, :, :], split(k.m_equal), AX.X, ALU.add))
    dve.wait_ge(e.exp, 1)
    link(dve, k, dve.scalar_tensor_tensor(out=k.m_exp[:, :, :], in0=k.m_rank[:, :, :], scalar=2.0, in1=k.m_exp[:, :, :],
                                          op0=ALU.is_lt, op1=ALU.mult))
    link(dve, k, dve.tensor_reduce(k.m_top[:, :], k.m_exp[:, :, :], AX.X, ALU.add))
    link(dve, k, dve.reciprocal(k.m_top[:, :], k.m_top[:, :]))
    dve.tensor_tensor(k.m_gate[:, :, 0:8], k.m_exp[:, :, :], k.m_top[:, :, None].broadcast_to(wide),
                      ALU.mult).then_inc(e.gates, 1)
    dve.wait_ge(e.gates, 1)


def experts_vector(dve, k, e, ne, similar):
    if similar:
        similar_vector(dve, k, e)
    gates_vector(dve, k, e, similar)
    with dve.Fori(0, QUADS) as q:
        for i in range(ne):
            G = q * ne + (e.first + i)
            bank = k.w2[:, 512 * (i % 2):512 * (i % 2) + 512].rearrange("p (j n) -> p j n", j=4)
            dve.wait_ge(e.out_psum, G + 1)
            dve.wait_ge(e.added, slot_before(G, i, ne))
            dve.tensor_tensor(k.m_scaled[:, i % 2, :, :], bank,
                              k.m_gate[:, bass.ds(q * 4, 4), i:i + 1].broadcast_to([P, 4, P]),
                              ALU.mult).then_inc(e.scaled, 1)
    dve.wait_ge(e.added, e.first + ne * QUADS)
    for c in range(2):
        dve.wait_ge(e.bias_psum, c + 1)
        rows = k.x[:, 8 * c:8 * c + 8, :].rearrange("p t n -> p (t n)")
        dve.tensor_tensor(rows, rows, (k.w2, k.w0)[c][:, :], ALU.add).then_inc(e.done, 1)
    dve.wait_ge(e.done, 2)


def experts_gpsimd(pool, k, e, ne, similar):
    if similar:
        pool.wait_ge(e.sim_norm2, 1)
        pool.tensor_scalar(k.m_simn[:, :], k.m_simn[:, :], 1e-24, None, ALU.max).then_inc(e.sim_floor, 1)
        pool.wait_ge(e.sim_floor, 1)
        pool.tensor_tensor(k.m_simn[:, :], k.m_simn[:, :], k.power[0:8, 0:1], ALU.pow).then_inc(e.sim_rnorm, 1)
        pool.wait_ge(e.norm2, 1)
        pool.tensor_scalar(k.m_norm2[:, :], k.m_norm2[:, :], 1e-24, None, ALU.max).then_inc(e.floor, 1)
        pool.wait_ge(e.floor, 1)
        pool.tensor_tensor(k.m_norm2[:, :], k.m_norm2[:, :], k.power[:, :], ALU.pow).then_inc(e.rnorm, 1)
    with pool.Fori(0, QUADS) as q:
        for i in range(ne):
            G = q * ne + (e.first + i)
            rows = k.x[:, bass.ds(q * 4, 4), :]
            wait_apart(pool, k, e.scaled, G + 1)
            pool.wait_ge(e.added, G)
            pool.tensor_tensor(rows, rows, k.m_scaled[:, i % 2, :, :], ALU.add).then_inc(e.added, 1)



def first_loads(k, a):
    return [
        (k.x[:, :, :], a["x"].rearrange("(t p) d -> p t d", p=P)),
        (k.a_ly[:, :], a["a_ly"]), (k.a_lx[:, :], a["a_lx"]), (k.a_tx[:, :, :], a["a_tx"]),
        (k.a_ty[:, :, :], a["a_ty"]), (k.a_lo[:, :], a["a_lo"]), (k.a_to0[:, :], a["a_to0"]),
        (k.a_to1[:, :], a["a_to1"]), (k.a_mask[0:SEQ, :], a["a_mask"]), (k.a_mask[SEQ:P, :], a["a_mask"]),
        (k.rope[:, :], a["rope"]), (k.band[:, :], a["band"]), (k.shift[:, :], a["shift"]),
        (k.s_w[:, :, :, :], a["s_w"]), (k.s_cols[:, :, :], a["s_cols"]), (k.s_bo[:, :, :], a["s_bo"]),
        (k.member[:, :], a["member"]), (k.m_tri[:, :], a["m_tri"]),
        (k.f_bytes[:, :], a["f_w"]), (k.f_ws[:, :], a["f_ws"].partition_broadcast(P)),
        (k.f_bias[:, :], a["f_bias"].partition_broadcast(P)),
    ]


N_LOADS = 21

B_LOADS, C_LOADS = 3, 4


def load_local(sp, k, a, d):
    row = (lambda x: x[d]) if isinstance(d, int) else (lambda x: x[bass.ds(d, 1)].rearrange("a p n -> p (a n)"))
    sp.dma_start(k.b_wqkv[:, :], row(a["b_wqkv"])).then_inc(k.b_loaded, 16)
    sp.dma_start(k.b_wo[:, :, :].rearrange("p h n -> p (h n)"), row(a["b_wo"])).then_inc(k.b_loaded, 16)
    sp.dma_start(k.b_scales[:, :], row(a["b_scales"]).partition_broadcast(P)).then_inc(k.b_loaded, 16)


def load_gated(sp, k, a, d):
    row = (lambda x: x[d]) if isinstance(d, int) else (lambda x: x[bass.ds(d, 1)].rearrange("a p n -> p (a n)"))
    sp.dma_start(k.c_w1[:, :], row(a["c_w1"])).then_inc(k.c_loaded, 16)
    sp.dma_start(k.c_w2[:, :, :].rearrange("p c n -> p (c n)"), row(a["c_w2"])).then_inc(k.c_loaded, 16)
    sp.dma_start(k.c_cols[:, :], row(a["c_cols"])).then_inc(k.c_loaded, 16)
    sp.dma_start(k.c_b2[:, :], row(a["c_b2"])).then_inc(k.c_loaded, 16)


def layers(eng, run):
    with eng.Fori(0, DEPTH) as d:
        run(d * TILES + (PHANTOM + TILES), d * QUADS + PHANTOM)


def small_ctx(sp, k, a, n):
    first, ctx = PHANTOM + TILES * n, a["ctxT"]
    before = (k.v_psum, PHANTOM + TILES) if n == 0 else (k.d.v_psum, first)
    for s in range(2):
        sp.wait_ge(*before)
        sp.dma_start(k.ctxT[:, s, :], ctx[s, :, :]).then_inc(k.ctx_loaded[s], 16)
    with sp.Fori(2, TILES - 1, 2) as t:
        for s in range(2):
            sp.wait_ge(k.d.v_psum, t + s + (first - 1))
            sp.dma_start(k.ctxT[:, s, :], ctx[bass.ds(t + s, 1), :, :].rearrange("a p n -> p (a n)")
                         ).then_inc(k.ctx_loaded[s], 16)


EXPERT2_LOADS, EXPERT3_LOADS = 5, 7


def load_experts(sp, k, a, n, e, ne):
    pairs = [(k.m_fc[:, 0:ne, :], a[f"m{n}_fc"]), (k.m_proj[:, 0:ne, :, :], a[f"m{n}_proj"]),
             (k.m_bfc[:, 0:ne, :], a[f"m{n}_bfc"]), (k.m_brow[0:ne, :], a[f"m{n}_brow"])]
    if n == 2:
        pairs += [(k.m_wr[:, :], a["m2_wr"])]
    else:
        pairs += [(k.m_wp[:, :], a["m3_wp"]), (k.m_sim[:, :], a["m3_sim"]),
                  (k.m_temp[:, :], a["m3_temp"].partition_broadcast(P))]
    for dst, src in pairs:
        sp.dma_start(dst, src).then_inc(e.loaded, 16)


def sync_program(nc, sp, k, a, out):
    first = PHANTOM
    for dst, src in first_loads(k, a):
        sp.dma_start(dst, src).then_inc(k.loaded, 16)
    ctx = a["ctxT"]
    for s in range(2):
        sp.dma_start(k.ctxT[:, s, :], ctx[s, :, :]).then_inc(k.ctx_loaded[s], 16)
    load_local(sp, k, a, 0)
    load_gated(sp, k, a, 0)
    with sp.Fori(2, TILES - 1, 2) as t:
        for s in range(2):
            sp.wait_ge(k.v_psum, t + s + first - 1)
            sp.dma_start(k.ctxT[:, s, :], ctx[bass.ds(t + s, 1), :, :].rearrange("a p n -> p (a n)")
                         ).then_inc(k.ctx_loaded[s], 16)
    sp.wait_ge(k.updated, PHANTOM + TILES)
    load_experts(sp, k, a, 2, k.e[0], 9)
    with sp.Fori(1, DEPTH) as d:
        sp.wait_ge(k.updated, d * TILES + (PHANTOM + TILES))
        load_local(sp, k, a, d)
        sp.wait_ge(k.y_done, d * QUADS + PHANTOM)
        load_gated(sp, k, a, d)
    small_ctx(sp, k, a, 0)
    small_ctx(sp, k, a, 1)
    sp.wait_ge(k.e[0].done, 2)
    load_experts(sp, k, a, 3, k.e[1], 8)
    small_ctx(sp, k, a, 2)
    sp.wait_ge(k.e[1].done, 2)
    sp.dma_start(out.rearrange("(t p) d -> p t d", p=P), k.x[:, :, :]).then_inc(k.stored, 16)
    sp.wait_ge(k.stored, 16)


def tensor_program(nc, pe, k):
    pe.wait_ge(k.loaded, 16 * N_LOADS)
    pe.wait_ge(k.consts, 5)
    cross0_tensor(pe, k, PHANTOM)

    def run(first, qfirst):
        local_tensor(pe, k, first)
        gated_tensor(pe, k, first, qfirst)
    layers(pe, run)
    pe.wait_ge(k.y_done, PHANTOM + DEPTH * QUADS)
    small_tensor(pe, k, 0)
    fp8_tensor(pe, k)
    pe.wait_ge(k.f.done, 1)
    small_tensor(pe, k, 1)
    experts2, experts3 = k.e
    pe.wait_ge(experts2.loaded, 16 * EXPERT2_LOADS)
    pe.wait_ge(k.d.updated, PHANTOM + 2 * TILES)
    experts_prelude_tensor(pe, k, experts2, False)
    experts_tensor(pe, k, experts2, 9)
    experts_bias_tensor(pe, k, experts2, 9)
    pe.wait_ge(experts2.done, 2)
    quantise_tensor(pe, k)
    small_tensor(pe, k, 2)
    pe.wait_ge(experts3.loaded, 16 * EXPERT3_LOADS)
    pe.wait_ge(k.d.updated, PHANTOM + 3 * TILES)
    experts_prelude_tensor(pe, k, experts3, True)
    experts_tensor(pe, k, experts3, 8)
    experts_bias_tensor(pe, k, experts3, 8)


def scalar_program(nc, act, k):
    act.wait_ge(k.consts, 5)
    cross0_scalar(act, k, PHANTOM)

    def run(first, qfirst):
        local_scalar(act, k, first)
        gated_scalar(act, k, first, qfirst)
    layers(act, run)
    small_scalar(act, k, 0, 8 ** -0.5)
    fp8_scalar(act, k)
    small_scalar(act, k, 1, 1.0)
    experts_scalar(act, k, k.e[0], 9, False, ACT.Gelu_apprx_tanh)
    small_scalar(act, k, 2, 8 ** -0.5)
    experts_scalar(act, k, k.e[1], 8, True, ACT.Gelu)


def vector_program(nc, dve, k):
    dve.memset(k.ones[:, :], 1.0).then_inc(k.consts, 1)
    dve.memset(k.sT[:, :, :], 0.0).then_inc(k.consts, 1)
    dve.memset(k.s_v[:, :, :, :, :, :], 0.0)
    dve.memset(k.m_gate[:, :, 8:9], 1.0)
    dve.memset(k.onescol[:, :], 1.0)
    dve.memset(k.ones4[:, :], 1.0).then_inc(k.consts, 1)
    dve.wait_ge(k.loaded, 16 * N_LOADS)
    cross0_vector(dve, k, PHANTOM)
    dve.wait_ge(k.updated, PHANTOM + TILES)
    fresh_vector(dve, k, 1)

    def run(first, qfirst):
        local_vector(dve, k, first)
        gated_vector(dve, k, first, qfirst)
    layers(dve, run)
    dve.wait_ge(k.y_done, PHANTOM + DEPTH * QUADS)
    dve.tensor_tensor(k.x[:, :, :], k.x[:, :, :], k.y[:, :, :], ALU.add).then_inc(k.x_done, 1)
    dve.wait_ge(k.x_done, 1)
    small_vector(dve, k, 0)
    dve.wait_ge(k.d.updated, PHANTOM + TILES)
    fresh_vector(dve, k, 2)
    fp8_weight_vector(dve, k)
    fp8_vector(dve, k)
    small_vector(dve, k, 1)
    dve.wait_ge(k.d.updated, PHANTOM + 2 * TILES)
    fresh_vector(dve, k, 3)
    experts_vector(dve, k, k.e[0], 9, False)
    quantise_vector(dve, k)
    small_vector(dve, k, 2)
    dve.wait_ge(k.d.updated, PHANTOM + 3 * TILES)
    fresh_vector(dve, k, 4)
    experts_vector(dve, k, k.e[1], 8, True)


def gpsimd_program(nc, pool, k):
    pool.memset(k.ident[:, :], 0.0).then_inc(k.powers, 1)
    pool.memset(k.power[:, :], -0.5).then_inc(k.powers, 1)
    pool.memset(k.eps[:, :], EPS).then_inc(k.powers, 1)
    pool.wait_ge(k.powers, 3)
    pool.affine_select(out=k.ident[:, :], in_=k.ident[:, :], compare_op=ALU.not_equal, fill=1.0, base=0,
                       pattern=[[-1, P]], channel_multiplier=1).then_inc(k.consts, 1)
    pool.wait_ge(k.consts, 4)
    pool.tensor_copy(k.ident16[:, :], k.ident[:, :]).then_inc(k.consts, 1)
    cross0_gpsimd(pool, k, PHANTOM)
    fresh_gpsimd(pool, k, 1)
    pool.wait_ge(k.all_normed, 1)

    def run(first, qfirst):
        local_gpsimd(pool, k, first, qfirst)
        gated_gpsimd(pool, k, first, qfirst)
    layers(pool, run)
    small_gpsimd(pool, k, 0)
    fresh_gpsimd(pool, k, 2)
    small_gpsimd(pool, k, 1)
    fresh_gpsimd(pool, k, 3)
    experts_gpsimd(pool, k, k.e[0], 9, False)
    small_gpsimd(pool, k, 2)
    fresh_gpsimd(pool, k, 4)
    experts_gpsimd(pool, k, k.e[1], 8, True)



def tables():
    f = np.float32
    half = np.arange(0, HD, 2, dtype=f)
    t = np.arange(SEQ, dtype=f)
    angle = t[:, None] * (f(1.0) / f(10000.0) ** (half / f(HD)))[None, :]
    base = (half + f(0.4 * HD)) / f(1.4 * HD)
    grow = base[None, :] ** ((t - SEQ // 2) / (WINDOW // 2))[:, None]
    cos, sin = np.cos(angle), np.sin(angle)
    rope = np.concatenate([cos * grow, cos * grow, -sin * grow, sin * grow,
                           cos / grow, cos / grow, -sin / grow, sin / grow], axis=1).astype(f)
    i, j = np.arange(SEQ)[:, None], np.arange(SEQ)[None, :]
    band = np.where((i < j) | (i > j + WINDOW), f(-1e30), f(0)).astype(f)
    shift = np.eye(P, k=1, dtype=f)
    shift[SEQ - 1, SEQ] = 0
    member = (np.arange(P)[:, None] % 64 // 8 == np.arange(8)[None, :]).astype(f)
    lower = np.tile(np.tril(np.ones((8, 8), f), -1).reshape(1, 64), (P, 1))
    return {"m_tri": lower, "member": member, "rope": np.tile(rope, (2, 1)), "band": np.tile(band, (2, 1)), "shift": shift}


def layout(i):
    n = {name: np.asarray(v) for name, v in i.items()}
    a = {}
    a["x"] = n["x"].reshape(TILES * P, P)
    a["ctxT"] = n["ctx_1024"].reshape(TILES, P, P).transpose(0, 2, 1)
    a["a_mask"] = n["mask_SxS2_ff0"].T
    a["a_ly"] = n["L0_xattn_Ly"].transpose(1, 0, 2).reshape(P, 1024)
    a["a_lx"] = n["L0_xattn_Lx"].transpose(1, 0, 2).reshape(P, 1024)
    a["a_tx"] = n["L0_xattn_Tx"].reshape(PAIRS, 2, P, HD).transpose(2, 1, 0, 3).reshape(P, 2, 512)
    a["a_ty"] = n["L0_xattn_Ty"].reshape(PAIRS, 2, P, HD).transpose(1, 3, 0, 2).reshape(P, PAIRS, P)
    a["a_lo"] = n["L0_xattn_Lo"].reshape(PAIRS, P).T
    a["a_to0"] = n["L0_xattn_To0"].reshape(PAIRS, P).T
    a["a_to1"] = n["L0_xattn_To1"].reshape(1, P)
    wqkv = n["L0_ffn_Wqkv"].reshape(DEPTH, P, 3, PAIRS, 2, HD)
    v_even_first = wqkv[:, :, 2].transpose(0, 1, 3, 2, 4).reshape(DEPTH, P, 1024)
    a["b_wqkv"] = np.concatenate([n["L0_ffn_Wqkv"][:, :, :2048], v_even_first], axis=2)
    a["b_wo"] = n["L0_ffn_Wo"].reshape(DEPTH, PAIRS, P, P).transpose(0, 2, 1, 3).reshape(DEPTH, P, 1024)
    halves = [np.roll(n[s], r, axis=1) for s in ("L0_ffn_q_scale", "L0_ffn_k_scale") for r in (0, HD // 2)]
    a["b_scales"] = np.concatenate(halves, axis=1).reshape(DEPTH, 1, 4 * HD)
    a["c_w1"] = n["L0_ffn_W1"]
    w2 = np.zeros((DEPTH, 3 * P, P), np.float32)
    w2[:, :HID] = n["L0_ffn_W2"]
    a["c_w2"] = w2.reshape(DEPTH, 3, P, P).transpose(0, 2, 1, 3).reshape(DEPTH, P, 3 * P)
    cols = np.zeros((DEPTH, 8, P), np.float32)
    cols[:, 0], cols[:, 1] = n["L0_ffn_ln_g"], n["L0_ffn_ln_b"]
    for c, (at, m) in enumerate(CHUNKS):
        cols[:, 2 + c, :m] = n["L0_ffn_b1"][:, at:at + m]
        cols[:, 5 + c, :m] = n["L0_ffn_b1"][:, HID + at:HID + at + m]
    a["c_cols"] = cols.transpose(0, 2, 1)
    a["c_b2"] = n["L0_ffn_b2"].reshape(DEPTH, 1, P)
    heads_apart = (lambda w: w.reshape(P, PAIRS, 2, 8).transpose(0, 2, 1, 3).reshape(P, P))
    per_stage = [[n["L1_xattn_w_q"], n["L1_xattn_w_k"], n["L1_xattn_w_v"], n["L1_xattn_w_out"]],
                 [n[f"L2_xattn_W{c}"].T for c in "qkvo"], [n[f"L3_xattn_W{c}"].T for c in "qkvo"]]
    a["s_w"] = np.stack([np.stack([wq, wk, heads_apart(wv), wo], 1) for wq, wk, wv, wo in per_stage], 1)
    zero = np.zeros(P, np.float32)
    a["s_cols"] = np.stack([np.stack(c, 1) for c in (
        [n["L1_xattn_b_q"], n["L1_xattn_b_k"], n["L1_xattn_b_v"]], [zero] * 3,
        [n["L3_xattn_bq"], n["L3_xattn_bk"], n["L3_xattn_bv"]])], 1)
    a["s_bo"] = np.stack([n["L1_xattn_b_out"], n["L2_xattn_bo"], n["L3_xattn_bo"]])[None]
    a["f_w"] = n["L1_ffn_weight"].view(np.uint8).T
    a["f_ws"] = n["L1_ffn_weight_scale"].reshape(1, 1)
    a["f_bias"] = n["L1_ffn_bias"].reshape(1, P)
    both = (lambda routed, shared: np.concatenate([routed, shared[None]]))
    layers2 = [both(n["L2_ffn_" + w], n["L2_ffn_" + w + "_s"]) for w in ("Wfc", "bfc", "Wproj", "bproj")]
    layers3 = [n["L3_ffn_" + w] for w in ("W1", "b1", "W2", "b2")]
    for m, (fc, bfc, proj, brow) in ((2, layers2), (3, layers3)):
        a[f"m{m}_fc"] = fc.transpose(1, 0, 2)
        a[f"m{m}_bfc"] = bfc.reshape(-1, 4, P).transpose(2, 0, 1)
        a[f"m{m}_proj"] = proj.reshape(-1, 4, P, P).transpose(2, 0, 1, 3)
        a[f"m{m}_brow"] = brow
    a["m2_wr"] = n["L2_ffn_Wr"]
    a["m3_wp"] = n["L3_ffn_Wp"].T
    a["m3_sim"] = n["L3_ffn_sim_matrix"]
    a["m3_temp"] = n["L3_ffn_temperature"].reshape(1, 1)
    a.update(tables())
    return {name: np.ascontiguousarray(v) for name, v in a.items()}


def kernel(**inputs):
    import concourse.bacc as bacc
    from concourse.bass_utils import run_bass_kernel_spmd

    nc = bacc.Bacc("TRN2", target_bir_lowering=False, num_devices=1)
    arrays = layout(inputs)
    dram = {name: nc.dram_tensor("in_" + name, v.shape, mybir.dt.from_np(v.dtype), kind="ExternalInput").ap()
            for name, v in arrays.items()}
    out = nc.dram_tensor("out", (TILES * P, P), F32, kind="ExternalOutput").ap()
    build(nc, dram, out)
    r = run_bass_kernel_spmd(nc, [{"in_" + name: v for name, v in arrays.items()}], core_ids=[0])
    return r.results[0]["out"].reshape(32, SEQ, P)
```

```python
from contextlib import ExitStack

import numpy as np

import concourse.bass as bass
from concourse import mybir

F32 = mybir.dt.float32
BF16 = mybir.dt.bfloat16
I32 = mybir.dt.int32
ALU = mybir.AluOpType
ACT = mybir.ActivationFunctionType
AX = mybir.AxisListType

P = 128
SEQ = 64
TILES = 16
HEADS, HD = 16, 64
PAIRS = HEADS // 2
DEPTH = 6
WINDOW = 32
EPS = 1e-5
HID = 341
CHUNKS = [(0, 128), (128, 128), (256, 85)]
PHANTOM = 2



class Names:
    pass


def build(nc, a, out):
    ctx = ExitStack()
    with ctx:
        def sb(name, shape, dt=F32):
            return ctx.enter_context(nc.sbuf_tensor(name, shape, dt))

        def pb(name, shape, dt=F32):
            return ctx.enter_context(nc.psum_tensor(name, shape, dt))

        k = Names()
        primed = []

        def sem(name, first=0):
            s = ctx.enter_context(nc.semaphore(name))
            if first:
                primed.append((s, first))
            return s

        k.x = sb("x_all", [P, TILES, P])
        k.y = sb("y_all", [P, TILES, P])
        k.ident = sb("ident", [P, P])
        k.shift = sb("shift", [P, P])
        k.ones = sb("ones", [1, P])
        k.onescol = sb("onescol", [P, 1])
        k.power = sb("power", [P, HEADS])
        k.eps = sb("eps", [P, HEADS])
        k.ctxT = sb("ctxT", [P, 2, P])
        k.stats = sb("stats", [P, 2, 6])
        k.mv = sb("mv", [P, 2, 2])
        k.rstd = sb("rstd", [P, 2, 1])
        k.normed = sb("normed", [P, 2, P])
        k.xT = sb("xT", [P, 2, P])
        k.qT = sb("qT", [P, 2, PAIRS, P])
        k.kT = sb("kT", [P, 2, PAIRS, P])
        k.v2 = sb("v2", [P, 2, 2, 512])
        k.logit = sb("logit", [P, 2, HEADS, SEQ])
        k.prob = sb("prob", [P, 2, HEADS, SEQ])
        k.probT = sb("probT", [P, PAIRS, P])
        k.oT = sb("oT", [P, PAIRS, P])
        k.top = sb("top", [P, 2, HEADS])
        k.den = sb("den", [P, 2, HEADS])
        k.rden = sb("rden", [P, 2, HEADS])
        k.w0 = pb("w0", [P, 1024])
        k.w1 = pb("w1", [P, 1024])
        k.w2 = pb("w2", [P, 1024])
        k.pt = pb("pt", [P, 512])
        k.py = pb("py", [P, 512])

        k.m_fc = sb("m_fc", [P, 9, 512])
        k.a_ly, k.a_lx, k.a_tx, k.a_ty = (k.m_fc[:, 2 * i:2 * i + 2, :].rearrange("p a n -> p (a n)")
                                          for i in range(4))
        k.a_tx = k.a_tx.rearrange("p (a n) -> p a n", a=2)
        k.a_ty = k.a_ty.rearrange("p (h n) -> p h n", h=PAIRS)
        k.a_lo = sb("a_lo", [P, PAIRS])
        k.a_to0 = sb("a_to0", [P, PAIRS])
        k.a_to1 = sb("a_to1", [1, P])
        k.a_mask = sb("a_mask", [P, SEQ])

        k.b_wqkv = sb("b_wqkv", [P, 3072])
        k.b_wo = sb("b_wo", [P, PAIRS, P])
        k.b_scales = sb("b_scales", [P, 4 * HD])
        k.rope = sb("rope", [P, 4 * HD])
        k.rot = sb("rot", [P, 4, HD])
        k.band = sb("band", [P, SEQ])
        k.ytile = sb("ytile", [P, 2, P])
        k.sT = sb("sT", [P, 2, P])
        k.straight = sb("straight", [P, 2, HEADS, HD])
        k.turned = sb("turned", [P, 2, HEADS, HD])
        k.straights = [k.straight, sb("straight_odd", [P, 2, HEADS, HD])]
        k.sq = sb("sq", [P, 2, HEADS, HD])
        k.norm2 = sb("norm2", [P, 2, HEADS])
        k.newton = sb("newton", [P, 2, HEADS])
        k.rnorms = sb("rnorms", [P, 2, 2, HEADS])
        k.c_w1 = sb("c_w1", [P, 2 * HID])
        k.c_w2 = sb("c_w2", [P, 3, P])
        k.c_cols = sb("c_cols", [P, 8])
        k.c_b2 = sb("c_b2", [1, P])
        k.xs = sb("xs", [P, 2, 4, P])
        k.xnT = sb("xnT", [P, 2, 512])
        k.gate = sb("gate", [P, 3, 512])
        k.hid = sb("hid", [P, 3, 512])
        k.stats4 = sb("stats4", [P, TILES, 6])
        k.mv4 = sb("mv4", [P, TILES, 2])
        k.rstd4 = sb("rstd4", [P, TILES])

        k.s_w = sb("s_w", [P, 3, 4, P])
        k.s_cols = sb("s_cols", [P, 3, 3])
        k.s_bo = sb("s_bo", [1, 3, P])
        k.member = sb("member", [P, 8])
        k.s_qT = sb("s_qT", [P, 2, P])
        k.s_v = sb("s_v", [P, 2, 2, PAIRS, 2, 8])
        k.s_rows = sb("s_rows", [P, P])
        k.s_oT = sb("s_oT", [P, P])
        k.wmax = sb("wmax", [P, 4])
        k.wmaxT = sb("wmaxT", [4, 1])
        k.wdiag = sb("wdiag", [4, 4])
        k.ones4 = sb("ones4", [4, P])
        k.wstep = sb("wstep", [P, 4])
        k.wrstep = sb("wrstep", [P, 4])

        k.band16 = sb("band16", [P, SEQ], BF16)
        k.ident16 = sb("ident16", [P, P], BF16)
        k.f_bytes = sb("f_bytes", [P, P], mybir.dt.uint8)
        k.f_w = sb("f_w", [P, P], BF16)
        k.f_ws = sb("f_ws", [P, 1])
        k.f_bias = sb("f_bias", [P, P])
        k.f_scale = sb("f_scale", [P, TILES])
        k.f_rscale = sb("f_rscale", [P, TILES])
        k.m_proj = sb("m_proj", [P, 9, 4, P])
        k.m_bfc = sb("m_bfc", [P, 9, 4])
        k.m_brow = sb("m_brow", [9, P])
        k.m_wr = sb("m_wr", [P, 8])
        k.m_wp = sb("m_wp", [P, P])
        k.m_sim = sb("m_sim", [8, P])
        k.m_simsq = sb("m_simsq", [8, P])
        k.m_simn = sb("m_simn", [8, 1])
        k.m_temp = sb("m_temp", [P, 1])
        k.m_rtemp = sb("m_rtemp", [P, 1])
        k.m_tri = sb("m_tri", [P, SEQ])
        k.m_norm2 = sb("m_norm2", [P, TILES])
        k.m_logit = sb("m_logit", [P, TILES, 8])
        k.m_exp = sb("m_exp", [P, TILES, 8])
        k.m_rank = sb("m_rank", [P, TILES, 8])
        k.m_top = sb("m_top", [P, TILES])
        k.m_gate = sb("m_gate", [P, TILES, 9])
        wide = (lambda b: b[:, :, :, :].rearrange("p a h n -> p (a h n)"))
        k.s_k8 = wide(k.straight).rearrange("p (s j n) -> p s j n", s=2, j=8)
        k.m_scaled = wide(k.xs).rearrange("p (s j n) -> p s j n", s=2, j=4)
        k.f_int, k.f_mag = (wide(k.sq)[:, i * P:(i + 1) * P].bitcast(mybir.dt.int32) for i in range(2))
        k.f_val, k.f_low = (wide(k.sq)[:, i * P:(i + 1) * P] for i in range(2, 4))
        k.f_q, k.f_qT = (k.prob[:, i, :, :].rearrange("p h n -> p (h n)").bitcast(BF16)
                         .rearrange("p (t n) -> p t n", n=P) for i in range(2))
        k.m_xT = k.qT[:, :, :, :].rearrange("p a h n -> p (a h n)").rearrange("p (q n) -> p q n", q=4)
        k.m_projT = k.kT[:, :, :, :].rearrange("p a h n -> p (a h n)")
        k.m_sq = k.logit[:, :, :, :].rearrange("p a h n -> p (a h n)")
        k.m_greater = k.sq[:, 0, :, :].rearrange("p h n -> p (h n)").rearrange("p (t m) -> p t m", t=TILES)
        k.m_equal = k.sq[:, 1, :, :].rearrange("p h n -> p (h n)").rearrange("p (t m) -> p t m", t=TILES)
        k.m_gateT = k.v2[0:9, :, :, :].rearrange("p a b n -> p (a b n)")
        k.m_hid = [b[:, :, :, :].rearrange("p a h n -> p (a h n)").rearrange("p (c n) -> p c n", c=4)
                   for b in (k.straight, k.turned)]

        k.loaded = sem("loaded")
        k.stored = sem("stored")
        k.consts = sem("consts")
        k.powers = sem("powers")
        k.band_ready = sem("band_ready")
        k.xT_psum = sem("xT_psum", PHANTOM)
        k.xT_ready = sem("xT_ready", PHANTOM)
        k.q_psum = sem("q_psum", PHANTOM)
        k.k_psum = sem("k_psum", PHANTOM)
        k.v_psum = sem("v_psum", PHANTOM)
        k.qT_ready = sem("qT_ready", PHANTOM)
        k.kT_ready = sem("kT_ready", PHANTOM)
        k.v_ready = sem("v_ready", PHANTOM)
        k.s_psum = sem("s_psum", PHANTOM)
        k.masked = sem("masked", PHANTOM)
        k.top_ready = sem("top_ready", PHANTOM)
        k.shifted = sem("shifted", PHANTOM)
        k.exp_ready = sem("exp_ready", PHANTOM)
        k.den_ready = sem("den_ready", PHANTOM)
        k.rden_ready = sem("rden_ready", PHANTOM)
        k.prob_ready = sem("prob_ready", PHANTOM)
        k.pT_psum = sem("pT_psum", PHANTOM)
        k.pT_ready = sem("pT_ready", PHANTOM)
        k.o_psum = sem("o_psum", PHANTOM)
        k.oT_ready = sem("oT_ready", PHANTOM)
        k.y_psum = sem("y_psum", PHANTOM)
        k.updated = sem("updated", PHANTOM)
        k.ctx_loaded = [sem("ctx_even"), sem("ctx_odd")]

        k.norm = Names()
        k.norm.stat = sem("norm_stat", PHANTOM)
        k.norm.mv = sem("norm_mv", PHANTOM)
        k.norm.eps = sem("norm_eps", PHANTOM)
        k.norm.rstd = sem("norm_rstd", PHANTOM)
        k.norm.normed = sem("norm_normed", PHANTOM)
        k.all_stat = sem("all_stat")
        k.all_mv = sem("all_mv")
        k.all_eps = sem("all_eps")
        k.all_rstd = sem("all_rstd")
        k.all_normed = sem("all_normed")
        B = PHANTOM + TILES
        k.b_loaded = sem("b_loaded")
        k.rot_ready = sem("rot_ready")
        k.y_copied = sem("y_copied", B)
        k.half_shifted = sem("half_shifted", B)
        k.q_squared = sem("q_squared", B)
        k.k_squared = sem("k_squared", B)
        k.q_turned = sem("q_turned", B)
        k.k_turned = sem("k_turned", B)
        k.q_norm2 = sem("q_norm2", B)
        k.k_norm2 = sem("k_norm2", B)
        k.newton_step = sem("newton_step", NEWTON * B)
        k.q_added = sem("q_added", B)
        k.k_added = sem("k_added", B)
        k.q_final = sem("q_final", B)
        k.k_final = sem("k_final", B)
        k.qT_psum = sem("qT_psum", B)
        k.kT_psum = sem("kT_psum", B)
        k.c_loaded = sem("c_loaded")
        k.sh_psum = sem("sh_psum", PHANTOM)
        k.xs_low = sem("xs_low", PHANTOM)
        k.xs_high = sem("xs_high", PHANTOM)
        k.quad_stat = sem("quad_stat", PHANTOM)
        k.quad_mv = sem("quad_mv", PHANTOM)
        k.quad_eps = sem("quad_eps", PHANTOM)
        k.quad_rstd = sem("quad_rstd", PHANTOM)
        k.quad_normed = sem("quad_normed", PHANTOM)
        k.quad_turned = sem("quad_turned", PHANTOM)
        k.xnT_ready = sem("xnT_ready", PHANTOM)
        k.hid_psum = sem("hid_psum", 3 * PHANTOM)
        k.gated = sem("gated", 3 * PHANTOM)
        k.hid_ready = sem("hid_ready", 3 * PHANTOM)
        k.out_psum = sem("out_psum", PHANTOM)
        k.y_done = sem("y_done", PHANTOM)
        k.d = Names()
        k.d.xT_psum = sem("small_xT_psum", PHANTOM)
        k.d.xT_ready = sem("small_xT_ready", PHANTOM)
        k.d.q_psum = sem("small_q_psum", PHANTOM)
        k.d.k_psum = sem("small_k_psum", PHANTOM)
        k.d.v_psum = sem("small_v_psum", PHANTOM)
        k.d.q_ready = sem("small_q_ready", PHANTOM)
        k.d.k8_ready = sem("small_k8_ready", PHANTOM)
        k.d.v_ready = sem("small_v_ready", PHANTOM)
        k.d.s_psum = sem("small_s_psum", PHANTOM)
        k.d.top = sem("small_top", PHANTOM)
        k.d.shifted = sem("small_shifted", PHANTOM)
        k.d.exp = sem("small_exp", PHANTOM)
        k.d.den = sem("small_den", PHANTOM)
        k.d.rden = sem("small_rden", PHANTOM)
        k.d.pT_psum = sem("small_pT_psum", PHANTOM)
        k.d.pT_ready = sem("small_pT_ready", PHANTOM)
        k.d.o_psum = sem("small_o_psum", PHANTOM)
        k.d.rows = sem("small_rows", PHANTOM)
        k.d.o_turned = sem("small_o_turned", PHANTOM)
        k.d.oT_ready = sem("small_oT_ready", PHANTOM)
        k.d.y_psum = sem("small_y_psum", PHANTOM)
        k.d.updated = sem("small_updated", PHANTOM)
        k.quant = Names()
        k.quant.wmax = sem("quant_wmax")
        k.quant.turned = sem("quant_turned")
        k.quant.diag = sem("quant_diag")
        k.quant.spread = sem("quant_spread")
        k.quant.done = sem("quant_done")
        k.f = Names()
        k.f.weight = sem("fp8_weight")
        k.f.quantised = sem("fp8_quantised")
        k.f.turned = sem("fp8_turned")
        k.f.qT = sem("fp8_qT")
        k.f.product = sem("fp8_product")
        k.f.done = sem("fp8_done")
        k.e = []
        for n in (2, 3):
            e = Names()
            e.loaded = sem(f"experts{n}_loaded")
            e.xnT = sem(f"experts{n}_xnT")
            e.turned = sem(f"experts{n}_turned")
            e.logits = sem(f"experts{n}_logits")
            e.below = sem(f"experts{n}_below")
            e.exp = sem(f"experts{n}_exp")
            e.gates = sem(f"experts{n}_gates")
            e.gate_turned = sem(f"experts{n}_gate_turned")
            e.gateT = sem(f"experts{n}_gateT")
            e.bias_psum = sem(f"experts{n}_bias_psum")
            e.done = sem(f"experts{n}_done")
            e.first = PHANTOM if n == 2 else PHANTOM + 9 * QUADS
            k.e.append(e)
        e.projT = sem("experts3_projT")
        e.squares = sem("experts3_squares")
        e.sim_norm2 = sem("experts3_sim_norm2")
        e.sim_floor = sem("experts3_sim_floor")
        e.sim_rnorm = sem("experts3_sim_rnorm")
        e.sim_scaled = sem("experts3_sim_scaled")
        e.sim_turned = sem("experts3_sim_turned")
        e.sim_T = sem("experts3_sim_T")
        e.norm2 = sem("experts3_norm2")
        e.floor = sem("experts3_floor")
        e.rnorm = sem("experts3_rnorm")
        e.cooled = sem("experts3_cooled")
        e.raw = sem("experts3_raw")
        hid_psum, hid_ready = (sem(name, 4 * PHANTOM) for name in ("experts_hid_psum", "experts_hid_ready"))
        out_psum, scaled, added = (sem("experts_" + name, PHANTOM) for name in ("out_psum", "scaled", "added"))
        for e in k.e:
            e.hid_psum, e.hid_ready, e.out_psum, e.scaled, e.added = hid_psum, hid_ready, out_psum, scaled, added
        k.vector_link, k.links = sem("vector_link"), 0
        k.x_done = sem("x_done")

        block = ctx.enter_context(nc.Block())

        @block.sync
        def _(sp):
            sync_program(nc, sp, k, a, out)

        @block.tensor
        def _(pe):
            tensor_program(nc, pe, k)

        @block.scalar
        def _(act):
            scalar_program(nc, act, k)

        @block.vector
        def _(dve):
            vector_program(nc, dve, k)

        @block.gpsimd
        def _(pool):
            for s, first in primed:
                pool.sem_inc(s, first)
            gpsimd_program(nc, pool, k)


def steps(eng, first, step):
    with eng.Fori(1, TILES - 2, 2) as t:
        step(first + t, 1, t)
        step(first + t + 1, 0, t + 1)
    step(first + (TILES - 1), 1, TILES - 1)


def tile(ap, t):
    return ap[:, t, :] if isinstance(t, int) else ap[:, bass.ds(t, 1), :].rearrange("p a n -> p (a n)")



def cross0_tensor(pe, k, first):
    def front(T, s):
        pe.wait_ge(k.norm.normed, T + 1)
        pe.wait_ge(k.xT_ready, T)
        pe.transpose(k.pt[:, 0:P], k.normed[:, s, :], k.ident[:, :]).then_inc(k.xT_psum, 1)
        pe.wait_ge(k.xT_ready, T + 1)
        pe.wait_ge(k.oT_ready, T - 1)
        for h in range(PAIRS):
            mm = pe.matmul(k.w0[:, h * P:(h + 1) * P], k.a_ly[:, h * P:(h + 1) * P], k.xT[:, s, :],
                           start=True, stop=True)
        mm.then_inc(k.q_psum, 1)
        pe.wait_ge(k.ctx_loaded[s], 8 * (T - s - first) + 16)
        pe.wait_ge(k.masked, T)
        for h in range(PAIRS):
            mm = pe.matmul(k.w1[:, h * P:(h + 1) * P], k.a_lx[:, h * P:(h + 1) * P], k.ctxT[:, s, :],
                           start=True, stop=True)
        mm.then_inc(k.k_psum, 1)
        pe.wait_ge(k.pT_ready, T - 1)
        for b in range(2):
            for p in range(2):
                mm = pe.matmul(k.w2[64 * p:64 * p + 64, 512 * b:512 * b + 512],
                               k.ctxT[:, s, 64 * b:64 * b + 64], k.a_tx[:, p, :], start=True, stop=True)
        mm.then_inc(k.v_psum, 1)

    def step(T, s, t):
        front(T, s)
        attend_tail_tensor(pe, k, T - 1, 1 - s, k.a_ty, k.a_to1, k.qT_ready)
        wait_apart(pe, k, k.qT_ready, T + 1)
        pe.wait_ge(k.kT_ready, T + 1)
        scores_tensor(pe, k, s)

    front(first, 0)
    pe.wait_ge(k.qT_ready, first + 1)
    pe.wait_ge(k.kT_ready, first + 1)
    scores_tensor(pe, k, 0)
    steps(pe, first, step)
    attend_tail_tensor(pe, k, first + TILES - 1, 1, k.a_ty, k.a_to1, k.qT_ready, ahead=0)


def wait_apart(eng, k, s, value):
    if not isinstance(value, int):
        eng.to_reg(value)
    eng.wait_ge(k.consts, 5)
    eng.wait_ge(s, value)


def link(dve, k, instruction):
    k.links += 1
    instruction.then_inc(k.vector_link, 1)
    dve.wait_ge(k.vector_link, k.links)


def scores_tensor(pe, k, s):
    for h in range(PAIRS):
        for p in range(2):
            for b in range(2):
                r = slice(64 * p, 64 * p + 64)
                c = slice(64 * b, 64 * b + 64)
                mm = pe.matmul(k.w1[c, 512 * p + 64 * h:512 * p + 64 * h + 64], k.qT[r, s, h, c],
                               k.kT[r, s, h, c], start=True, stop=True)
    mm.then_inc(k.s_psum, 1)


def attend_tail_tensor(pe, k, T, s, w_out, b_out, w0_free, ahead=1):
    pe.wait_ge(k.prob_ready, T + 1)
    pe.wait_ge(k.v_ready, T + 1 + ahead)
    for h in range(PAIRS):
        mm = pe.transpose(k.w2[:, h * P:(h + 1) * P], k.prob[:, s, 2 * h:2 * h + 2, :].rearrange("p a m -> p (a m)"), k.ident[:, :])
    mm.then_inc(k.pT_psum, 1)
    wait_apart(pe, k, k.pT_ready, T + 1)
    pe.wait_ge(w0_free, T + 1 + ahead)
    for n in range(PAIRS):
        for p in range(2):
            h = (n + 4 * p) % PAIRS
            for b in range(2):
                r = slice(64 * p, 64 * p + 64)
                mm = pe.matmul(k.w0[r, h * P + 64 * b:h * P + 64 * b + 64], k.v2[r, s, b, 64 * h:64 * h + 64],
                               k.probT[r, h, 64 * b:64 * b + 64], start=True, stop=True)
    mm.then_inc(k.o_psum, 1)
    pe.wait_ge(k.oT_ready, T + 1)
    pe.wait_ge(k.updated, T)
    for h in range(PAIRS):
        mm = pe.matmul(k.py[:, 0:P], k.oT[:, h, :], w_out[:, h, :],
                       start=(h == 0), stop=(b_out is None and h == PAIRS - 1))
    if b_out is not None:
        mm = pe.matmul(k.py[:, 0:P], k.ones[0:1, :], b_out[0:1, :], start=False, stop=True)
    mm.then_inc(k.y_psum, 1)


def cross0_scalar(act, k, first):
    def front(T, s):
        act.wait_ge(k.xT_psum, T + 1)
        act.copy(k.xT[:, s, :], k.pt[:, 0:P]).then_inc(k.xT_ready, 1)

    def fill(T, s):
        act.wait_ge(k.k_psum, T + 1)
        act.copy(k.kT[:, s, :, :], k.w1[:, :]).then_inc(k.kT_ready, 1)
        act.wait_ge(k.v_psum, T + 1)
        act.copy(k.v2[:, s, :, :], k.w2[:, :]).then_inc(k.v_ready, 1)

    def step(T, s, t):
        front(T, s)
        exp_scalar(act, k, T - 1, 1 - s, 0.125)
        fill(T, s)
        probT_scalar(act, k, T - 1)

    front(first, 0)
    fill(first, 0)
    steps(act, first, step)
    exp_scalar(act, k, first + TILES - 1, 1, 0.125)
    probT_scalar(act, k, first + TILES - 1)


def exp_scalar(act, k, T, s, scale):
    act.wait_ge(k.shifted, T + 1)
    act.activation(k.prob[:, s, :, :], k.logit[:, s, :, :], ACT.Exp, scale=scale).then_inc(k.exp_ready, 1)


def probT_scalar(act, k, T):
    act.wait_ge(k.pT_psum, T + 1)
    act.wait_ge(k.o_psum, T)
    act.copy(k.probT[:, :, :], k.w2[:, :]).then_inc(k.pT_ready, 1)


def softmax_shift_vector(dve, k, T, s, mask):
    dve.wait_ge(k.s_psum, T + 1)
    flat = k.logit[:, s, :, :]
    dve.tensor_tensor(flat.rearrange("p (h a) m -> p a h m", a=2),
                      k.w1[:, :].rearrange("p (a h m) -> p a h m", a=2, m=SEQ),
                      mask[:, None, None, :].broadcast_to([P, 2, PAIRS, SEQ]), ALU.add).then_inc(k.masked, 1)
    dve.wait_ge(k.masked, T + 1)
    dve.tensor_reduce(k.top[:, s, :], flat, AX.X, ALU.max).then_inc(k.top_ready, 1)
    dve.wait_ge(k.top_ready, T + 1)
    dve.tensor_tensor(flat, flat, k.top[:, s, :, None].broadcast_to([P, HEADS, SEQ]),
                      ALU.subtract).then_inc(k.shifted, 1)


def softmax_sum_vector(dve, k, T, s):
    dve.wait_ge(k.exp_ready, T + 1)
    dve.tensor_reduce(k.den[:, s, :], k.prob[:, s, :, :], AX.X,
                      ALU.add).then_inc(k.den_ready, 1)
    dve.wait_ge(k.den_ready, T + 1)
    dve.reciprocal(k.rden[:, s, :], k.den[:, s, :]).then_inc(k.rden_ready, 1)


def softmax_scale_gpsimd(pool, k, T, s):
    pool.wait_ge(k.rden_ready, T + 1)
    flat = k.prob[:, s, :, :]
    pool.tensor_tensor(flat, flat, k.rden[:, s, :, None].broadcast_to([P, HEADS, SEQ]),
                       ALU.mult).then_inc(k.prob_ready, 1)


def stats_vector(dve, k, n, T, s, rows):
    dve.bn_stats(k.stats[:, s, :], rows).then_inc(n.stat, 1)
    wait_apart(dve, k, n.stat, T + 1)
    dve.bn_aggr(k.mv[:, s, :], k.stats[:, s, :]).then_inc(n.mv, 1)


def normalise_vector(dve, k, n, T, s, rows, to):
    dve.wait_ge(n.rstd, T + 1)
    return dve.tensor_scalar(to, rows, k.mv[:, s, 0:1], k.rstd[:, s, :], ALU.subtract, ALU.mult)


def rstd_gpsimd(pool, k, n, T, s):
    pool.wait_ge(n.mv, T + 1)
    pool.tensor_tensor(k.rstd[:, s, :], k.mv[:, s, 1:2], k.eps[:, 0:1], ALU.add).then_inc(n.eps, 1)
    pool.wait_ge(n.eps, T + 1)
    pool.tensor_tensor(k.rstd[:, s, :], k.rstd[:, s, :], k.power[:, 0:1], ALU.pow).then_inc(n.rstd, 1)


def cross0_vector(dve, k, first):
    def norm(T, s, t):
        rows = tile(k.x, t)
        stats_vector(dve, k, k.norm, T, s, rows)
        dve.wait_ge(k.xT_psum, T - 1)
        normalise_vector(dve, k, k.norm, T, s, rows, k.normed[:, s, :]).then_inc(k.norm.normed, 1)

    def q_bias(T, s):
        dve.wait_ge(k.q_psum, T + 1)
        dve.tensor_tensor(k.qT[:, s, :, :], k.w0[:, :].rearrange("p (h n) -> p h n", n=P),
                          k.a_lo[:, :, None].broadcast_to([P, PAIRS, P]), ALU.add).then_inc(k.qT_ready, 1)

    def tail(T, t):
        dve.wait_ge(k.o_psum, T + 1)
        dve.wait_ge(k.y_psum, T)
        dve.tensor_tensor(k.oT[:, :, :], k.w0[:, :].rearrange("p (h n) -> p h n", n=P),
                          k.a_to0[:, :, None].broadcast_to([P, PAIRS, P]), ALU.add).then_inc(k.oT_ready, 1)
        dve.wait_ge(k.y_psum, T + 1)
        dve.tensor_tensor(tile(k.x, t), tile(k.x, t), k.py[:, 0:P], ALU.add).then_inc(k.updated, 1)

    def step(T, s, t):
        norm(T, s, t)
        softmax_shift_vector(dve, k, T - 1, 1 - s, k.a_mask)
        q_bias(T, s)
        softmax_sum_vector(dve, k, T - 1, 1 - s)
        tail(T - 1, t - 1)

    norm(first, 0, 0)
    q_bias(first, 0)
    steps(dve, first, step)
    last = first + TILES - 1
    softmax_shift_vector(dve, k, last, 1, k.a_mask)
    softmax_sum_vector(dve, k, last, 1)
    tail(last, TILES - 1)


def cross0_gpsimd(pool, k, first):
    def step(T, s, t):
        rstd_gpsimd(pool, k, k.norm, T, s)
        softmax_scale_gpsimd(pool, k, T - 1, 1 - s)

    rstd_gpsimd(pool, k, k.norm, first, 0)
    steps(pool, first, step)
    softmax_scale_gpsimd(pool, k, first + TILES - 1, 1)



def fresh_vector(dve, k, n):
    with dve.Fori(0, TILES) as t:
        dve.bn_stats(tile(k.stats4, t), tile(k.x, t)).then_inc(k.all_stat, 1)
    dve.wait_ge(k.all_stat, n * TILES)
    for t in range(TILES):
        agg = dve.bn_aggr(k.mv4[:, t, :], k.stats4[:, t, :])
    agg.then_inc(k.all_mv, 1)
    dve.wait_ge(k.all_rstd, n)
    for t in range(TILES):
        last = dve.tensor_scalar(k.y[:, t, :], k.x[:, t, :], k.mv4[:, t, 0:1], k.rstd4[:, t:t + 1],
                                 ALU.subtract, ALU.mult)
    last.then_inc(k.all_normed, 1)


def fresh_gpsimd(pool, k, n):
    pool.wait_ge(k.all_mv, n)
    pool.tensor_tensor(k.rstd4[:, :], k.mv4[:, :, 1], k.eps[:, 0:1].broadcast_to([P, TILES]),
                       ALU.add).then_inc(k.all_eps, 1)
    pool.wait_ge(k.all_eps, n)
    pool.tensor_tensor(k.rstd4[:, :], k.rstd4[:, :], k.power[:, 0:1].broadcast_to([P, TILES]),
                       ALU.pow).then_inc(k.all_rstd, 1)




BEHIND = 3


def local_steps(eng, first, step):
    def single(i):
        step(first + i, i % 2, i, [0 <= i + n < TILES for n in (2, 1, 0, -1, -2, -3)])

    every = [True] * 6
    for i in range(3):
        single(i)
    with eng.Fori(3, TILES - 4, 2) as t:
        step(first + t, 1, t, every)
        step(first + t + 1, 0, t + 1, every)
    for i in range(TILES - 3, TILES + BEHIND):
        single(i)


def local_tensor(pe, k, first):
    def step(T, s, t, has):
        _, after, this, before, before2, before3 = has
        if this:
            pe.wait_ge(k.half_shifted, T + 1)
            if before2:
                pe.wait_ge(k.qT_ready, T - 1)
            elif before:
                pe.wait_ge(k.q_turned, T)
            for c in range(2):
                mm = pe.matmul(k.w0[:, 512 * c:512 * c + 512], k.sT[:, s, :], k.b_wqkv[:, 512 * c:512 * c + 512],
                               start=True, stop=True)
            mm.then_inc(k.q_psum, 1)
        if before3:
            pe.wait_ge(k.oT_ready, T - 2)
            pe.wait_ge(k.updated, T - 3)
            for h in range(PAIRS):
                mm = pe.matmul(k.py[:, 0:P], k.oT[:, h, :], k.b_wo[:, h, :], start=(h == 0), stop=(h == PAIRS - 1))
            mm.then_inc(k.y_psum, 1)
        if this:
            if before2:
                pe.wait_ge(k.shifted, T - 1)
            elif before:
                pe.wait_ge(k.k_turned, T)
            for c in range(2):
                mm = pe.matmul(k.w1[:, 512 * c:512 * c + 512], k.sT[:, s, :],
                               k.b_wqkv[:, 1024 + 512 * c:1536 + 512 * c], start=True, stop=True)
            mm.then_inc(k.k_psum, 1)
        if before:
            if before2 and not before3:
                wait_apart(pe, k, k.v_ready, T - 1)
            for b in range(2):
                for p in range(2):
                    mm = pe.matmul(k.w2[64 * p:64 * p + 64, 512 * b:512 * b + 512],
                                   k.sT[:, 1 - s, 64 * b:64 * b + 64], k.b_wqkv[:, 2048 + 512 * p:2560 + 512 * p],
                                   start=True, stop=True)
            mm.then_inc(k.v_psum, 1)
        if after:
            turn_y(T + 1, 1 - s)
        if before:
            if this:
                pe.wait_ge(k.q_turned, T + 1)
            else:
                pe.wait_ge(k.qT_ready, T - 1)
            pe.wait_ge(k.q_final, T)
            for h in range(PAIRS):
                mm = pe.transpose(k.w0[:, h * P:(h + 1) * P],
                                  k.straights[1 - s][:, 0, 2 * h:2 * h + 2, :].rearrange("p a d -> p (a d)"), k.ident[:, :])
            mm.then_inc(k.qT_psum, 1)
        if before2:
            if before:
                pe.wait_ge(k.v_ready, T)
            pe.wait_ge(k.prob_ready, T - 1)
            for h in range(PAIRS):
                mm = pe.transpose(k.w2[:, h * P:(h + 1) * P],
                                  k.prob[:, s, 2 * h:2 * h + 2, :].rearrange("p a m -> p (a m)"), k.ident[:, :])
            mm.then_inc(k.pT_psum, 1)
        if before:
            if this:
                pe.wait_ge(k.k_turned, T + 1)
            else:
                pe.wait_ge(k.shifted, T - 1)
            pe.wait_ge(k.k_final, T)
            for h in range(PAIRS):
                mm = pe.transpose(k.w1[:, h * P:(h + 1) * P],
                                  k.straights[1 - s][:, 1, 2 * h:2 * h + 2, :].rearrange("p a d -> p (a d)"), k.ident[:, :])
            mm.then_inc(k.kT_psum, 1)
        if before2:
            wait_apart(pe, k, k.pT_ready, T - 1)
            for n in range(PAIRS):
                for p in range(2):
                    h = (n + 4 * p) % PAIRS
                    for b in range(2):
                        r = slice(64 * p, 64 * p + 64)
                        mm = pe.matmul(k.w2[r, h * P + 64 * b:h * P + 64 * b + 64],
                                       k.v2[r, s, b, 64 * h:64 * h + 64], k.probT[r, h, 64 * b:64 * b + 64],
                                       start=True, stop=True)
            mm.then_inc(k.o_psum, 1)
        if before:
            wait_apart(pe, k, k.kT_ready, T)
            pe.wait_ge(k.qT_ready, T)
            for p in range(2):
                r = slice(64 * p, 64 * p + 64)
                for b in range(2):
                    pe.matmul(k.w1[64 * b:64 * b + 64, 512 * p:512 * p + 512], k.ident16[r, r],
                              k.band16[r, None, :].broadcast_to([SEQ, PAIRS, SEQ]), start=True, stop=False,
                              skip_group_check=True)
            for h in range(PAIRS):
                for p in range(2):
                    for b in range(2):
                        r = slice(64 * p, 64 * p + 64)
                        c = slice(64 * b, 64 * b + 64)
                        mm = pe.matmul(k.w1[c, 512 * p + 64 * h:512 * p + 64 * h + 64], k.qT[r, 1 - s, h, c],
                                       k.kT[r, 1 - s, h, c], start=False, stop=True, skip_group_check=True)
            mm.then_inc(k.s_psum, 1)

    def turn_y(T, s):
        pe.wait_ge(k.y_copied, T + 1)
        pe.wait_ge(k.half_shifted, T)
        pe.transpose(k.pt[:, 0:P], k.ytile[:, s, :], k.ident[:, :]).then_inc(k.xT_psum, 1)

    pe.wait_ge(k.band_ready, 1)
    pe.wait_ge(k.b_loaded, B_LOADS * (first - PHANTOM))
    turn_y(first, 0)
    local_steps(pe, first, step)


def local_scalar(act, k, first, qfirst):
    def copy_y(T, s, t):
        act.copy(k.ytile[:, s, :], tile(k.y, t)).then_inc(k.y_copied, 1)

    def shift(T, s):
        act.wait_ge(k.xT_psum, T + 1)
        act.copy(k.sT[0:64, s, :], k.pt[0:64, 0:P])
        act.copy(k.sT[64:P, s, :].rearrange("p (b n) -> p b n", b=2)[:, :, 1:SEQ],
                 k.pt[64:P, 0:P].rearrange("p (b n) -> p b n", b=2)[:, :, 0:SEQ - 1]).then_inc(k.half_shifted, 1)

    def step(T, s, t, has):
        after2, after, this, before, before2, _ = has
        if this:
            act.wait_ge(k.q_psum, T + 1)
            act.wait_ge(k.q_norm2, T)
            act.activation(k.sq[:, 0, :, :], k.w0[:, :], ACT.Square).then_inc(k.q_squared, 1)
        if before2:
            exp_scalar(act, k, T - 2, s, 8.0)
        if this:
            act.wait_ge(k.k_psum, T + 1)
            act.wait_ge(k.k_norm2, T)
            act.activation(k.sq[:, 1, :, :], k.w1[:, :], ACT.Square).then_inc(k.k_squared, 1)
        if before:
            act.wait_ge(k.v_psum, T)
            act.copy(k.v2[:, 1 - s, :, :], k.w2[:, :]).then_inc(k.v_ready, 1)
        if after:
            shift(T + 1, 1 - s)
        if after2:
            copy_y(T + 2, s, t + 2)
        if before:
            act.wait_ge(k.qT_psum, T)
            act.copy(k.qT[:, 1 - s, :, :], k.w0[:, :]).then_inc(k.qT_ready, 1)
        if before2:
            act.wait_ge(k.pT_psum, T - 1)
            act.copy(k.probT[:, :, :], k.w2[:, :]).then_inc(k.pT_ready, 1)
        if before:
            act.wait_ge(k.kT_psum, T)
            act.copy(k.kT[:, 1 - s, :, :], k.w1[:, :]).then_inc(k.kT_ready, 1)
        if before2:
            act.wait_ge(k.o_psum, T - 1)
            act.copy(k.oT[:, :, :], k.w2[:, :]).then_inc(k.oT_ready, 1)

    act.wait_ge(k.all_normed, 1)
    act.wait_ge(k.y_done, qfirst)
    copy_y(first, 0, 0)
    copy_y(first + 1, 1, 1)
    shift(first, 0)
    local_steps(act, first, step)


NEWTON = 11


def local_vector(dve, k, first):
    def rotate(T, s, i, w, turned, squared, transposed, added):
        dve.wait_ge(squared, T + 1)
        dve.wait_ge(transposed, T - 1)
        heads = w[:, :].rearrange("p (h d) -> p h d", d=HD)
        dve.tensor_tensor(k.straights[s][:, i, :, :], heads,
                          k.rot[:, 2 * i, None, :].broadcast_to([P, HEADS, HD]), ALU.mult)
        dve.wait_ge(added, T)
        half = HD // 2
        for to, of in ((slice(0, half), slice(half, HD)), (slice(half, HD), slice(0, half))):
            last = dve.tensor_tensor(k.turned[:, i, :, to], heads[:, :, of],
                                     k.rot[:, 2 * i + 1, None, to].broadcast_to([P, HEADS, half]), ALU.mult)
        last.then_inc(turned, 1)

    def reciprocal_norms(T, s):
        m, u = k.norm2[:, :, :], k.newton[:, :, :]
        r = k.rnorms[:, s, :, :]
        dve.wait_ge(k.q_norm2, T + 1)
        dve.wait_ge(k.k_norm2, T + 1)
        dve.tensor_scalar(m, m, 1e-24, None, ALU.max).then_inc(k.newton_step, 1)
        done = T * NEWTON + 1
        dve.wait_ge(k.newton_step, done)
        dve.tensor_scalar(r.bitcast(I32), m.bitcast(I32), -0.5, float(0x5f3759df), ALU.mult,
                          ALU.add).then_inc(k.newton_step, 1)
        for n in range(3):
            dve.wait_ge(k.newton_step, T * NEWTON + (2 + 3 * n))
            dve.tensor_tensor(u, r, r, ALU.mult).then_inc(k.newton_step, 1)
            dve.wait_ge(k.newton_step, T * NEWTON + (3 + 3 * n))
            dve.scalar_tensor_tensor(out=u, in0=u, scalar=-0.5, in1=m, op0=ALU.mult,
                                     op1=ALU.mult).then_inc(k.newton_step, 1)
            dve.wait_ge(k.newton_step, T * NEWTON + (4 + 3 * n))
            dve.scalar_tensor_tensor(out=r, in0=u, scalar=1.5, in1=r, op0=ALU.add,
                                     op1=ALU.mult).then_inc(k.newton_step, 1)

    def step(T, s, t, has):
        _, _, this, _, before2, before3 = has
        if before2:
            scores = k.w1[:, :].rearrange("p (a h m) -> p h a m", a=2, m=SEQ)
            by_pair = (lambda ap: ap.rearrange("p (h a) -> p h a", a=2))
            dve.wait_ge(k.s_psum, T - 1)
            dve.tensor_reduce(by_pair(k.top[:, s, :]), scores, AX.X, ALU.max).then_inc(k.top_ready, 1)
            dve.wait_ge(k.top_ready, T - 1)
            dve.tensor_tensor(k.logit[:, s, :, :].rearrange("p (h a) m -> p h a m", a=2), scores,
                              by_pair(k.top[:, s, :])[:, :, :, None].broadcast_to([P, PAIRS, 2, SEQ]),
                              ALU.subtract).then_inc(k.shifted, 1)
        if this:
            rotate(T, s, 0, k.w0, k.q_turned, k.q_squared, k.qT_psum, k.q_added)
        if before2:
            softmax_sum_vector(dve, k, T - 2, s)
        if this:
            rotate(T, s, 1, k.w1, k.k_turned, k.k_squared, k.kT_psum, k.k_added)
        if before3:
            dve.wait_ge(k.y_psum, T - 2)
            dve.tensor_tensor(tile(k.y, t - 3), tile(k.y, t - 3), k.py[:, 0:P], ALU.add).then_inc(k.updated, 1)
        if this:
            for i, norm2 in enumerate((k.q_norm2, k.k_norm2)):
                dve.tensor_reduce(k.norm2[:, i, :], k.sq[:, i, :, :], AX.X, ALU.add).then_inc(norm2, 1)
            reciprocal_norms(T, s)

    dve.wait_ge(k.b_loaded, B_LOADS * (first - PHANTOM))
    dve.tensor_tensor(k.rot[:, :, :].rearrange("p a d -> p (a d)"), k.rope[:, :], k.b_scales[:, :],
                      ALU.mult).then_inc(k.rot_ready, 1)
    dve.wait_ge(k.rot_ready, (first - PHANTOM) // TILES)
    local_steps(dve, first, step)


def local_gpsimd(pool, k, first):
    def norm(T, s, i, added, final):
        pool.wait_ge(added, T + 1)
        pool.tensor_tensor(k.straights[s][:, i, :, :], k.straights[s][:, i, :, :],
                           k.rnorms[:, s, i, :, None].broadcast_to([P, HEADS, HD]), ALU.mult).then_inc(final, 1)

    def add(T, s, i, turned, added):
        pool.wait_ge(turned, T + 1)
        pool.tensor_tensor(k.straights[s][:, i, :, :], k.straights[s][:, i, :, :], k.turned[:, i, :, :],
                           ALU.add).then_inc(added, 1)

    def step(T, s, t, has):
        _, _, this, before, before2, _ = has
        if before:
            pool.wait_ge(k.newton_step, T * NEWTON)
            norm(T - 1, 1 - s, 0, k.q_added, k.q_final)
            norm(T - 1, 1 - s, 1, k.k_added, k.k_final)
        if before2:
            softmax_scale_gpsimd(pool, k, T - 2, s)
        if this:
            add(T, s, 0, k.q_turned, k.q_added)
            add(T, s, 1, k.k_turned, k.k_added)

    local_steps(pool, first, step)



QUADS = TILES // 4


def gated_tensor(pe, k, first, qfirst):
    def front(Q, q, s):
        pe.wait_ge(k.xnT_ready, Q)
        pe.matmul(k.pt[:, 0:256].rearrange("p (j d) -> p j d", j=4), k.shift[:, :], k.y[:, 4 * q:4 * q + 4, 64:P],
                  start=True, stop=True).then_inc(k.sh_psum, 1)
        pe.wait_ge(k.quad_normed, Q + 1)
        pe.wait_ge(k.xs_high, Q + 1)
        for j in range(4):
            mm = pe.transpose(k.pt[:, j * P:(j + 1) * P], k.xs[:, s, j, :], k.ident[:, :])
        mm.then_inc(k.quad_turned, 1)

    def hidden(Q, s):
        pe.wait_ge(k.xnT_ready, Q + 1)
        for c, (at, n) in enumerate(CHUNKS):
            w = (k.w0, k.w1, k.w2)[c]
            pe.wait_ge(k.hid_ready, 3 * Q + (c - 2))
            pe.matmul(w[0:n, 0:512], k.c_w1[:, HID + at:HID + at + n], k.xnT[:, s, :], start=True, stop=True)
            pe.matmul(w[0:n, 512:1024], k.c_w1[:, at:at + n], k.xnT[:, s, :],
                      start=True, stop=True).then_inc(k.hid_psum, 1)

    def output(Q):
        pe.wait_ge(k.y_done, Q)
        pe.wait_ge(k.hid_ready, 3 * Q + 3)
        for j in range(4):
            for c, (at, n) in enumerate(CHUNKS):
                pe.matmul(k.py[:, j * P:(j + 1) * P], k.hid[0:n, c, j * P:(j + 1) * P], k.c_w2[0:n, c, :],
                          start=(c == 0), stop=False)
            mm = pe.matmul(k.py[:, j * P:(j + 1) * P], k.ones[0:1, :], k.c_b2[0:1, :], start=False, stop=True)
        mm.then_inc(k.out_psum, 1)

    pe.wait_ge(k.c_loaded, C_LOADS * (first - PHANTOM))
    pe.wait_ge(k.updated, first + TILES)
    front(qfirst, 0, 0)
    for q in range(QUADS):
        if q + 1 < QUADS:
            front(qfirst + (q + 1), q + 1, (q + 1) % 2)
        hidden(qfirst + q, q % 2)
        output(qfirst + q)


def gated_scalar(act, k, first, qfirst):
    def front(Q, q, s):
        act.wait_ge(k.quad_turned, Q - 1)
        act.copy(k.xs[:, s, :, 0:64], k.y[:, 4 * q:4 * q + 4, 0:64]).then_inc(k.xs_low, 1)
        act.wait_ge(k.sh_psum, Q + 1)
        act.copy(k.xs[:, s, :, 64:P], k.pt[:, 0:256].rearrange("p (j d) -> p j d", j=4)).then_inc(k.xs_high, 1)

    def gelu(Q):
        for c, (at, n) in enumerate(CHUNKS):
            act.wait_ge(k.hid_psum, 3 * Q + (c + 1))
            act.wait_ge(k.hid_ready, 3 * Q + (c - 2))
            act.activation(k.gate[0:n, c, :], (k.w0, k.w1, k.w2)[c][0:n, 0:512], ACT.Gelu,
                           bias=k.c_cols[0:n, 5 + c:6 + c]).then_inc(k.gated, 1)

    act.wait_ge(k.updated, first + TILES)
    act.wait_ge(k.c_loaded, C_LOADS * (first - PHANTOM))
    front(qfirst, 0, 0)
    for q in range(QUADS):
        if q + 1 < QUADS:
            front(qfirst + (q + 1), q + 1, (q + 1) % 2)
        gelu(qfirst + q)


def gated_vector(dve, k, first, qfirst):
    def front(Q, q, s):
        dve.wait_ge(k.xs_low, Q + 1)
        dve.wait_ge(k.xs_high, Q + 1)
        for j in range(4):
            last = dve.bn_stats(k.stats4[:, 4 * s + j, :], k.xs[:, s, j, :])
        last.then_inc(k.quad_stat, 1)
        wait_apart(dve, k, k.quad_stat, Q + 1)
        for j in range(4):
            last = dve.bn_aggr(k.mv4[:, 4 * s + j, :], k.stats4[:, 4 * s + j, :])
        last.then_inc(k.quad_mv, 1)
        dve.wait_ge(k.quad_rstd, Q + 1)
        for j in range(4):
            last = dve.tensor_scalar(k.xs[:, s, j, :], k.xs[:, s, j, :], k.mv4[:, 4 * s + j, 0:1],
                                     k.rstd4[:, 4 * s + j:4 * s + j + 1], ALU.subtract, ALU.mult)
        last.then_inc(k.quad_normed, 1)
        dve.wait_ge(k.quad_turned, Q + 1)
        dve.tensor_scalar(k.xnT[:, s, :], k.pt[:, :], k.c_cols[:, 0:1], k.c_cols[:, 1:2],
                          ALU.mult, ALU.add).then_inc(k.xnT_ready, 1)

    def hidden(Q):
        for c, (at, n) in enumerate(CHUNKS):
            dve.wait_ge(k.gated, 3 * Q + (c + 1))
            dve.wait_ge(k.out_psum, Q)
            dve.scalar_tensor_tensor(out=k.hid[0:n, c, :], in0=(k.w0, k.w1, k.w2)[c][0:n, 512:1024],
                                     scalar=k.c_cols[0:n, 2 + c:3 + c], in1=k.gate[0:n, c, :],
                                     op0=ALU.add, op1=ALU.mult).then_inc(k.hid_ready, 1)

    def output(Q, q):
        dve.wait_ge(k.out_psum, Q + 1)
        rows = k.y[:, 4 * q:4 * q + 4, :].rearrange("p j n -> p (j n)")
        dve.tensor_tensor(rows, rows, k.py[:, :], ALU.add).then_inc(k.y_done, 1)

    dve.wait_ge(k.c_loaded, C_LOADS * (first - PHANTOM))
    front(qfirst, 0, 0)
    for q in range(QUADS):
        if q + 1 < QUADS:
            front(qfirst + (q + 1), q + 1, (q + 1) % 2)
        hidden(qfirst + q)
        output(qfirst + q, q)


def gated_gpsimd(pool, k, first, qfirst):
    for q in range(QUADS):
        Q, s = qfirst + q, q % 2
        r = k.rstd4[:, 4 * s:4 * s + 4]
        pool.wait_ge(k.quad_mv, Q + 1)
        pool.tensor_tensor(r, k.mv4[:, 4 * s:4 * s + 4, 1], k.eps[:, 0:4], ALU.add).then_inc(k.quad_eps, 1)
        pool.wait_ge(k.quad_eps, Q + 1)
        pool.tensor_tensor(r, r, k.power[:, 0:4], ALU.pow).then_inc(k.quad_rstd, 1)



def small_tensor(pe, k, n):
    d, first = k.d, PHANTOM + TILES * n

    def front(T, s):
        pe.wait_ge(k.norm.normed, T + (TILES + 1))
        pe.wait_ge(d.v_ready, T)
        pe.transpose(k.pt[:, 0:P], k.normed[:, s, :], k.ident[:, :]).then_inc(d.xT_psum, 1)
        pe.wait_ge(k.ctx_loaded[s], 8 * (T - s - first) + (16 + 128 * (n + 1)))
        pe.wait_ge(d.oT_ready, T - 1)
        pe.matmul(k.w0[:, 512:512 + P], k.s_w[:, n, 1, :], k.ctxT[:, s, :], start=True, stop=True).then_inc(d.k_psum, 1)
        pe.wait_ge(d.xT_ready, T + 1)
        pe.wait_ge(d.rows, T - 1)
        pe.matmul(k.w0[:, 0:P], k.s_w[:, n, 0, :], k.xT[:, s, :], start=True, stop=True).then_inc(d.q_psum, 1)
        for p in range(2):
            for b in range(2):
                mm = pe.matmul(k.pt[64 * p:64 * p + 64, 64 * b:64 * b + 64], k.ctxT[:, s, 64 * b:64 * b + 64],
                               k.s_w[:, n, 2, 64 * p:64 * p + 64], start=True, stop=True)
        mm.then_inc(d.v_psum, 1)

    def scores(T, s):
        wait_apart(pe, k, d.q_ready, T + 1)
        pe.wait_ge(d.k8_ready, T + 1)
        pe.wait_ge(d.shifted, T)
        for b in range(2):
            for g in range(2):
                r = slice(64 * g, 64 * g + 64)
                mm = pe.matmul(k.w1[64 * b:64 * b + 64, 512 * g:512 * g + 512], k.s_qT[r, s, 64 * b:64 * b + 64],
                               k.s_k8[r, s, :, 64 * b:64 * b + 64], start=True, stop=True)
        mm.then_inc(d.s_psum, 1)

    def tail(T, s, ahead=1):
        pe.wait_ge(d.exp, T + 1)
        pe.wait_ge(d.pT_ready, T)
        for h in range(PAIRS):
            mm = pe.transpose(k.w2[:, h * P:(h + 1) * P],
                              k.prob[:, s, 2 * h:2 * h + 2, :].rearrange("p a m -> p (a m)"), k.ident[:, :])
        mm.then_inc(d.pT_psum, 1)
        wait_apart(pe, k, d.pT_ready, T + 1)
        pe.wait_ge(d.q_ready, T + 1 + ahead)
        for b in range(2):
            for h in range(PAIRS):
                mm = pe.matmul(k.w0[64 * b:64 * b + 64, 16 * h:16 * h + 16], k.probT[:, h, 64 * b:64 * b + 64],
                               k.s_v[:, s, b, h, :, :].rearrange("p a d -> p (a d)"), start=True, stop=True)
        mm.then_inc(d.o_psum, 1)
        pe.wait_ge(d.rows, T + 1)
        pe.wait_ge(d.k8_ready, T + 1 + ahead)
        pe.transpose(k.w0[:, 512:512 + P], k.s_rows[:, :], k.ident[:, :]).then_inc(d.o_turned, 1)
        pe.wait_ge(d.oT_ready, T + 1)
        pe.wait_ge(d.updated, T)
        pe.matmul(k.py[:, 0:P], k.s_oT[:, :], k.s_w[:, n, 3, :], start=True, stop=False)
        pe.matmul(k.py[:, 0:P], k.ones[0:1, :], k.s_bo[0:1, n, :], start=False, stop=True).then_inc(d.y_psum, 1)

    def step(T, s, t):
        front(T, s)
        tail(T - 1, 1 - s)
        scores(T, s)

    front(first, 0)
    scores(first, 0)
    steps(pe, first, step)
    tail(first + TILES - 1, 1, ahead=0)


def small_scalar(act, k, n, scale):
    d, first = k.d, PHANTOM + TILES * n

    def front(T, s):
        act.wait_ge(d.xT_psum, T + 1)
        act.copy(k.xT[:, s, :], k.pt[:, 0:P]).then_inc(d.xT_ready, 1)
        act.wait_ge(d.q_psum, T + 1)
        act.activation(k.s_qT[:, s, :], k.w0[:, 0:P], ACT.Identity, bias=k.s_cols[:, n, 0:1]).then_inc(d.q_ready, 1)
        act.wait_ge(d.v_psum, T + 1)
        for p in range(2):
            last = act.copy(k.s_v[64 * p:64 * p + 64, s, :, :, p, :],
                            k.pt[64 * p:64 * p + 64, 0:P].rearrange("p (b h d) -> p b h d", b=2, d=8))
        last.then_inc(d.v_ready, 1)

    def exp(T, s):
        act.wait_ge(d.shifted, T + 1)
        act.activation(k.prob[:, s, :, :], k.logit[:, s, :, :], ACT.Exp, scale=scale).then_inc(d.exp, 1)

    def tail(T):
        act.wait_ge(d.pT_psum, T + 1)
        act.wait_ge(d.o_psum, T)
        act.copy(k.probT[:, :, :], k.w2[:, :]).then_inc(d.pT_ready, 1)
        act.wait_ge(d.o_turned, T + 1)
        act.wait_ge(d.y_psum, T)
        act.activation(k.s_oT[:, :], k.w0[:, 512:512 + P], ACT.Identity,
                       bias=k.s_cols[:, n, 2:3]).then_inc(d.oT_ready, 1)

    def step(T, s, t):
        exp(T - 1, 1 - s)
        front(T, s)
        tail(T - 1)

    front(first, 0)
    steps(act, first, step)
    last = first + TILES - 1
    exp(last, 1)
    tail(last)


def small_vector(dve, k, n):
    d, first = k.d, PHANTOM + TILES * n

    def norm(T, s, t):
        rows = tile(k.x, t)
        stats_vector(dve, k, k.norm, T + TILES, s, rows)
        dve.wait_ge(d.xT_psum, T - 1)
        normalise_vector(dve, k, k.norm, T + TILES, s, rows, k.normed[:, s, :]).then_inc(k.norm.normed, 1)

    def keys(T, s):
        dve.wait_ge(d.k_psum, T + 1)
        dve.scalar_tensor_tensor(out=k.s_k8[:, s, :, :], in0=k.w0[:, None, 512:512 + P].broadcast_to([P, 8, P]),
                                 scalar=k.s_cols[:, n, 1:2], in1=k.member[:, :, None].broadcast_to([P, 8, P]),
                                 op0=ALU.add, op1=ALU.mult).then_inc(d.k8_ready, 1)

    def softmax(T, s):
        logits = k.w1[:, :].rearrange("p (h m) -> p h m", m=SEQ)
        dve.wait_ge(d.s_psum, T + 1)
        dve.tensor_reduce(k.top[:, s, :], logits, AX.X, ALU.max).then_inc(d.top, 1)
        dve.wait_ge(d.top, T + 1)
        dve.tensor_tensor(k.logit[:, s, :, :], logits, k.top[:, s, :, None].broadcast_to([P, HEADS, SEQ]),
                          ALU.subtract).then_inc(d.shifted, 1)

    def total(T, s):
        dve.wait_ge(d.exp, T + 1)
        dve.tensor_reduce(k.den[:, s, :], k.prob[:, s, :, :], AX.X, ALU.add).then_inc(d.den, 1)
        dve.wait_ge(d.den, T + 1)
        dve.reciprocal(k.rden[:, s, :], k.den[:, s, :]).then_inc(d.rden, 1)

    def tail(T, s, t):
        dve.wait_ge(d.o_psum, T + 1)
        dve.wait_ge(d.rden, T + 1)
        dve.wait_ge(d.o_turned, T)
        dve.tensor_tensor(k.s_rows[:, :].rearrange("p (h d) -> p h d", d=8),
                          k.w0[:, 0:P].rearrange("p (h d) -> p h d", d=8),
                          k.rden[:, s, :, None].broadcast_to([P, HEADS, 8]), ALU.mult).then_inc(d.rows, 1)
        dve.wait_ge(d.y_psum, T + 1)
        dve.tensor_tensor(tile(k.x, t), tile(k.x, t), k.py[:, 0:P], ALU.add).then_inc(d.updated, 1)

    def step(T, s, t):
        softmax(T - 1, 1 - s)
        norm(T, s, t)
        keys(T, s)
        total(T - 1, 1 - s)
        tail(T - 1, 1 - s, t - 1)

    norm(first, 0, 0)
    keys(first, 0)
    steps(dve, first, step)
    last = first + TILES - 1
    softmax(last, 1)
    total(last, 1)
    tail(last, 1, TILES - 1)


def small_gpsimd(pool, k, n):
    first = PHANTOM + TILES * n

    def step(T, s, t):
        rstd_gpsimd(pool, k, k.norm, T + TILES, s)

    step(first, 0, 0)
    steps(pool, first, step)



def quantise_vector(dve, k):
    q = k.quant
    w = k.s_w[:, 2, :, :]
    dve.tensor_reduce(k.wmax[:, :], w, AX.X, ALU.max, apply_absolute_value=True).then_inc(q.wmax, 1)
    dve.wait_ge(q.turned, 1)
    link(dve, k, dve.tensor_reduce(k.wmaxT[:, :], k.pt[0:4, 0:P], AX.X, ALU.max))
    dve.tensor_scalar(k.wdiag[:, :], k.ident[0:4, 0:4], k.wmaxT[:, 0:1], None, ALU.mult).then_inc(q.diag, 1)
    dve.wait_ge(q.spread, 1)
    link(dve, k, dve.tensor_scalar(k.wstep[:, :], k.pt[:, P:P + 4], 1.0 / 127.0, None, ALU.mult))
    link(dve, k, dve.reciprocal(k.wrstep[:, :], k.wstep[:, :]))
    wide = (lambda c: c[:, :, None].broadcast_to([P, 4, P]))
    link(dve, k, dve.tensor_tensor(w, w, wide(k.wrstep), ALU.mult))
    link(dve, k, dve.tensor_scalar(w, w, 12582912.0, 12582912.0, ALU.add, ALU.subtract))
    link(dve, k, dve.tensor_scalar(w, w, -128.0, 127.0, ALU.max, ALU.min))
    dve.tensor_tensor(w, w, wide(k.wstep), ALU.mult).then_inc(q.done, 1)


def quantise_tensor(pe, k):
    pe.wait_ge(k.quant.wmax, 1)
    pe.transpose(k.pt[0:4, 0:P], k.wmax[:, :], k.ident[:, :]).then_inc(k.quant.turned, 1)
    pe.wait_ge(k.quant.diag, 1)
    pe.matmul(k.pt[:, P:P + 4], k.ones4[:, :], k.wdiag[:, :], start=True, stop=True).then_inc(k.quant.spread, 1)
    pe.wait_ge(k.quant.done, 1)



def fp8_weight_vector(dve, k):
    integer = mybir.dt.int32
    link(dve, k, dve.tensor_copy(k.f_int[:, :], k.f_bytes[:, :]))
    link(dve, k, dve.tensor_scalar(k.f_mag[:, :], k.f_int[:, :], 127, None, ALU.bitwise_and))
    link(dve, k, dve.tensor_scalar(k.f_low[:, :], k.f_mag[:, :], 2.0 ** -9, 2.0 ** -6, ALU.mult, ALU.min))
    link(dve, k, dve.tensor_scalar(k.f_val[:, :].bitcast(integer), k.f_mag[:, :], 20, None, ALU.logical_shift_left))
    link(dve, k, dve.scalar_tensor_tensor(out=k.f_val[:, :], in0=k.f_val[:, :], scalar=2.0 ** 120,
                                          in1=k.f_low[:, :], op0=ALU.mult, op1=ALU.max))
    link(dve, k, dve.tensor_scalar(k.f_low[:, :], k.f_int[:, :], 128.0, -2.0, ALU.is_ge, ALU.mult))
    dve.scalar_tensor_tensor(out=k.f_w[:, :], in0=k.f_low[:, :], scalar=1.0, in1=k.f_val[:, :],
                             op0=ALU.add, op1=ALU.mult).then_inc(k.f.weight, 1)


def fp8_vector(dve, k):
    f = k.f
    y, words = k.y[:, :, :], k.logit[:, :, :, :].rearrange("p a h n -> p (a h n)").rearrange("p (t n) -> p t n", n=P)
    wide = (lambda c: c[:, :, None].broadcast_to([P, TILES, P]))
    dve.wait_ge(k.all_normed, 2)
    link(dve, k, dve.tensor_reduce(k.f_scale[:, :], y, AX.X, ALU.max, apply_absolute_value=True))
    link(dve, k, dve.tensor_scalar(k.f_scale[:, :], k.f_scale[:, :], 1e-12, 1.0 / 448.0, ALU.max, ALU.mult))
    link(dve, k, dve.reciprocal(k.f_rscale[:, :], k.f_scale[:, :]))
    link(dve, k, dve.tensor_tensor(y, y, wide(k.f_rscale), ALU.mult))
    link(dve, k, dve.tensor_scalar(words.bitcast(mybir.dt.int32), y.bitcast(mybir.dt.int32), 0x7F800000, None,
                                   ALU.bitwise_and))
    link(dve, k, dve.tensor_scalar(words, words, 2.0 ** -6, 1.5 * 2.0 ** 20, ALU.max, ALU.mult))
    link(dve, k, dve.tensor_tensor(y, y, words, ALU.add))
    dve.tensor_tensor(k.f_q[:, :, :], y, words, ALU.subtract).then_inc(f.quantised, 1)
    link(dve, k, dve.tensor_tensor(k.x[:, :, :], k.x[:, :, :], k.f_bias[:, None, :].broadcast_to([P, TILES, P]),
                                   ALU.add))
    link(dve, k, dve.tensor_scalar(k.f_scale[:, :], k.f_scale[:, :], k.f_ws[:, 0:1], None, ALU.mult))
    for t in range(TILES):
        w = k.w1 if t < 8 else k.w2
        if t % 8 == 0:
            dve.wait_ge(f.product, t // 8 + 1)
        last = dve.scalar_tensor_tensor(out=k.x[:, t, :], in0=w[:, (t % 8) * P:(t % 8 + 1) * P],
                                        scalar=k.f_scale[:, t:t + 1], in1=k.x[:, t, :], op0=ALU.mult, op1=ALU.add)
    last.then_inc(f.done, 1)
    dve.wait_ge(f.done, 1)


def fp8_tensor(pe, k):
    f, turned = k.f, k.w0[:, :].bitcast(BF16)
    pe.wait_ge(f.quantised, 1)
    pe.wait_ge(f.weight, 1)
    for t in range(TILES):
        mm = pe.transpose(turned[:, t * P:(t + 1) * P], k.f_q[:, t, :], k.ident16[:, :])
        if t % 8 == 7:
            mm.then_inc(f.turned, 1)
    for t in range(TILES):
        if t % 8 == 0:
            pe.wait_ge(f.qT, t // 8 + 1)
        w = k.w1 if t < 8 else k.w2
        mm = pe.matmul(w[:, (t % 8) * P:(t % 8 + 1) * P], k.f_qT[:, t, :], k.f_w[:, :], start=True, stop=True)
        if t % 8 == 7:
            mm.then_inc(f.product, 1)


def fp8_scalar(act, k):
    f, turned = k.f, k.w0[:, :].bitcast(BF16)
    for c in range(2):
        act.wait_ge(f.turned, c + 1)
        act.copy(k.f_qT[:, 8 * c:8 * c + 8, :], turned[:, 1024 * c:1024 * c + 1024]).then_inc(f.qT, 1)



def experts_prelude_tensor(pe, k, e, similar):
    for q in range(QUADS):
        if q == 0:
            pe.wait_ge(k.all_normed, 4 if similar else 3)
        else:
            pe.wait_ge(e.xnT, q)
        for j in range(4):
            mm = pe.transpose(k.pt[:, j * P:(j + 1) * P], k.y[:, 4 * q + j, :], k.ident[:, :])
        mm.then_inc(e.turned, 1)
        pe.wait_ge(e.xnT, q + 1)
        if similar:
            w = (k.w0, k.w1)[q // 2]
            pe.matmul(w[:, 512 * (q % 2):512 * (q % 2) + 512], k.m_wp[:, :], k.m_xT[:, q, :],
                      start=True, stop=True).then_inc(e.raw, 1)
        else:
            for j in range(4):
                t = 4 * q + j
                mm = pe.matmul(k.py[:, 8 * t:8 * t + 8], k.m_xT[:, q, j * P:(j + 1) * P], k.m_wr[:, :],
                               start=True, stop=True)
    if similar:
        pe.wait_ge(e.sim_scaled, 1)
        pe.transpose(k.pt[:, 0:8], k.m_sim[:, :], k.ident[0:8, 0:8]).then_inc(e.sim_turned, 1)
        pe.wait_ge(e.sim_T, 1)
        for t in range(TILES):
            if t % 4 == 0:
                pe.wait_ge(e.projT, t // 4 + 1)
                pe.wait_ge(e.squares, t // 4 + 1)
            pe.matmul(k.py[:, 8 * t:8 * t + 8], k.m_projT[:, t * P:(t + 1) * P], k.m_wr[:, :], start=True, stop=True)
            mm = pe.matmul(k.py[:, P + t:P + t + 1], k.m_sq[:, t * P:(t + 1) * P], k.onescol[:, :],
                           start=True, stop=True)
    mm.then_inc(e.logits, 1)


def experts_tensor(pe, k, e, ne):
    bank = (lambda i: k.w2[:, 512 * (i % 2):512 * (i % 2) + 512])

    def quad(q):
        G = (lambda i: q * ne + (e.first + i))

        def hidden(i):
            for c in range(4):
                w = (k.w0, k.w1)[c // 2]
                pe.wait_ge(e.hid_ready, 4 * G(i) + (c - 3))
                pe.matmul(w[:, 512 * (c % 2):512 * (c % 2) + 512], k.m_fc[:, i, c * P:(c + 1) * P],
                          k.m_xT[:, bass.ds(q, 1), :].rearrange("p a n -> p (a n)"),
                          start=True, stop=True).then_inc(e.hid_psum, 1)

        def output(i):
            pe.wait_ge(e.hid_ready, 4 * G(i) + 4)
            pe.wait_ge(e.scaled, slot_before(G(i), i, ne))
            for j in range(4):
                for c in range(4):
                    mm = pe.matmul(bank(i)[:, j * P:(j + 1) * P], k.m_hid[i % 2][:, c, j * P:(j + 1) * P],
                                   k.m_proj[:, i, c, :], start=(c == 0), stop=(c == 3))
            mm.then_inc(e.out_psum, 1)

        for i in range(ne):
            hidden(i)
            if i:
                output(i - 1)
        output(ne - 1)

    with pe.Fori(0, QUADS) as q:
        quad(q)


def slot_before(G, i, ne):
    return G if i == 0 and ne % 2 else G - 1


def experts_bias_tensor(pe, k, e, ne):
    pe.wait_ge(e.gates, 1)
    for t in range(TILES):
        w = k.w0 if t < 8 else k.w1
        mm = pe.transpose(w[0:ne, (t % 8) * P:(t % 8 + 1) * P], k.m_gate[:, t, 0:ne], k.ident[:, :])
        if t % 8 == 7:
            mm.then_inc(e.gate_turned, 1)
    for t in range(TILES):
        if t % 8 == 0:
            pe.wait_ge(e.gateT, t // 8 + 1)
            if t == 0:
                pe.wait_ge(e.scaled, e.first + ne * QUADS)
        w = k.w2 if t < 8 else k.w0
        mm = pe.matmul(w[:, (t % 8) * P:(t % 8 + 1) * P], k.m_gateT[0:ne, t * P:(t + 1) * P], k.m_brow[0:ne, :],
                       start=True, stop=True)
        if t % 8 == 7:
            mm.then_inc(e.bias_psum, 1)


def experts_scalar(act, k, e, ne, similar, gelu):
    for q in range(QUADS):
        act.wait_ge(e.turned, q + 1)
        act.copy(k.m_xT[:, q, :], k.pt[:, :]).then_inc(e.xnT, 1)
        if similar:
            w = (k.w0, k.w1)[q // 2][:, 512 * (q % 2):512 * (q % 2) + 512]
            act.wait_ge(e.raw, q + 1)
            act.copy(k.m_projT[:, 512 * q:512 * q + 512], w).then_inc(e.projT, 1)
            act.activation(k.m_sq[:, 512 * q:512 * q + 512], w, ACT.Square).then_inc(e.squares, 1)
    if similar:
        act.wait_ge(e.sim_turned, 1)
        act.copy(k.m_wr[:, :], k.pt[:, 0:8]).then_inc(e.sim_T, 1)
    act.wait_ge(e.below, 1)
    act.activation(k.m_exp[:, :, :], k.m_exp[:, :, :], ACT.Exp).then_inc(e.exp, 1)

    with act.Fori(0, QUADS) as q:
        for i in range(ne):
            G = q * ne + (e.first + i)
            for c in range(4):
                w = (k.w0, k.w1)[c // 2]
                act.wait_ge(e.hid_psum, 4 * G + (c + 1))
                if c == 0:
                    act.wait_ge(e.out_psum, slot_before(G, i, ne))
                act.activation(k.m_hid[i % 2][:, c, :], w[:, 512 * (c % 2):512 * (c % 2) + 512], gelu,
                               bias=k.m_bfc[:, i, c:c + 1]).then_inc(e.hid_ready, 1)
    for c in range(2):
        act.wait_ge(e.gate_turned, c + 1)
        act.copy(k.m_gateT[0:ne, 1024 * c:1024 * c + 1024], (k.w0, k.w1)[c][0:ne, :]).then_inc(e.gateT, 1)


def similar_vector(dve, k, e):
    dve.wait_ge(e.loaded, 16 * EXPERT3_LOADS)
    link(dve, k, dve.tensor_tensor(k.m_simsq[:, :], k.m_sim[:, :], k.m_sim[:, :], ALU.mult))
    dve.reciprocal(k.m_rtemp[:, :], k.m_temp[:, :]).then_inc(e.cooled, 1)
    dve.tensor_reduce(k.m_simn[:, :], k.m_simsq[:, :], AX.X, ALU.add).then_inc(e.sim_norm2, 1)
    dve.wait_ge(e.sim_rnorm, 1)
    dve.tensor_scalar(k.m_sim[:, :], k.m_sim[:, :], k.m_simn[:, 0:1], None, ALU.mult).then_inc(e.sim_scaled, 1)


def gates_vector(dve, k, e, similar):
    lg, wide = k.m_logit[:, :, :], [P, TILES, 8]
    dve.wait_ge(e.logits, 1)
    raw = k.py[:, 0:P].rearrange("p (t e) -> p t e", e=8)
    if similar:
        dve.tensor_copy(k.m_norm2[:, :], k.py[:, P:P + TILES]).then_inc(e.norm2, 1)
        dve.wait_ge(e.rnorm, 1)
        link(dve, k, dve.tensor_tensor(lg, raw, k.m_norm2[:, :, None].broadcast_to(wide), ALU.mult))
        dve.wait_ge(e.cooled, 1)
        link(dve, k, dve.tensor_scalar(lg, lg, k.m_rtemp[:, 0:1], None, ALU.mult))
    else:
        link(dve, k, dve.tensor_copy(lg, raw))
    link(dve, k, dve.tensor_reduce(k.m_top[:, :], lg, AX.X, ALU.max))
    dve.tensor_tensor(k.m_exp[:, :, :], lg, k.m_top[:, :, None].broadcast_to(wide), ALU.subtract).then_inc(e.below, 1)
    pairs = [P, TILES, 8, 8]
    split = (lambda b: b.rearrange("p t (e j) -> p t e j", e=8))
    link(dve, k, dve.tensor_tensor(split(k.m_greater), lg[:, :, None, :].broadcast_to(pairs), lg[:, :, :, None].broadcast_to(pairs),
                                   ALU.is_gt))
    link(dve, k, dve.tensor_tensor(split(k.m_equal), lg[:, :, None, :].broadcast_to(pairs), lg[:, :, :, None].broadcast_to(pairs),
                                   ALU.is_equal))
    link(dve, k, dve.tensor_tensor(k.m_equal, k.m_equal, k.m_tri[:, None, :].broadcast_to([P, TILES, SEQ]),
                                   ALU.mult))
    link(dve, k, dve.tensor_tensor(k.m_equal, k.m_equal, k.m_greater, ALU.add))
    link(dve, k, dve.tensor_reduce(k.m_rank[:, :, :], split(k.m_equal), AX.X, ALU.add))
    dve.wait_ge(e.exp, 1)
    link(dve, k, dve.scalar_tensor_tensor(out=k.m_exp[:, :, :], in0=k.m_rank[:, :, :], scalar=2.0, in1=k.m_exp[:, :, :],
                                          op0=ALU.is_lt, op1=ALU.mult))
    link(dve, k, dve.tensor_reduce(k.m_top[:, :], k.m_exp[:, :, :], AX.X, ALU.add))
    link(dve, k, dve.reciprocal(k.m_top[:, :], k.m_top[:, :]))
    dve.tensor_tensor(k.m_gate[:, :, 0:8], k.m_exp[:, :, :], k.m_top[:, :, None].broadcast_to(wide),
                      ALU.mult).then_inc(e.gates, 1)
    dve.wait_ge(e.gates, 1)


def experts_vector(dve, k, e, ne, similar):
    if similar:
        similar_vector(dve, k, e)
    gates_vector(dve, k, e, similar)
    with dve.Fori(0, QUADS) as q:
        for i in range(ne):
            G = q * ne + (e.first + i)
            bank = k.w2[:, 512 * (i % 2):512 * (i % 2) + 512].rearrange("p (j n) -> p j n", j=4)
            dve.wait_ge(e.out_psum, G + 1)
            dve.wait_ge(e.added, slot_before(G, i, ne))
            dve.tensor_tensor(k.m_scaled[:, i % 2, :, :], bank,
                              k.m_gate[:, bass.ds(q * 4, 4), i:i + 1].broadcast_to([P, 4, P]),
                              ALU.mult).then_inc(e.scaled, 1)
    dve.wait_ge(e.added, e.first + ne * QUADS)
    for c in range(2):
        dve.wait_ge(e.bias_psum, c + 1)
        rows = k.x[:, 8 * c:8 * c + 8, :].rearrange("p t n -> p (t n)")
        dve.tensor_tensor(rows, rows, (k.w2, k.w0)[c][:, :], ALU.add).then_inc(e.done, 1)
    dve.wait_ge(e.done, 2)


def experts_gpsimd(pool, k, e, ne, similar):
    if similar:
        pool.wait_ge(e.sim_norm2, 1)
        pool.tensor_scalar(k.m_simn[:, :], k.m_simn[:, :], 1e-24, None, ALU.max).then_inc(e.sim_floor, 1)
        pool.wait_ge(e.sim_floor, 1)
        pool.tensor_tensor(k.m_simn[:, :], k.m_simn[:, :], k.power[0:8, 0:1], ALU.pow).then_inc(e.sim_rnorm, 1)
        pool.wait_ge(e.norm2, 1)
        pool.tensor_scalar(k.m_norm2[:, :], k.m_norm2[:, :], 1e-24, None, ALU.max).then_inc(e.floor, 1)
        pool.wait_ge(e.floor, 1)
        pool.tensor_tensor(k.m_norm2[:, :], k.m_norm2[:, :], k.power[:, :], ALU.pow).then_inc(e.rnorm, 1)
    with pool.Fori(0, QUADS) as q:
        for i in range(ne):
            G = q * ne + (e.first + i)
            rows = k.x[:, bass.ds(q * 4, 4), :]
            wait_apart(pool, k, e.scaled, G + 1)
            pool.wait_ge(e.added, G)
            pool.tensor_tensor(rows, rows, k.m_scaled[:, i % 2, :, :], ALU.add).then_inc(e.added, 1)



def first_loads(k, a):
    return [
        (k.x[:, :, :], a["x"].rearrange("(t p) d -> p t d", p=P)),
        (k.a_ly[:, :], a["a_ly"]), (k.a_lx[:, :], a["a_lx"]), (k.a_tx[:, :, :], a["a_tx"]),
        (k.a_ty[:, :, :], a["a_ty"]), (k.a_lo[:, :], a["a_lo"]), (k.a_to0[:, :], a["a_to0"]),
        (k.a_to1[:, :], a["a_to1"]), (k.a_mask[0:SEQ, :], a["a_mask"]), (k.a_mask[SEQ:P, :], a["a_mask"]),
        (k.rope[:, :], a["rope"]), (k.band[:, :], a["band"]), (k.shift[:, :], a["shift"]),
        (k.s_w[:, :, :, :], a["s_w"]), (k.s_cols[:, :, :], a["s_cols"]), (k.s_bo[:, :, :], a["s_bo"]),
        (k.member[:, :], a["member"]), (k.m_tri[:, :], a["m_tri"]),
        (k.f_bytes[:, :], a["f_w"]), (k.f_ws[:, :], a["f_ws"].partition_broadcast(P)),
        (k.f_bias[:, :], a["f_bias"].partition_broadcast(P)),
    ]


N_LOADS = 21

B_LOADS, C_LOADS = 3, 4


def load_local(sp, k, a, d):
    row = (lambda x: x[d]) if isinstance(d, int) else (lambda x: x[bass.ds(d, 1)].rearrange("a p n -> p (a n)"))
    sp.dma_start(k.b_wqkv[:, :], row(a["b_wqkv"])).then_inc(k.b_loaded, 16)
    sp.dma_start(k.b_wo[:, :, :].rearrange("p h n -> p (h n)"), row(a["b_wo"])).then_inc(k.b_loaded, 16)
    sp.dma_start(k.b_scales[:, :], row(a["b_scales"]).partition_broadcast(P)).then_inc(k.b_loaded, 16)


def load_gated(sp, k, a, d):
    row = (lambda x: x[d]) if isinstance(d, int) else (lambda x: x[bass.ds(d, 1)].rearrange("a p n -> p (a n)"))
    sp.dma_start(k.c_w1[:, :], row(a["c_w1"])).then_inc(k.c_loaded, 16)
    sp.dma_start(k.c_w2[:, :, :].rearrange("p c n -> p (c n)"), row(a["c_w2"])).then_inc(k.c_loaded, 16)
    sp.dma_start(k.c_cols[:, :], row(a["c_cols"])).then_inc(k.c_loaded, 16)
    sp.dma_start(k.c_b2[:, :], row(a["c_b2"])).then_inc(k.c_loaded, 16)


def layers(eng, run):
    with eng.Fori(0, DEPTH) as d:
        run(d * TILES + (PHANTOM + TILES), d * QUADS + PHANTOM)


def small_ctx(sp, k, a, n):
    first, ctx = PHANTOM + TILES * n, a["ctxT"]
    before = (k.v_psum, PHANTOM + TILES) if n == 0 else (k.d.v_psum, first)
    for s in range(2):
        sp.wait_ge(*before)
        sp.dma_start(k.ctxT[:, s, :], ctx[s, :, :]).then_inc(k.ctx_loaded[s], 16)
    with sp.Fori(2, TILES - 1, 2) as t:
        for s in range(2):
            sp.wait_ge(k.d.v_psum, t + s + (first - 1))
            sp.dma_start(k.ctxT[:, s, :], ctx[bass.ds(t + s, 1), :, :].rearrange("a p n -> p (a n)")
                         ).then_inc(k.ctx_loaded[s], 16)


EXPERT2_LOADS, EXPERT3_LOADS = 5, 7


def load_experts(sp, k, a, n, e, ne):
    pairs = [(k.m_fc[:, 0:ne, :], a[f"m{n}_fc"]), (k.m_proj[:, 0:ne, :, :], a[f"m{n}_proj"]),
             (k.m_bfc[:, 0:ne, :], a[f"m{n}_bfc"]), (k.m_brow[0:ne, :], a[f"m{n}_brow"])]
    if n == 2:
        pairs += [(k.m_wr[:, :], a["m2_wr"])]
    else:
        pairs += [(k.m_wp[:, :], a["m3_wp"]), (k.m_sim[:, :], a["m3_sim"]),
                  (k.m_temp[:, :], a["m3_temp"].partition_broadcast(P))]
    for dst, src in pairs:
        sp.dma_start(dst, src).then_inc(e.loaded, 16)


def sync_program(nc, sp, k, a, out):
    first = PHANTOM
    for dst, src in first_loads(k, a):
        sp.dma_start(dst, src).then_inc(k.loaded, 16)
    ctx = a["ctxT"]
    for s in range(2):
        sp.dma_start(k.ctxT[:, s, :], ctx[s, :, :]).then_inc(k.ctx_loaded[s], 16)
    load_local(sp, k, a, 0)
    load_gated(sp, k, a, 0)
    with sp.Fori(2, TILES - 1, 2) as t:
        for s in range(2):
            sp.wait_ge(k.v_psum, t + s + first - 1)
            sp.dma_start(k.ctxT[:, s, :], ctx[bass.ds(t + s, 1), :, :].rearrange("a p n -> p (a n)")
                         ).then_inc(k.ctx_loaded[s], 16)
    sp.wait_ge(k.updated, PHANTOM + TILES)
    load_experts(sp, k, a, 2, k.e[0], 9)
    with sp.Fori(1, DEPTH) as d:
        sp.wait_ge(k.updated, d * TILES + (PHANTOM + TILES))
        load_local(sp, k, a, d)
        sp.wait_ge(k.y_done, d * QUADS + PHANTOM)
        load_gated(sp, k, a, d)
    small_ctx(sp, k, a, 0)
    small_ctx(sp, k, a, 1)
    sp.wait_ge(k.e[0].done, 2)
    load_experts(sp, k, a, 3, k.e[1], 8)
    small_ctx(sp, k, a, 2)
    sp.wait_ge(k.e[1].done, 2)
    sp.dma_start(out.rearrange("(t p) d -> p t d", p=P), k.x[:, :, :]).then_inc(k.stored, 16)
    sp.wait_ge(k.stored, 16)


def tensor_program(nc, pe, k):
    pe.wait_ge(k.loaded, 16 * N_LOADS)
    pe.wait_ge(k.consts, 5)
    cross0_tensor(pe, k, PHANTOM)

    def run(first, qfirst):
        local_tensor(pe, k, first)
        gated_tensor(pe, k, first, qfirst)
    layers(pe, run)
    pe.wait_ge(k.y_done, PHANTOM + DEPTH * QUADS)
    small_tensor(pe, k, 0)
    fp8_tensor(pe, k)
    pe.wait_ge(k.f.done, 1)
    small_tensor(pe, k, 1)
    experts2, experts3 = k.e
    pe.wait_ge(experts2.loaded, 16 * EXPERT2_LOADS)
    pe.wait_ge(k.d.updated, PHANTOM + 2 * TILES)
    experts_prelude_tensor(pe, k, experts2, False)
    experts_tensor(pe, k, experts2, 9)
    experts_bias_tensor(pe, k, experts2, 9)
    pe.wait_ge(experts2.done, 2)
    quantise_tensor(pe, k)
    small_tensor(pe, k, 2)
    pe.wait_ge(experts3.loaded, 16 * EXPERT3_LOADS)
    pe.wait_ge(k.d.updated, PHANTOM + 3 * TILES)
    experts_prelude_tensor(pe, k, experts3, True)
    experts_tensor(pe, k, experts3, 8)
    experts_bias_tensor(pe, k, experts3, 8)


def scalar_program(nc, act, k):
    act.wait_ge(k.consts, 5)
    cross0_scalar(act, k, PHANTOM)

    def run(first, qfirst):
        local_scalar(act, k, first, qfirst)
        gated_scalar(act, k, first, qfirst)
    layers(act, run)
    small_scalar(act, k, 0, 8 ** -0.5)
    fp8_scalar(act, k)
    small_scalar(act, k, 1, 1.0)
    experts_scalar(act, k, k.e[0], 9, False, ACT.Gelu_apprx_tanh)
    small_scalar(act, k, 2, 8 ** -0.5)
    experts_scalar(act, k, k.e[1], 8, True, ACT.Gelu)


def vector_program(nc, dve, k):
    dve.memset(k.ones[:, :], 1.0).then_inc(k.consts, 1)
    dve.memset(k.sT[:, :, :], 0.0).then_inc(k.consts, 1)
    dve.memset(k.s_v[:, :, :, :, :, :], 0.0)
    dve.memset(k.m_gate[:, :, 8:9], 1.0)
    dve.memset(k.onescol[:, :], 1.0)
    dve.memset(k.ones4[:, :], 1.0).then_inc(k.consts, 1)
    dve.wait_ge(k.loaded, 16 * N_LOADS)
    dve.tensor_copy(k.band16[:, :], k.band[:, :]).then_inc(k.band_ready, 1)
    cross0_vector(dve, k, PHANTOM)
    dve.wait_ge(k.updated, PHANTOM + TILES)
    fresh_vector(dve, k, 1)

    def run(first, qfirst):
        local_vector(dve, k, first)
        gated_vector(dve, k, first, qfirst)
    layers(dve, run)
    dve.wait_ge(k.y_done, PHANTOM + DEPTH * QUADS)
    dve.tensor_tensor(k.x[:, :, :], k.x[:, :, :], k.y[:, :, :], ALU.add).then_inc(k.x_done, 1)
    dve.wait_ge(k.x_done, 1)
    small_vector(dve, k, 0)
    dve.wait_ge(k.d.updated, PHANTOM + TILES)
    fresh_vector(dve, k, 2)
    fp8_weight_vector(dve, k)
    fp8_vector(dve, k)
    small_vector(dve, k, 1)
    dve.wait_ge(k.d.updated, PHANTOM + 2 * TILES)
    fresh_vector(dve, k, 3)
    experts_vector(dve, k, k.e[0], 9, False)
    quantise_vector(dve, k)
    small_vector(dve, k, 2)
    dve.wait_ge(k.d.updated, PHANTOM + 3 * TILES)
    fresh_vector(dve, k, 4)
    experts_vector(dve, k, k.e[1], 8, True)


def gpsimd_program(nc, pool, k):
    pool.memset(k.ident[:, :], 0.0).then_inc(k.powers, 1)
    pool.memset(k.power[:, :], -0.5).then_inc(k.powers, 1)
    pool.memset(k.eps[:, :], EPS).then_inc(k.powers, 1)
    pool.wait_ge(k.powers, 3)
    pool.affine_select(out=k.ident[:, :], in_=k.ident[:, :], compare_op=ALU.not_equal, fill=1.0, base=0,
                       pattern=[[-1, P]], channel_multiplier=1).then_inc(k.consts, 1)
    pool.wait_ge(k.consts, 4)
    pool.tensor_copy(k.ident16[:, :], k.ident[:, :]).then_inc(k.consts, 1)
    cross0_gpsimd(pool, k, PHANTOM)
    fresh_gpsimd(pool, k, 1)

    def run(first, qfirst):
        local_gpsimd(pool, k, first)
        gated_gpsimd(pool, k, first, qfirst)
    layers(pool, run)
    small_gpsimd(pool, k, 0)
    fresh_gpsimd(pool, k, 2)
    small_gpsimd(pool, k, 1)
    fresh_gpsimd(pool, k, 3)
    experts_gpsimd(pool, k, k.e[0], 9, False)
    small_gpsimd(pool, k, 2)
    fresh_gpsimd(pool, k, 4)
    experts_gpsimd(pool, k, k.e[1], 8, True)



def tables():
    f = np.float32
    half = np.arange(0, HD, 2, dtype=f)
    t = np.arange(SEQ, dtype=f)
    angle = t[:, None] * (f(1.0) / f(10000.0) ** (half / f(HD)))[None, :]
    base = (half + f(0.4 * HD)) / f(1.4 * HD)
    grow = base[None, :] ** ((t - SEQ // 2) / (WINDOW // 2))[:, None]
    cos, sin = np.cos(angle), np.sin(angle)
    rope = np.concatenate([cos * grow, cos * grow, -sin * grow, sin * grow,
                           cos / grow, cos / grow, -sin / grow, sin / grow], axis=1).astype(f)
    i, j = np.arange(SEQ)[:, None], np.arange(SEQ)[None, :]
    band = np.where((i < j) | (i > j + WINDOW), f(-1e30), f(0)).astype(f)
    shift = np.eye(P, k=1, dtype=f)
    shift[SEQ - 1, SEQ] = 0
    member = (np.arange(P)[:, None] % 64 // 8 == np.arange(8)[None, :]).astype(f)
    lower = np.tile(np.tril(np.ones((8, 8), f), -1).reshape(1, 64), (P, 1))
    return {"m_tri": lower, "member": member, "rope": np.tile(rope, (2, 1)), "band": np.tile(band, (2, 1)), "shift": shift}


def layout(i):
    n = {name: np.asarray(v) for name, v in i.items()}
    a = {}
    a["x"] = n["x"].reshape(TILES * P, P)
    a["ctxT"] = n["ctx_1024"].reshape(TILES, P, P).transpose(0, 2, 1)
    a["a_mask"] = n["mask_SxS2_ff0"].T
    a["a_ly"] = n["L0_xattn_Ly"].transpose(1, 0, 2).reshape(P, 1024)
    a["a_lx"] = n["L0_xattn_Lx"].transpose(1, 0, 2).reshape(P, 1024)
    a["a_tx"] = n["L0_xattn_Tx"].reshape(PAIRS, 2, P, HD).transpose(2, 1, 0, 3).reshape(P, 2, 512)
    a["a_ty"] = n["L0_xattn_Ty"].reshape(PAIRS, 2, P, HD).transpose(1, 3, 0, 2).reshape(P, PAIRS, P)
    a["a_lo"] = n["L0_xattn_Lo"].reshape(PAIRS, P).T
    a["a_to0"] = n["L0_xattn_To0"].reshape(PAIRS, P).T
    a["a_to1"] = n["L0_xattn_To1"].reshape(1, P)
    wqkv = n["L0_ffn_Wqkv"].reshape(DEPTH, P, 3, PAIRS, 2, HD)
    v_even_first = wqkv[:, :, 2].transpose(0, 1, 3, 2, 4).reshape(DEPTH, P, 1024)
    a["b_wqkv"] = np.concatenate([n["L0_ffn_Wqkv"][:, :, :2048], v_even_first], axis=2)
    a["b_wo"] = n["L0_ffn_Wo"].reshape(DEPTH, PAIRS, P, P).transpose(0, 2, 1, 3).reshape(DEPTH, P, 1024)
    halves = [np.roll(n[s], r, axis=1) for s in ("L0_ffn_q_scale", "L0_ffn_k_scale") for r in (0, HD // 2)]
    a["b_scales"] = np.concatenate(halves, axis=1).reshape(DEPTH, 1, 4 * HD)
    a["c_w1"] = n["L0_ffn_W1"]
    w2 = np.zeros((DEPTH, 3 * P, P), np.float32)
    w2[:, :HID] = n["L0_ffn_W2"]
    a["c_w2"] = w2.reshape(DEPTH, 3, P, P).transpose(0, 2, 1, 3).reshape(DEPTH, P, 3 * P)
    cols = np.zeros((DEPTH, 8, P), np.float32)
    cols[:, 0], cols[:, 1] = n["L0_ffn_ln_g"], n["L0_ffn_ln_b"]
    for c, (at, m) in enumerate(CHUNKS):
        cols[:, 2 + c, :m] = n["L0_ffn_b1"][:, at:at + m]
        cols[:, 5 + c, :m] = n["L0_ffn_b1"][:, HID + at:HID + at + m]
    a["c_cols"] = cols.transpose(0, 2, 1)
    a["c_b2"] = n["L0_ffn_b2"].reshape(DEPTH, 1, P)
    heads_apart = (lambda w: w.reshape(P, PAIRS, 2, 8).transpose(0, 2, 1, 3).reshape(P, P))
    per_stage = [[n["L1_xattn_w_q"], n["L1_xattn_w_k"], n["L1_xattn_w_v"], n["L1_xattn_w_out"]],
                 [n[f"L2_xattn_W{c}"].T for c in "qkvo"], [n[f"L3_xattn_W{c}"].T for c in "qkvo"]]
    a["s_w"] = np.stack([np.stack([wq, wk, heads_apart(wv), wo], 1) for wq, wk, wv, wo in per_stage], 1)
    zero = np.zeros(P, np.float32)
    a["s_cols"] = np.stack([np.stack(c, 1) for c in (
        [n["L1_xattn_b_q"], n["L1_xattn_b_k"], n["L1_xattn_b_v"]], [zero] * 3,
        [n["L3_xattn_bq"], n["L3_xattn_bk"], n["L3_xattn_bv"]])], 1)
    a["s_bo"] = np.stack([n["L1_xattn_b_out"], n["L2_xattn_bo"], n["L3_xattn_bo"]])[None]
    a["f_w"] = n["L1_ffn_weight"].view(np.uint8).T
    a["f_ws"] = n["L1_ffn_weight_scale"].reshape(1, 1)
    a["f_bias"] = n["L1_ffn_bias"].reshape(1, P)
    both = (lambda routed, shared: np.concatenate([routed, shared[None]]))
    layers2 = [both(n["L2_ffn_" + w], n["L2_ffn_" + w + "_s"]) for w in ("Wfc", "bfc", "Wproj", "bproj")]
    layers3 = [n["L3_ffn_" + w] for w in ("W1", "b1", "W2", "b2")]
    for m, (fc, bfc, proj, brow) in ((2, layers2), (3, layers3)):
        a[f"m{m}_fc"] = fc.transpose(1, 0, 2)
        a[f"m{m}_bfc"] = bfc.reshape(-1, 4, P).transpose(2, 0, 1)
        a[f"m{m}_proj"] = proj.reshape(-1, 4, P, P).transpose(2, 0, 1, 3)
        a[f"m{m}_brow"] = brow
    a["m2_wr"] = n["L2_ffn_Wr"]
    a["m3_wp"] = n["L3_ffn_Wp"].T
    a["m3_sim"] = n["L3_ffn_sim_matrix"]
    a["m3_temp"] = n["L3_ffn_temperature"].reshape(1, 1)
    a.update(tables())
    return {name: np.ascontiguousarray(v) for name, v in a.items()}


def kernel(**inputs):
    import concourse.bacc as bacc
    from concourse.bass_utils import run_bass_kernel_spmd

    nc = bacc.Bacc("TRN2", target_bir_lowering=False, num_devices=1)
    arrays = layout(inputs)
    dram = {name: nc.dram_tensor("in_" + name, v.shape, mybir.dt.from_np(v.dtype), kind="ExternalInput").ap()
            for name, v in arrays.items()}
    out = nc.dram_tensor("out", (TILES * P, P), F32, kind="ExternalOutput").ap()
    build(nc, dram, out)
    r = run_bass_kernel_spmd(nc, [{"in_" + name: v for name, v in arrays.items()}], core_ids=[0])
    return r.results[0]["out"].reshape(32, SEQ, P)
```

```python
from contextlib import ExitStack

import numpy as np

import concourse.bass as bass
from concourse import mybir

F32 = mybir.dt.float32
BF16 = mybir.dt.bfloat16
I32 = mybir.dt.int32
ALU = mybir.AluOpType
ACT = mybir.ActivationFunctionType
AX = mybir.AxisListType

P = 128
SEQ = 64
TILES = 16
HEADS, HD = 16, 64
PAIRS = HEADS // 2
DEPTH = 6
WINDOW = 32
EPS = 1e-5
HID = 341
CHUNKS = [(0, 128), (128, 128), (256, 85)]
PHANTOM = 2



class Names:
    pass


def build(nc, a, out):
    ctx = ExitStack()
    with ctx:
        def sb(name, shape, dt=F32):
            return ctx.enter_context(nc.sbuf_tensor(name, shape, dt))

        def pb(name, shape, dt=F32):
            return ctx.enter_context(nc.psum_tensor(name, shape, dt))

        k = Names()
        primed = []

        def sem(name, first=0):
            s = ctx.enter_context(nc.semaphore(name))
            if first:
                primed.append((s, first))
            return s

        k.x = sb("x_all", [P, TILES, P])
        k.y = sb("y_all", [P, TILES, P])
        k.ident = sb("ident", [P, P])
        k.shift = sb("shift", [P, P])
        k.ones = sb("ones", [1, P])
        k.onescol = sb("onescol", [P, 1])
        k.power = sb("power", [P, HEADS])
        k.eps = sb("eps", [P, HEADS])
        k.ctxT = sb("ctxT", [P, 2, P])
        k.norm, k.fresh = Names(), Names()
        k.norm.stats = sb("norm_stats", [P, 2, 6])
        k.norm.means = sb("norm_means", [P, 2, 2])
        k.norm.roots = sb("norm_roots", [P, 2, 1])
        k.fresh.stats = sb("fresh_stats", [P, 2, 6])
        k.fresh.means = sb("fresh_means", [P, 2, 2])
        k.fresh.roots = sb("fresh_roots", [P, 2, 1])
        k.normed = sb("normed", [P, 2, P])
        k.xT = sb("xT", [P, 2, P])
        k.qT = sb("qT", [P, 2, PAIRS, P])
        k.kT = sb("kT", [P, 2, PAIRS, P])
        k.v2 = sb("v2", [P, 2, 2, 512])
        k.logit = sb("logit", [P, 2, HEADS, SEQ])
        k.prob = sb("prob", [P, 2, HEADS, SEQ])
        k.probT = sb("probT", [P, PAIRS, P])
        k.oT = sb("oT", [P, PAIRS, P])
        k.top = sb("top", [P, 2, HEADS])
        k.den = sb("den", [P, 2, HEADS])
        k.rden = sb("rden", [P, 2, HEADS])
        k.w0 = pb("w0", [P, 1024])
        k.w1 = pb("w1", [P, 1024])
        k.w2 = pb("w2", [P, 1024])
        k.pt = pb("pt", [P, 512])
        k.py = pb("py", [P, 512])

        k.m_fc = sb("m_fc", [P, 9, 512])
        k.a_ly, k.a_lx, k.a_tx, k.a_ty = (k.m_fc[:, 2 * i:2 * i + 2, :].rearrange("p a n -> p (a n)")
                                          for i in range(4))
        k.a_tx = k.a_tx.rearrange("p (a n) -> p a n", a=2)
        k.a_ty = k.a_ty.rearrange("p (h n) -> p h n", h=PAIRS)
        k.a_lo = sb("a_lo", [P, PAIRS])
        k.a_to0 = sb("a_to0", [P, PAIRS])
        k.a_to1 = sb("a_to1", [1, P])
        k.a_mask = sb("a_mask", [P, SEQ])

        k.b_wqkv = sb("b_wqkv", [P, 3072])
        k.b_wo = sb("b_wo", [P, PAIRS, P])
        k.b_scales = sb("b_scales", [P, 4 * HD])
        k.rope = sb("rope", [P, 4 * HD])
        k.rot = sb("rot", [P, 4, HD])
        k.band = sb("band", [P, SEQ])
        k.ytile = sb("ytile", [P, 2, P])
        k.sT = sb("sT", [P, 2, P])
        k.straight = sb("straight", [P, 2, HEADS, HD])
        k.turned = sb("turned", [P, 2, HEADS, HD])
        k.straights = [k.straight, sb("straight_odd", [P, 2, HEADS, HD])]
        k.sq = sb("sq", [P, 2, HEADS, HD])
        k.norm2 = sb("norm2", [P, 2, HEADS])
        k.newton = sb("newton", [P, 2, HEADS])
        k.rnorms = sb("rnorms", [P, 2, 2, HEADS])
        k.c_w1 = sb("c_w1", [P, 2 * HID])
        k.c_w2 = sb("c_w2", [P, 3, P])
        k.c_cols = sb("c_cols", [P, 8])
        k.xs = sb("xs", [P, 2, 4, P])
        k.xnT = sb("xnT", [P, 2, 512])
        k.gate = sb("gate", [P, 3, 512])
        k.hid = sb("hid", [P, 3, 512])
        k.stats4 = sb("stats4", [P, TILES, 6])
        k.mv4 = sb("mv4", [P, TILES, 2])
        k.rstd4 = sb("rstd4", [P, TILES])

        k.s_w = sb("s_w", [P, 3, 4, P])
        k.s_cols = sb("s_cols", [P, 3, 3])
        k.s_bo = sb("s_bo", [1, 3, P])
        k.member = sb("member", [P, 8])
        k.s_qT = sb("s_qT", [P, 2, P])
        k.s_v = sb("s_v", [P, 2, 2, PAIRS, 2, 8])
        k.s_rows = sb("s_rows", [P, P])
        k.s_oT = sb("s_oT", [P, P])
        k.wmax = sb("wmax", [P, 4])
        k.wmaxT = sb("wmaxT", [4, 1])
        k.wdiag = sb("wdiag", [4, 4])
        k.ones4 = sb("ones4", [4, P])
        k.wstep = sb("wstep", [P, 4])
        k.wrstep = sb("wrstep", [P, 4])

        k.band16 = sb("band16", [P, SEQ], BF16)
        k.ident16 = sb("ident16", [P, P], BF16)
        k.f_bytes = sb("f_bytes", [P, P], mybir.dt.uint8)
        k.f_w = sb("f_w", [P, P], BF16)
        k.f_ws = sb("f_ws", [P, 1])
        k.f_bias = sb("f_bias", [P, P])
        k.f_scale = sb("f_scale", [P, TILES])
        k.f_rscale = sb("f_rscale", [P, TILES])
        k.m_proj = sb("m_proj", [P, 9, 4, P])
        k.m_bfc = sb("m_bfc", [P, 9, 4])
        k.m_brow = sb("m_brow", [9, P])
        k.m_wr = sb("m_wr", [P, 8])
        k.m_wp = sb("m_wp", [P, P])
        k.m_sim = sb("m_sim", [8, P])
        k.m_simsq = sb("m_simsq", [8, P])
        k.m_simn = sb("m_simn", [8, 1])
        k.m_temp = sb("m_temp", [P, 1])
        k.m_rtemp = sb("m_rtemp", [P, 1])
        k.m_tri = sb("m_tri", [P, SEQ])
        k.m_norm2 = sb("m_norm2", [P, TILES])
        k.m_logit = sb("m_logit", [P, TILES, 8])
        k.m_exp = sb("m_exp", [P, TILES, 8])
        k.m_rank = sb("m_rank", [P, TILES, 8])
        k.m_top = sb("m_top", [P, TILES])
        k.m_gate = sb("m_gate", [P, TILES, 9])
        wide = (lambda b: b[:, :, :, :].rearrange("p a h n -> p (a h n)"))
        k.s_k8 = wide(k.straight).rearrange("p (s j n) -> p s j n", s=2, j=8)
        k.m_scaled = wide(k.xs).rearrange("p (s j n) -> p s j n", s=2, j=4)
        k.f_int, k.f_mag = (wide(k.sq)[:, i * P:(i + 1) * P].bitcast(mybir.dt.int32) for i in range(2))
        k.f_val, k.f_low = (wide(k.sq)[:, i * P:(i + 1) * P] for i in range(2, 4))
        k.f_q, k.f_qT = (k.prob[:, i, :, :].rearrange("p h n -> p (h n)").bitcast(BF16)
                         .rearrange("p (t n) -> p t n", n=P) for i in range(2))
        k.m_xT = k.qT[:, :, :, :].rearrange("p a h n -> p (a h n)").rearrange("p (q n) -> p q n", q=4)
        k.m_projT = k.kT[:, :, :, :].rearrange("p a h n -> p (a h n)")
        k.m_sq = k.logit[:, :, :, :].rearrange("p a h n -> p (a h n)")
        k.m_greater = k.sq[:, 0, :, :].rearrange("p h n -> p (h n)").rearrange("p (t m) -> p t m", t=TILES)
        k.m_equal = k.sq[:, 1, :, :].rearrange("p h n -> p (h n)").rearrange("p (t m) -> p t m", t=TILES)
        k.m_gateT = k.v2[0:9, :, :, :].rearrange("p a b n -> p (a b n)")
        k.m_hid = [b[:, :, :, :].rearrange("p a h n -> p (a h n)").rearrange("p (c n) -> p c n", c=4)
                   for b in (k.straight, k.turned)]

        k.x_head = sem("x_head")
        k.loaded = sem("loaded")
        k.loaded_later = sem("loaded_later")
        k.stored = sem("stored")
        k.consts = sem("consts")
        k.powers = sem("powers")
        k.band_ready = sem("band_ready")
        k.xT_psum = sem("xT_psum", PHANTOM)
        k.xT_ready = sem("xT_ready", PHANTOM)
        k.q_psum = sem("q_psum", PHANTOM)
        k.k_psum = sem("k_psum", PHANTOM)
        k.v_psum = sem("v_psum", PHANTOM)
        k.qT_ready = sem("qT_ready", PHANTOM)
        k.kT_ready = sem("kT_ready", PHANTOM)
        k.v_ready = sem("v_ready", PHANTOM)
        k.s_psum = sem("s_psum", PHANTOM)
        k.masked = sem("masked", PHANTOM)
        k.top_ready = sem("top_ready", PHANTOM)
        k.shifted = sem("shifted", PHANTOM)
        k.exp_ready = sem("exp_ready", PHANTOM)
        k.den_ready = sem("den_ready", PHANTOM)
        k.rden_ready = sem("rden_ready", PHANTOM)
        k.prob_ready = sem("prob_ready", PHANTOM)
        k.pT_psum = sem("pT_psum", PHANTOM)
        k.pT_ready = sem("pT_ready", PHANTOM)
        k.o_psum = sem("o_psum", PHANTOM)
        k.oT_ready = sem("oT_ready", PHANTOM)
        k.y_psum = sem("y_psum", PHANTOM)
        k.updated = sem("updated", PHANTOM)
        k.ctx_loaded = [sem("ctx_even"), sem("ctx_odd")]

        k.norm.stat = sem("norm_stat", PHANTOM)
        k.norm.mv = sem("norm_mv", PHANTOM)
        k.norm.eps = sem("norm_eps", PHANTOM)
        k.norm.rstd = sem("norm_rstd", PHANTOM)
        k.norm.normed = sem("norm_normed", PHANTOM)
        k.fresh.stat = sem("fresh_stat", PHANTOM)
        k.fresh.mv = sem("fresh_mv", PHANTOM)
        k.fresh.eps = sem("fresh_eps", PHANTOM)
        k.fresh.rstd = sem("fresh_rstd", PHANTOM)
        k.fresh.normed = sem("fresh_normed", PHANTOM)
        B = PHANTOM + TILES
        k.b_loaded = sem("b_loaded")
        k.rot_ready = sem("rot_ready")
        k.low_shifted = sem("low_shifted", PHANTOM)
        k.low_exp = sem("low_exp", PHANTOM)
        k.y_copied = sem("y_copied", B)
        k.half_shifted = sem("half_shifted", B)
        k.q_squared = sem("q_squared", B)
        k.k_squared = sem("k_squared", B)
        k.q_turned = sem("q_turned", B)
        k.k_turned = sem("k_turned", B)
        k.q_norm2 = sem("q_norm2", B)
        k.k_norm2 = sem("k_norm2", B)
        k.newton_step = sem("newton_step", NEWTON * B)
        k.q_added = sem("q_added", B)
        k.k_added = sem("k_added", B)
        k.q_final = sem("q_final", B)
        k.k_final = sem("k_final", B)
        k.qT_psum = sem("qT_psum", B)
        k.kT_psum = sem("kT_psum", B)
        k.c_loaded = sem("c_loaded")
        k.sh_psum = sem("sh_psum", PHANTOM)
        k.xs_low = sem("xs_low", PHANTOM)
        k.xs_high = sem("xs_high", PHANTOM)
        k.quad_stat = sem("quad_stat", PHANTOM)
        k.quad_mv = sem("quad_mv", PHANTOM)
        k.quad_eps = sem("quad_eps", PHANTOM)
        k.quad_rstd = sem("quad_rstd", PHANTOM)
        k.quad_normed = sem("quad_normed", PHANTOM)
        k.quad_turned = sem("quad_turned", PHANTOM)
        k.xnT_ready = sem("xnT_ready", PHANTOM)
        k.hid_psum = sem("hid_psum", 3 * PHANTOM)
        k.gated = sem("gated", 3 * PHANTOM)
        k.hid_ready = sem("hid_ready", 3 * PHANTOM)
        k.out_psum = sem("out_psum", PHANTOM)
        k.y_done = sem("y_done", PHANTOM)
        k.d = Names()
        k.d.xT_psum = sem("small_xT_psum", PHANTOM)
        k.d.xT_ready = sem("small_xT_ready", PHANTOM)
        k.d.q_psum = sem("small_q_psum", PHANTOM)
        k.d.k_psum = sem("small_k_psum", PHANTOM)
        k.d.v_psum = sem("small_v_psum", PHANTOM)
        k.d.q_ready = sem("small_q_ready", PHANTOM)
        k.d.k8_ready = sem("small_k8_ready", PHANTOM)
        k.d.v_ready = sem("small_v_ready", PHANTOM)
        k.d.s_psum = sem("small_s_psum", PHANTOM)
        k.d.top = sem("small_top", PHANTOM)
        k.d.shifted = sem("small_shifted", PHANTOM)
        k.d.exp = sem("small_exp", PHANTOM)
        k.d.den = sem("small_den", PHANTOM)
        k.d.rden = sem("small_rden", PHANTOM)
        k.d.pT_psum = sem("small_pT_psum", PHANTOM)
        k.d.pT_ready = sem("small_pT_ready", PHANTOM)
        k.d.o_psum = sem("small_o_psum", PHANTOM)
        k.d.rows = sem("small_rows", PHANTOM)
        k.d.o_turned = sem("small_o_turned", PHANTOM)
        k.d.oT_ready = sem("small_oT_ready", PHANTOM)
        k.d.y_psum = sem("small_y_psum", PHANTOM)
        k.d.updated = sem("small_updated", PHANTOM)
        k.quant = Names()
        k.quant.wmax = sem("quant_wmax")
        k.quant.turned = sem("quant_turned")
        k.quant.diag = sem("quant_diag")
        k.quant.spread = sem("quant_spread")
        k.quant.done = sem("quant_done")
        k.f = Names()
        k.f.weight = sem("fp8_weight")
        k.f.quantised = sem("fp8_quantised")
        k.f.turned = sem("fp8_turned")
        k.f.qT = sem("fp8_qT")
        k.f.product = sem("fp8_product")
        k.f.done = sem("fp8_done")
        k.e = []
        for n in (2, 3):
            e = Names()
            e.loaded = sem(f"experts{n}_loaded")
            e.xnT = sem(f"experts{n}_xnT")
            e.turned = sem(f"experts{n}_turned")
            e.logits = sem(f"experts{n}_logits")
            e.below = sem(f"experts{n}_below")
            e.exp = sem(f"experts{n}_exp")
            e.gates = sem(f"experts{n}_gates")
            e.gate_turned = sem(f"experts{n}_gate_turned")
            e.gateT = sem(f"experts{n}_gateT")
            e.bias_psum = sem(f"experts{n}_bias_psum")
            e.done = sem(f"experts{n}_done")
            e.first = PHANTOM if n == 2 else PHANTOM + 9 * QUADS
            k.e.append(e)
        e.projT = sem("experts3_projT")
        e.squares = sem("experts3_squares")
        e.sim_norm2 = sem("experts3_sim_norm2")
        e.sim_floor = sem("experts3_sim_floor")
        e.sim_rnorm = sem("experts3_sim_rnorm")
        e.sim_scaled = sem("experts3_sim_scaled")
        e.sim_turned = sem("experts3_sim_turned")
        e.sim_T = sem("experts3_sim_T")
        e.norm2 = sem("experts3_norm2")
        e.floor = sem("experts3_floor")
        e.rnorm = sem("experts3_rnorm")
        e.cooled = sem("experts3_cooled")
        e.raw = sem("experts3_raw")
        hid_psum, hid_ready = (sem(name, 4 * PHANTOM) for name in ("experts_hid_psum", "experts_hid_ready"))
        out_psum, scaled, added = (sem("experts_" + name, PHANTOM) for name in ("out_psum", "scaled", "added"))
        for e in k.e:
            e.hid_psum, e.hid_ready, e.out_psum, e.scaled, e.added = hid_psum, hid_ready, out_psum, scaled, added
        k.vector_link, k.links = sem("vector_link"), 0

        block = ctx.enter_context(nc.Block())

        @block.sync
        def _(sp):
            sync_program(nc, sp, k, a, out)

        @block.tensor
        def _(pe):
            tensor_program(nc, pe, k)

        @block.scalar
        def _(act):
            scalar_program(nc, act, k)

        @block.vector
        def _(dve):
            vector_program(nc, dve, k)

        @block.gpsimd
        def _(pool):
            for s, first in primed:
                pool.sem_inc(s, first)
            gpsimd_program(nc, pool, k)


def short_steps(eng, first, step):
    def single(i):
        step(first + i, i % 2, i, [0 <= i + n < TILES for n in (2, 1, 0, -1, -2)])

    for i in range(2):
        single(i)
    with eng.Fori(2, TILES - 3, 2) as t:
        step(first + t, 0, t, [True] * 5)
        step(first + t + 1, 1, t + 1, [True] * 5)
    for i in range(TILES - 2, TILES + 2):
        single(i)


def tile(ap, t):
    return ap[:, t, :] if isinstance(t, int) else ap[:, bass.ds(t, 1), :].rearrange("p a n -> p (a n)")



def cross0_tensor(pe, k, first):
    def turn_x(T, s):
        pe.wait_ge(k.norm.normed, T + 1)
        pe.wait_ge(k.xT_ready, T)
        pe.transpose(k.pt[:, 0:P], k.normed[:, s, :], k.ident[:, :]).then_inc(k.xT_psum, 1)

    def front(T, s, before):
        pe.wait_ge(k.xT_ready, T + 1)
        if before:
            pe.wait_ge(k.oT_ready, T - 1)
        for h in range(PAIRS):
            mm = pe.matmul(k.w0[:, h * P:(h + 1) * P], k.a_ly[:, h * P:(h + 1) * P], k.xT[:, s, :],
                           start=True, stop=True)
        mm.then_inc(k.q_psum, 1)
        pe.wait_ge(k.ctx_loaded[s], 8 * (T - s - first) + 16)
        pe.wait_ge(k.masked, T)
        if before:
            pe.wait_ge(k.pT_ready, T - 1)
        else:
            pe.wait_ge(k.v_ready, T)
        for h in range(PAIRS):
            mm = pe.matmul(k.w1[:, h * P:(h + 1) * P], k.a_lx[:, h * P:(h + 1) * P], k.ctxT[:, s, :],
                           start=True, stop=True)
        mm.then_inc(k.k_psum, 1)
        for b in range(2):
            for p in range(2):
                mm = pe.matmul(k.w2[64 * p:64 * p + 64, 512 * b:512 * b + 512],
                               k.ctxT[:, s, 64 * b:64 * b + 64], k.a_tx[:, p, :], start=True, stop=True)
        mm.then_inc(k.v_psum, 1)

    def rows(pairs):
        for h in pairs:
            mm = pe.matmul(k.py[:, 0:P], k.oT[:, h, :], k.a_ty[:, h, :], start=(h == 0), stop=False)
        return mm

    def step(T, s, t, has):
        after2, after, this, before, _ = has
        if isinstance(t, int) and t == TILES - 1:
            pe.wait_ge(k.xT_ready, first + TILES)
            quantise_tensor(pe, k, 0)
        if isinstance(t, int) and t == TILES:
            quantise_tensor(pe, k, 1)
        if this:
            wait_apart(pe, k, k.qT_ready, T + 1)
            pe.wait_ge(k.kT_ready, T + 1)
            scores_tensor(pe, k, s)
        if after:
            front(T + 1, 1 - s, before)
        if before:
            pe.wait_ge(k.oT_ready, T)
            pe.wait_ge(k.updated, T - 1)
            rows(range(0, 2))
        if this:
            pe.wait_ge(k.prob_ready, T + 1)
            pe.wait_ge(k.v_ready, T + 2 if after else T + 1)
            for h in range(PAIRS):
                mm = pe.transpose(k.w2[:, h * P:(h + 1) * P],
                                  k.prob[:, s, 2 * h:2 * h + 2, :].rearrange("p a m -> p (a m)"), k.ident[:, :])
            mm.then_inc(k.pT_psum, 1)
        if before:
            rows(range(2, 6))
        if this:
            wait_apart(pe, k, k.pT_ready, T + 1)
            pe.wait_ge(k.qT_ready, T + 2 if after else T + 1)
            for n in range(PAIRS):
                for p in range(2):
                    h = (n + 4 * p) % PAIRS
                    for b in range(2):
                        r = slice(64 * p, 64 * p + 64)
                        mm = pe.matmul(k.w0[r, h * P + 64 * b:h * P + 64 * b + 64],
                                       k.v2[r, s, b, 64 * h:64 * h + 64], k.probT[r, h, 64 * b:64 * b + 64],
                                       start=True, stop=True)
            mm.then_inc(k.o_psum, 1)
        if after2:
            turn_x(T + 2, s)
        if before:
            rows(range(6, PAIRS))
            pe.matmul(k.py[:, 0:P], k.ones[0:1, :], k.a_to1[0:1, :], start=False, stop=True).then_inc(k.y_psum, 1)

    turn_x(first, 0)
    turn_x(first + 1, 1)
    pe.wait_ge(k.loaded, 16 * N_URGENT)
    front(first, 0, False)
    short_steps(pe, first, step)


def wait_apart(eng, k, s, value):
    if not isinstance(value, int):
        eng.to_reg(value)
    eng.wait_ge(k.consts, 5)
    eng.wait_ge(s, value)


def link(dve, k, instruction):
    k.links += 1
    instruction.then_inc(k.vector_link, 1)
    dve.wait_ge(k.vector_link, k.links)


def scores_tensor(pe, k, s):
    for h in range(PAIRS):
        for p in range(2):
            for b in range(2):
                r = slice(64 * p, 64 * p + 64)
                c = slice(64 * b, 64 * b + 64)
                mm = pe.matmul(k.w1[c, 512 * p + 64 * h:512 * p + 64 * h + 64], k.qT[r, s, h, c],
                               k.kT[r, s, h, c], start=True, stop=True)
    mm.then_inc(k.s_psum, 1)


def cross0_scalar(act, k, first):
    def turned_x(T, s):
        act.wait_ge(k.xT_psum, T + 1)
        act.copy(k.xT[:, s, :], k.pt[:, 0:P]).then_inc(k.xT_ready, 1)

    def fill(T, s):
        act.wait_ge(k.k_psum, T + 1)
        act.copy(k.kT[:, s, :, :], k.w1[:, :]).then_inc(k.kT_ready, 1)
        act.wait_ge(k.v_psum, T + 1)
        act.copy(k.v2[:, s, :, :], k.w2[:, :]).then_inc(k.v_ready, 1)

    def step(T, s, t, has):
        after2, after, this, _, _ = has
        if this:
            exp_scalar(act, k, T, s, 0.125)
        if after:
            fill(T + 1, 1 - s)
        if this:
            act.wait_ge(k.pT_psum, T + 1)
            act.wait_ge(k.o_psum, T)
            act.copy(k.probT[:, :, :], k.w2[:, :]).then_inc(k.pT_ready, 1)
        if after2:
            turned_x(T + 2, s)

    turned_x(first, 0)
    turned_x(first + 1, 1)
    fill(first, 0)
    short_steps(act, first, step)



HALVES = [slice(0, HEADS // 2), slice(HEADS // 2, HEADS)]


def exp_scalar(act, k, T, s, scale):
    for heads, shifted, ready in zip(HALVES, (k.low_shifted, k.shifted), (k.low_exp, k.exp_ready)):
        act.wait_ge(shifted, T + 1)
        act.activation(k.prob[:, s, heads, :], k.logit[:, s, heads, :], ACT.Exp, scale=scale).then_inc(ready, 1)


def softmax_shift_vector(dve, k, T, s, logits):
    dve.tensor_reduce(by_pair(k.top[:, s, :]), logits, AX.X, ALU.max).then_inc(k.top_ready, 1)
    dve.wait_ge(k.top_ready, T + 1)
    for i, (heads, shifted) in enumerate(zip(HALVES, (k.low_shifted, k.shifted))):
        dve.tensor_tensor(by_pair(k.logit[:, s, heads, :]), logits[:, 4 * i:4 * i + 4, :, :],
                          by_pair(k.top[:, s, heads])[:, :, :, None].broadcast_to([P, PAIRS // 2, 2, SEQ]),
                          ALU.subtract).then_inc(shifted, 1)


def softmax_sum_vector(dve, k, T, s):
    for heads, ready in zip(HALVES, (k.low_exp, k.exp_ready)):
        dve.wait_ge(ready, T + 1)
        last = dve.tensor_reduce(k.den[:, s, heads], k.prob[:, s, heads, :], AX.X, ALU.add)
    last.then_inc(k.den_ready, 1)
    dve.wait_ge(k.den_ready, T + 1)
    dve.reciprocal(k.rden[:, s, :], k.den[:, s, :]).then_inc(k.rden_ready, 1)


def by_pair(ap):
    return ap.rearrange("p (h a) m -> p h a m" if len(ap.shape) == 3 else "p (h a) -> p h a", a=2)


def softmax_scale_gpsimd(pool, k, T, s):
    pool.wait_ge(k.rden_ready, T + 1)
    flat = k.prob[:, s, :, :]
    pool.tensor_tensor(flat, flat, k.rden[:, s, :, None].broadcast_to([P, HEADS, SEQ]),
                       ALU.mult).then_inc(k.prob_ready, 1)


def stats_vector(dve, k, n, T, s, rows):
    dve.bn_stats(n.stats[:, s, :], rows).then_inc(n.stat, 1)
    wait_apart(dve, k, n.stat, T + 1)
    dve.bn_aggr(n.means[:, s, :], n.stats[:, s, :]).then_inc(n.mv, 1)


def normalise_vector(dve, k, n, T, s, rows, to):
    dve.wait_ge(n.rstd, T + 1)
    return dve.tensor_scalar(to, rows, n.means[:, s, 0:1], n.roots[:, s, :], ALU.subtract, ALU.mult)


def rstd_gpsimd(pool, k, n, T, s):
    pool.wait_ge(n.mv, T + 1)
    pool.tensor_tensor(n.roots[:, s, :], n.means[:, s, 1:2], k.eps[:, 0:1], ALU.add).then_inc(n.eps, 1)
    pool.wait_ge(n.eps, T + 1)
    pool.tensor_tensor(n.roots[:, s, :], n.roots[:, s, :], k.power[:, 0:1], ALU.pow).then_inc(n.rstd, 1)


def cross0_vector(dve, k, first):
    def stats(T, s, t):
        stats_vector(dve, k, k.norm, T, s, tile(k.x, t))

    def normalise(T, s, t, before):
        if before:
            dve.wait_ge(k.xT_psum, T - 1)
        normalise_vector(dve, k, k.norm, T, s, tile(k.x, t), k.normed[:, s, :]).then_inc(k.norm.normed, 1)

    def q_bias(T, s):
        dve.wait_ge(k.q_psum, T + 1)
        dve.tensor_tensor(k.qT[:, s, :, :], k.w0[:, :].rearrange("p (h n) -> p h n", n=P),
                          k.a_lo[:, :, None].broadcast_to([P, PAIRS, P]), ALU.add).then_inc(k.qT_ready, 1)

    def step(T, s, t, has):
        after2, after, this, before, before2 = has
        if this:
            dve.wait_ge(k.s_psum, T + 1)
            logits = by_pair(k.logit[:, s, :, :])
            dve.tensor_tensor(logits.rearrange("p h a m -> p a h m"),
                              k.w1[:, :].rearrange("p (a h m) -> p a h m", a=2, m=SEQ),
                              k.a_mask[:, None, None, :].broadcast_to([P, 2, PAIRS, SEQ]), ALU.add).then_inc(k.masked, 1)
            dve.wait_ge(k.masked, T + 1)
            softmax_shift_vector(dve, k, T, s, logits)
        if before2:
            dve.wait_ge(k.y_psum, T - 1)
            dve.tensor_tensor(tile(k.x, t - 2), tile(k.x, t - 2), k.py[:, 0:P], ALU.add).then_inc(k.updated, 1)
        if this:
            softmax_sum_vector(dve, k, T, s)
        if before2:
            wait_apart(dve, k, k.updated, T - 1)
            stats_vector(dve, k, k.fresh, T - 2, s, tile(k.x, t - 2))
        if after2:
            stats(T + 2, s, t + 2)
        if after:
            q_bias(T + 1, 1 - s)
        if after2:
            normalise(T + 2, s, t + 2, True)
        if before2:
            normalise_vector(dve, k, k.fresh, T - 2, s, tile(k.x, t - 2), tile(k.y, t - 2)).then_inc(k.fresh.normed, 1)
        if this:
            dve.wait_ge(k.o_psum, T + 1)
            dve.wait_ge(k.y_psum, T)
            dve.tensor_tensor(k.oT[:, :, :], k.w0[:, :].rearrange("p (h n) -> p h n", n=P),
                              k.a_to0[:, :, None].broadcast_to([P, PAIRS, P]), ALU.add).then_inc(k.oT_ready, 1)
        if isinstance(t, int) and t == 1:
            dve.wait_ge(k.loaded_later, 16 * N_LATER)
            dve.tensor_copy(k.band16[:, :], k.band[:, :]).then_inc(k.band_ready, 1)
            quantise_largest(dve, k)
        if isinstance(t, int) and t == TILES - 1:
            fp8_weight_vector(dve, k)
            quantise_spread(dve, k)
        if isinstance(t, int) and t == TILES:
            quantise_weights(dve, k)

    for i in range(2):
        stats(first + i, i, i)
        normalise(first + i, i, i, False)
    dve.wait_ge(k.loaded, 16 * N_URGENT)
    q_bias(first, 0)
    short_steps(dve, first, step)


def cross0_gpsimd(pool, k, first):
    def step(T, s, t, has):
        after2, _, this, _, before2 = has
        if this:
            softmax_scale_gpsimd(pool, k, T, s)
        if after2:
            rstd_gpsimd(pool, k, k.norm, T + 2, s)
        if before2:
            rstd_gpsimd(pool, k, k.fresh, T - 2, s)

    rstd_gpsimd(pool, k, k.norm, first, 0)
    rstd_gpsimd(pool, k, k.norm, first + 1, 1)
    short_steps(pool, first, step)




BEHIND = 3


def local_steps(eng, first, step):
    def single(i):
        step(first + i, i % 2, i, [0 <= i + n < TILES for n in (2, 1, 0, -1, -2, -3)])

    every = [True] * 6
    for i in range(3):
        single(i)
    with eng.Fori(3, TILES - 4, 2) as t:
        step(first + t, 1, t, every)
        step(first + t + 1, 0, t + 1, every)
    for i in range(TILES - 3, TILES + BEHIND):
        single(i)


def last_step(t, n):
    return isinstance(t, int) and t == TILES + n


def local_tensor(pe, k, first, quad):
    def step(T, s, t, has):
        _, after, this, before, before2, before3 = has
        if last_step(t, -1):
            pe.wait_ge(k.half_shifted, first + TILES)
            quad.shift(0)
        if last_step(t, 1):
            quad.shift(1)
            quad.hidden(0, (0,))
        if this:
            pe.wait_ge(k.half_shifted, T + 1)
            if before2:
                pe.wait_ge(k.qT_ready, T - 1)
            elif before:
                pe.wait_ge(k.q_turned, T)
            for c in range(2):
                mm = pe.matmul(k.w0[:, 512 * c:512 * c + 512], k.sT[:, s, :], k.b_wqkv[:, 512 * c:512 * c + 512],
                               start=True, stop=True)
            mm.then_inc(k.q_psum, 1)
        if before:
            if before3:
                wait_apart(pe, k, k.oT_ready, T - 2)
            elif before2:
                wait_apart(pe, k, k.v_ready, T - 1)
            for b in range(2):
                for p in range(2):
                    mm = pe.matmul(k.w2[64 * p:64 * p + 64, 512 * b:512 * b + 512],
                                   k.sT[:, 1 - s, 64 * b:64 * b + 64], k.b_wqkv[:, 2048 + 512 * p:2560 + 512 * p],
                                   start=True, stop=True)
            mm.then_inc(k.v_psum, 1)
        if after:
            turn_y(T + 1, 1 - s)
        if this:
            if before2:
                pe.wait_ge(k.shifted, T - 1)
            elif before:
                pe.wait_ge(k.k_turned, T)
            for c in range(2):
                mm = pe.matmul(k.w1[:, 512 * c:512 * c + 512], k.sT[:, s, :],
                               k.b_wqkv[:, 1024 + 512 * c:1536 + 512 * c], start=True, stop=True)
            mm.then_inc(k.k_psum, 1)
        if before3:
            pe.wait_ge(k.oT_ready, T - 2)
            pe.wait_ge(k.updated, T - 3)
            rows(range(PAIRS // 2))
        if before:
            if this:
                pe.wait_ge(k.q_turned, T + 1)
            else:
                pe.wait_ge(k.qT_ready, T - 1)
            pe.wait_ge(k.q_final, T)
            for h in range(PAIRS):
                mm = pe.transpose(k.w0[:, h * P:(h + 1) * P],
                                  k.straights[1 - s][:, 0, 2 * h:2 * h + 2, :].rearrange("p a d -> p (a d)"), k.ident[:, :])
            mm.then_inc(k.qT_psum, 1)
        if before2:
            if before:
                pe.wait_ge(k.v_ready, T)
            pe.wait_ge(k.prob_ready, T - 1)
            for h in range(PAIRS):
                mm = pe.transpose(k.w2[:, h * P:(h + 1) * P],
                                  k.prob[:, s, 2 * h:2 * h + 2, :].rearrange("p a m -> p (a m)"), k.ident[:, :])
            mm.then_inc(k.pT_psum, 1)
        if before:
            if this:
                pe.wait_ge(k.k_turned, T + 1)
            else:
                pe.wait_ge(k.shifted, T - 1)
            pe.wait_ge(k.k_final, T)
            for h in range(PAIRS):
                mm = pe.transpose(k.w1[:, h * P:(h + 1) * P],
                                  k.straights[1 - s][:, 1, 2 * h:2 * h + 2, :].rearrange("p a d -> p (a d)"), k.ident[:, :])
            mm.then_inc(k.kT_psum, 1)
        if last_step(t, 1):
            quad.hidden(0, (1,))
        if before2:
            wait_apart(pe, k, k.pT_ready, T - 1)
            for n in range(PAIRS):
                for p in range(2):
                    h = (n + 4 * p) % PAIRS
                    for b in range(2):
                        r = slice(64 * p, 64 * p + 64)
                        mm = pe.matmul(k.w2[r, h * P + 64 * b:h * P + 64 * b + 64],
                                       k.v2[r, s, b, 64 * h:64 * h + 64], k.probT[r, h, 64 * b:64 * b + 64],
                                       start=True, stop=True)
            mm.then_inc(k.o_psum, 1)
        if before3:
            rows(range(PAIRS // 2, PAIRS)).then_inc(k.y_psum, 1)
        if before:
            wait_apart(pe, k, k.kT_ready, T)
            pe.wait_ge(k.qT_ready, T)
            for p in range(2):
                r = slice(64 * p, 64 * p + 64)
                for b in range(2):
                    pe.matmul(k.w1[64 * b:64 * b + 64, 512 * p:512 * p + 512], k.ident16[r, r],
                              k.band16[r, None, :].broadcast_to([SEQ, PAIRS, SEQ]), start=True, stop=False,
                              skip_group_check=True)
            for h in range(PAIRS):
                for p in range(2):
                    for b in range(2):
                        r = slice(64 * p, 64 * p + 64)
                        c = slice(64 * b, 64 * b + 64)
                        mm = pe.matmul(k.w1[c, 512 * p + 64 * h:512 * p + 64 * h + 64], k.qT[r, 1 - s, h, c],
                                       k.kT[r, 1 - s, h, c], start=False, stop=True, skip_group_check=True)
            mm.then_inc(k.s_psum, 1)
        if last_step(t, 0):
            quad.turn(0)

    def rows(pairs):
        for h in pairs:
            mm = pe.matmul(k.py[:, 0:P], k.oT[:, h, :], k.b_wo[:, h, :], start=(h == 0), stop=(h == PAIRS - 1))
        return mm

    def turn_y(T, s):
        pe.wait_ge(k.y_copied, T + 1)
        pe.wait_ge(k.half_shifted, T)
        pe.transpose(k.pt[:, 0:P], k.ytile[:, s, :], k.ident[:, :]).then_inc(k.xT_psum, 1)

    pe.wait_ge(k.band_ready, 1)
    pe.wait_ge(k.b_loaded, B_LOADS * (first - PHANTOM))
    pe.wait_ge(k.quant.done, 1)
    turn_y(first, 0)
    local_steps(pe, first, step)


def local_scalar(act, k, first, qfirst, quad):
    def copy_y(T, s, t):
        act.copy(k.ytile[:, s, :], tile(k.y, t)).then_inc(k.y_copied, 1)

    def shift(T, s):
        act.wait_ge(k.xT_psum, T + 1)
        act.copy(k.sT[0:64, s, :], k.pt[0:64, 0:P])
        act.copy(k.sT[64:P, s, :].rearrange("p (b n) -> p b n", b=2)[:, :, 1:SEQ],
                 k.pt[64:P, 0:P].rearrange("p (b n) -> p b n", b=2)[:, :, 0:SEQ - 1]).then_inc(k.half_shifted, 1)

    def step(T, s, t, has):
        after2, after, this, before, before2, _ = has
        if last_step(t, -1):
            quad.fetch(0)
        if before2:
            exp_scalar(act, k, T - 2, s, 8.0)
        if last_step(t, 1):
            quad.fetch(1)
        if this:
            act.wait_ge(k.q_psum, T + 1)
            act.wait_ge(k.q_norm2, T)
            act.activation(k.sq[:, 0, :, :], k.w0[:, :], ACT.Square).then_inc(k.q_squared, 1)
        if this:
            act.wait_ge(k.k_psum, T + 1)
            act.wait_ge(k.k_norm2, T)
            act.activation(k.sq[:, 1, :, :], k.w1[:, :], ACT.Square).then_inc(k.k_squared, 1)
        if before:
            act.wait_ge(k.v_psum, T)
            act.copy(k.v2[:, 1 - s, :, :], k.w2[:, :]).then_inc(k.v_ready, 1)
        if before:
            act.wait_ge(k.qT_psum, T)
            act.copy(k.qT[:, 1 - s, :, :], k.w0[:, :]).then_inc(k.qT_ready, 1)
        if before2:
            act.wait_ge(k.pT_psum, T - 1)
            act.copy(k.probT[:, :, :], k.w2[:, :]).then_inc(k.pT_ready, 1)
        if before:
            act.wait_ge(k.kT_psum, T)
            act.copy(k.kT[:, 1 - s, :, :], k.w1[:, :]).then_inc(k.kT_ready, 1)
        if after:
            shift(T + 1, 1 - s)
        if isinstance(t, int) and t == 0:
            act.wait_ge(k.fresh.normed, PHANTOM + TILES)
            act.wait_ge(k.y_done, qfirst)
        if after2:
            copy_y(T + 2, s, t + 2)
        if before2:
            act.wait_ge(k.o_psum, T - 1)
            act.wait_ge(k.y_psum, T - 2)
            act.copy(k.oT[:, :, :], k.w2[:, :]).then_inc(k.oT_ready, 1)

    act.wait_ge(k.fresh.normed, PHANTOM + 2)
    act.wait_ge(k.y_done, qfirst - 1)
    copy_y(first, 0, 0)
    copy_y(first + 1, 1, 1)
    shift(first, 0)
    local_steps(act, first, step)


NEWTON = 11


def local_vector(dve, k, first, quad):
    def rotate(T, s, i, w, turned, squared, transposed, added):
        dve.wait_ge(squared, T + 1)
        dve.wait_ge(transposed, T - 1)
        heads = w[:, :].rearrange("p (h d) -> p h d", d=HD)
        dve.tensor_tensor(k.straights[s][:, i, :, :], heads,
                          k.rot[:, 2 * i, None, :].broadcast_to([P, HEADS, HD]), ALU.mult)
        dve.wait_ge(added, T)
        half = HD // 2
        for to, of in ((slice(0, half), slice(half, HD)), (slice(half, HD), slice(0, half))):
            last = dve.tensor_tensor(k.turned[:, i, :, to], heads[:, :, of],
                                     k.rot[:, 2 * i + 1, None, to].broadcast_to([P, HEADS, half]), ALU.mult)
        last.then_inc(turned, 1)

    def reciprocal_norms(T, s):
        m, u = k.norm2[:, :, :], k.newton[:, :, :]
        r = k.rnorms[:, s, :, :]
        dve.wait_ge(k.q_norm2, T + 1)
        dve.wait_ge(k.k_norm2, T + 1)
        dve.tensor_scalar(m, m, 1e-24, None, ALU.max).then_inc(k.newton_step, 1)
        done = T * NEWTON + 1
        dve.wait_ge(k.newton_step, done)
        dve.tensor_scalar(r.bitcast(I32), m.bitcast(I32), -0.5, float(0x5f3759df), ALU.mult,
                          ALU.add).then_inc(k.newton_step, 1)
        for n in range(3):
            dve.wait_ge(k.newton_step, T * NEWTON + (2 + 3 * n))
            dve.tensor_tensor(u, r, r, ALU.mult).then_inc(k.newton_step, 1)
            dve.wait_ge(k.newton_step, T * NEWTON + (3 + 3 * n))
            dve.scalar_tensor_tensor(out=u, in0=u, scalar=-0.5, in1=m, op0=ALU.mult,
                                     op1=ALU.mult).then_inc(k.newton_step, 1)
            dve.wait_ge(k.newton_step, T * NEWTON + (4 + 3 * n))
            dve.scalar_tensor_tensor(out=r, in0=u, scalar=1.5, in1=r, op0=ALU.add,
                                     op1=ALU.mult).then_inc(k.newton_step, 1)

    def step(T, s, t, has):
        _, _, this, _, before2, before3 = has
        if before2:
            dve.wait_ge(k.s_psum, T - 1)
            softmax_shift_vector(dve, k, T - 2, s, k.w1[:, :].rearrange("p (a h m) -> p h a m", a=2, m=SEQ))
            softmax_sum_vector(dve, k, T - 2, s)
        if this:
            rotate(T, s, 0, k.w0, k.q_turned, k.q_squared, k.qT_psum, k.q_added)
            rotate(T, s, 1, k.w1, k.k_turned, k.k_squared, k.kT_psum, k.k_added)
            for i, norm2 in enumerate((k.q_norm2, k.k_norm2)):
                dve.tensor_reduce(k.norm2[:, i, :], k.sq[:, i, :, :], AX.X, ALU.add).then_inc(norm2, 1)
            reciprocal_norms(T, s)
        if last_step(t, -1):
            quad.stats(0)
        if last_step(t, 0):
            quad.normalise(0)
        if last_step(t, 1):
            quad.stats(1)
        if before3:
            dve.wait_ge(k.y_psum, T - 2)
            dve.tensor_tensor(tile(k.y, t - 3), tile(k.y, t - 3), k.py[:, 0:P], ALU.add).then_inc(k.updated, 1)
        if last_step(t, 0):
            quad.turned(0)

    dve.wait_ge(k.b_loaded, B_LOADS * (first - PHANTOM))
    dve.tensor_tensor(k.rot[:, :, :].rearrange("p a d -> p (a d)"), k.rope[:, :], k.b_scales[:, :],
                      ALU.mult).then_inc(k.rot_ready, 1)
    dve.wait_ge(k.rot_ready, (first - PHANTOM) // TILES)
    local_steps(dve, first, step)


def local_gpsimd(pool, k, first, quad):
    def norm(T, s, i, added, final):
        pool.wait_ge(added, T + 1)
        pool.tensor_tensor(k.straights[s][:, i, :, :], k.straights[s][:, i, :, :],
                           k.rnorms[:, s, i, :, None].broadcast_to([P, HEADS, HD]), ALU.mult).then_inc(final, 1)

    def add(T, s, i, turned, added):
        pool.wait_ge(turned, T + 1)
        pool.tensor_tensor(k.straights[s][:, i, :, :], k.straights[s][:, i, :, :], k.turned[:, i, :, :],
                           ALU.add).then_inc(added, 1)

    def step(T, s, t, has):
        _, _, this, before, before2, _ = has
        if before:
            pool.wait_ge(k.newton_step, T * NEWTON)
            norm(T - 1, 1 - s, 0, k.q_added, k.q_final)
            norm(T - 1, 1 - s, 1, k.k_added, k.k_final)
        if last_step(t, 0):
            quad.rstd(0)
        if before2:
            softmax_scale_gpsimd(pool, k, T - 2, s)
        if this:
            add(T, s, 0, k.q_turned, k.q_added)
            add(T, s, 1, k.k_turned, k.k_added)

    local_steps(pool, first, step)



QUADS = TILES // 4



class GatedTensor:
    def __init__(self, pe, k, first, qfirst):
        self.pe, self.k, self.first, self.qfirst = pe, k, first, qfirst

    def shift(self, q):
        pe, k = self.pe, self.k
        pe.wait_ge(k.updated, self.first + (4 * q + 4))
        pe.wait_ge(k.xnT_ready, self.qfirst + q)
        pe.matmul(k.pt[:, 0:256].rearrange("p (j d) -> p j d", j=4), k.shift[:, :], k.y[:, 4 * q:4 * q + 4, 64:P],
                  start=True, stop=True).then_inc(k.sh_psum, 1)

    def turn(self, q):
        pe, k, Q = self.pe, self.k, self.qfirst + q
        pe.wait_ge(k.quad_normed, Q + 1)
        pe.wait_ge(k.xs_high, Q + 1)
        for j in range(4):
            mm = pe.transpose(k.pt[:, j * P:(j + 1) * P], k.xs[:, q % 2, j, :], k.ident[:, :])
        mm.then_inc(k.quad_turned, 1)

    def hidden(self, q, chunks):
        pe, k, Q = self.pe, self.k, self.qfirst + q
        for c in chunks:
            at, n = CHUNKS[c]
            w = (k.w0, k.w1, k.w2)[c]
            if c == 0:
                pe.wait_ge(k.xnT_ready, Q + 1)
                pe.wait_ge(k.c_loaded, C_LOADS * (self.first - PHANTOM))
            if q == 0:
                pe.wait_ge((k.qT_ready, k.shifted, k.oT_ready)[c], self.first + TILES)
            pe.wait_ge(k.hid_ready, 3 * Q + (c - 2))
            pe.matmul(w[0:n, 0:512], k.c_w1[:, HID + at:HID + at + n], k.xnT[:, q % 2, :], start=True, stop=True)
            pe.matmul(w[0:n, 512:1024], k.c_w1[:, at:at + n], k.xnT[:, q % 2, :],
                      start=True, stop=True).then_inc(k.hid_psum, 1)

    def output(self, q):
        pe, k, Q = self.pe, self.k, self.qfirst + q
        if q == 0:
            pe.wait_ge(k.updated, self.first + TILES)
        pe.wait_ge(k.y_done, Q)
        pe.wait_ge(k.hid_ready, 3 * Q + 3)
        for j in range(4):
            for c, (at, n) in enumerate(CHUNKS):
                n += c == 2
                mm = pe.matmul(k.py[:, j * P:(j + 1) * P], k.hid[0:n, c, j * P:(j + 1) * P], k.c_w2[0:n, c, :],
                               start=(c == 0), stop=(c == 2))
        mm.then_inc(k.out_psum, 1)

    def rest(self):
        for q in range(QUADS):
            if q:
                self.hidden(q, (1,))
            if q + 1 < QUADS:
                self.turn(q + 1)
            self.hidden(q, (2,))
            if q + 2 < QUADS:
                self.shift(q + 2)
            if q + 1 < QUADS:
                self.hidden(q + 1, (0,))
            self.output(q)


class GatedScalar:
    def __init__(self, act, k, first, qfirst):
        self.act, self.k, self.first, self.qfirst = act, k, first, qfirst

    def fetch(self, q):
        act, k, Q, s = self.act, self.k, self.qfirst + q, q % 2
        act.wait_ge(k.updated, self.first + (4 * q + 4))
        act.wait_ge(k.quad_turned, Q - 1)
        act.copy(k.xs[:, s, :, 0:64], k.y[:, 4 * q:4 * q + 4, 0:64]).then_inc(k.xs_low, 1)
        act.wait_ge(k.sh_psum, Q + 1)
        act.copy(k.xs[:, s, :, 64:P], k.pt[:, 0:256].rearrange("p (j d) -> p j d", j=4)).then_inc(k.xs_high, 1)

    def rest(self):
        act, k = self.act, self.k
        act.wait_ge(k.c_loaded, C_LOADS * (self.first - PHANTOM))
        for q in range(QUADS):
            Q = self.qfirst + q
            for c, (at, n) in enumerate(CHUNKS):
                act.wait_ge(k.hid_psum, 3 * Q + (c + 1))
                act.wait_ge(k.hid_ready, 3 * Q + (c - 2))
                act.activation(k.gate[0:n, c, :], (k.w0, k.w1, k.w2)[c][0:n, 0:512], ACT.Gelu,
                               bias=k.c_cols[0:n, 5 + c:6 + c]).then_inc(k.gated, 1)
            if q + 2 < QUADS:
                self.fetch(q + 2)


class GatedVector:
    def __init__(self, dve, k, first, qfirst):
        self.dve, self.k, self.first, self.qfirst = dve, k, first, qfirst

    def stats(self, q):
        dve, k, Q, s = self.dve, self.k, self.qfirst + q, q % 2
        dve.wait_ge(k.xs_low, Q + 1)
        dve.wait_ge(k.xs_high, Q + 1)
        for j in range(4):
            last = dve.bn_stats(k.stats4[:, 4 * s + j, :], k.xs[:, s, j, :])
        last.then_inc(k.quad_stat, 1)
        wait_apart(dve, k, k.quad_stat, Q + 1)
        for j in range(4):
            last = dve.bn_aggr(k.mv4[:, 4 * s + j, :], k.stats4[:, 4 * s + j, :])
        last.then_inc(k.quad_mv, 1)

    def normalise(self, q):
        dve, k, Q, s = self.dve, self.k, self.qfirst + q, q % 2
        dve.wait_ge(k.quad_rstd, Q + 1)
        for j in range(4):
            last = dve.tensor_scalar(k.xs[:, s, j, :], k.xs[:, s, j, :], k.mv4[:, 4 * s + j, 0:1],
                                     k.rstd4[:, 4 * s + j:4 * s + j + 1], ALU.subtract, ALU.mult)
        last.then_inc(k.quad_normed, 1)

    def turned(self, q):
        dve, k, Q = self.dve, self.k, self.qfirst + q
        if q == 0:
            dve.wait_ge(k.c_loaded, C_LOADS * (self.first - PHANTOM))
        dve.wait_ge(k.quad_turned, Q + 1)
        dve.tensor_scalar(k.xnT[:, q % 2, :], k.pt[:, :], k.c_cols[:, 0:1], k.c_cols[:, 1:2],
                          ALU.mult, ALU.add).then_inc(k.xnT_ready, 1)

    def rest(self):
        dve, k = self.dve, self.k
        for q in range(QUADS):
            Q = self.qfirst + q
            if q + 1 < QUADS:
                self.normalise(q + 1)
            for c, (at, n) in enumerate(CHUNKS):
                dve.wait_ge(k.gated, 3 * Q + (c + 1))
                dve.wait_ge(k.out_psum, Q)
                dve.scalar_tensor_tensor(out=k.hid[0:n, c, :], in0=(k.w0, k.w1, k.w2)[c][0:n, 512:1024],
                                         scalar=k.c_cols[0:n, 2 + c:3 + c], in1=k.gate[0:n, c, :],
                                         op0=ALU.add, op1=ALU.mult).then_inc(k.hid_ready, 1)
                if c == 0 and q + 1 < QUADS:
                    self.turned(q + 1)
            if q + 2 < QUADS:
                self.stats(q + 2)
            dve.wait_ge(k.out_psum, Q + 1)
            rows = k.y[:, 4 * q:4 * q + 4, :].rearrange("p j n -> p (j n)")
            dve.tensor_tensor(rows, rows, k.py[:, :], ALU.add).then_inc(k.y_done, 1)


class GatedGpsimd:
    def __init__(self, pool, k, qfirst):
        self.pool, self.k, self.qfirst = pool, k, qfirst

    def rstd(self, q):
        pool, k, Q, s = self.pool, self.k, self.qfirst + q, q % 2
        r = k.rstd4[:, 4 * s:4 * s + 4]
        pool.wait_ge(k.quad_mv, Q + 1)
        pool.tensor_tensor(r, k.mv4[:, 4 * s:4 * s + 4, 1], k.eps[:, 0:4], ALU.add).then_inc(k.quad_eps, 1)
        pool.wait_ge(k.quad_eps, Q + 1)
        pool.tensor_tensor(r, r, k.power[:, 0:4], ALU.pow).then_inc(k.quad_rstd, 1)

    def rest(self):
        for q in range(1, QUADS):
            self.rstd(q)




def small_tensor(pe, k, n, before=None):
    d, first = k.d, PHANTOM + TILES * n

    def turn_x(T, s):
        pe.wait_ge(k.norm.normed, T + (TILES + 1))
        pe.wait_ge(d.v_ready, T)
        pe.transpose(k.pt[:, 0:P], k.normed[:, s, :], k.ident[:, :]).then_inc(d.xT_psum, 1)

    def front(T, s, ahead=2):
        pe.wait_ge(k.ctx_loaded[s], 8 * (T - s - first) + (16 + 128 * (n + 1)))
        if ahead:
            pe.wait_ge(d.oT_ready, T - ahead)
        pe.matmul(k.w0[:, 512:512 + P], k.s_w[:, n, 1, :], k.ctxT[:, s, :], start=True, stop=True).then_inc(d.k_psum, 1)
        pe.wait_ge(d.xT_ready, T + 1)
        if ahead:
            pe.wait_ge(d.rows, T - ahead)
        pe.matmul(k.w0[:, 0:P], k.s_w[:, n, 0, :], k.xT[:, s, :], start=True, stop=True).then_inc(d.q_psum, 1)

    def values(T, s):
        for p in range(2):
            for b in range(2):
                mm = pe.matmul(k.pt[64 * p:64 * p + 64, 64 * b:64 * b + 64], k.ctxT[:, s, 64 * b:64 * b + 64],
                               k.s_w[:, n, 2, 64 * p:64 * p + 64], start=True, stop=True)
        mm.then_inc(d.v_psum, 1)

    def scores(T, s):
        if not isinstance(T, int):
            pe.to_reg(T)
        wait_apart(pe, k, d.q_ready, T + 1)
        pe.wait_ge(d.k8_ready, T + 1)
        pe.wait_ge(d.shifted, T)
        for b in range(2):
            for g in range(2):
                r = slice(64 * g, 64 * g + 64)
                mm = pe.matmul(k.w1[64 * b:64 * b + 64, 512 * g:512 * g + 512], k.s_qT[r, s, 64 * b:64 * b + 64],
                               k.s_k8[r, s, :, 64 * b:64 * b + 64], start=True, stop=True)
        mm.then_inc(d.s_psum, 1)

    def turn(T, s):
        pe.wait_ge(d.exp, T + 1)
        pe.wait_ge(d.pT_ready, T)
        for h in range(PAIRS):
            mm = pe.transpose(k.w2[:, h * P:(h + 1) * P],
                              k.prob[:, s, 2 * h:2 * h + 2, :].rearrange("p a m -> p (a m)"), k.ident[:, :])
        mm.then_inc(d.pT_psum, 1)

    def attend(T, s, ahead):
        if not isinstance(T, int):
            pe.to_reg(T + 1 + ahead)
        wait_apart(pe, k, d.pT_ready, T + 1)
        pe.wait_ge(d.q_ready, T + 1 + ahead)
        for h in range(PAIRS):
            for b in range(2):
                mm = pe.matmul(k.w0[64 * b:64 * b + 64, 16 * h:16 * h + 16], k.probT[:, h, 64 * b:64 * b + 64],
                               k.s_v[:, s, b, h, :, :].rearrange("p a d -> p (a d)"), start=True, stop=True)
        mm.then_inc(d.o_psum, 1)

    def turn_rows(T, ahead):
        pe.wait_ge(d.rows, T + 1)
        pe.wait_ge(d.k8_ready, T + 1 + ahead)
        pe.transpose(k.w0[:, 512:512 + P], k.s_rows[:, :], k.ident[:, :]).then_inc(d.o_turned, 1)

    def rows(T):
        pe.wait_ge(d.oT_ready, T + 1)
        pe.wait_ge(d.updated, T)
        pe.matmul(k.py[:, 0:P], k.s_oT[:, :], k.s_w[:, n, 3, :], start=True, stop=False)
        pe.matmul(k.py[:, 0:P], k.ones[0:1, :], k.s_bo[0:1, n, :], start=False, stop=True).then_inc(d.y_psum, 1)

    def step(T, s, t, has):
        _, after, this, before, before2 = has
        if after:
            turn_x(T + 1, 1 - s)
        if this:
            scores(T, s)
        if before2:
            rows(T - 2)
        if before:
            turn(T - 1, 1 - s)
        if after:
            front(T + 1, 1 - s)
            values(T + 1, 1 - s)
        if before:
            attend(T - 1, 1 - s, 2 if after else 1 if this else 0)
            turn_rows(T - 1, 2 if after else 1 if this else 0)

    turn_x(first, 0)
    front(first, 0, ahead=0)
    values(first, 0)
    if before:
        pe.wait_ge(before, 1)
    short_steps(pe, first, step)


def small_scalar(act, k, n, scale):
    d, first = k.d, PHANTOM + TILES * n

    def turned_x(T, s):
        act.wait_ge(d.xT_psum, T + 1)
        act.copy(k.xT[:, s, :], k.pt[:, 0:P]).then_inc(d.xT_ready, 1)

    def front(T, s):
        act.wait_ge(d.q_psum, T + 1)
        act.activation(k.s_qT[:, s, :], k.w0[:, 0:P], ACT.Identity, bias=k.s_cols[:, n, 0:1]).then_inc(d.q_ready, 1)

    def values(T, s, before):
        act.wait_ge(d.v_psum, T + 1)
        if before:
            act.wait_ge(d.o_psum, T - 1)
        for p in range(2):
            last = act.copy(k.s_v[64 * p:64 * p + 64, s, :, :, p, :],
                            k.pt[64 * p:64 * p + 64, 0:P].rearrange("p (b h d) -> p b h d", b=2, d=8))
        last.then_inc(d.v_ready, 1)

    def step(T, s, t, has):
        _, after, this, before, _ = has
        if after:
            turned_x(T + 1, 1 - s)
        if before:
            act.wait_ge(d.pT_psum, T)
            act.wait_ge(d.o_psum, T - 1)
            act.copy(k.probT[:, :, :], k.w2[:, :]).then_inc(d.pT_ready, 1)
        if after:
            front(T + 1, 1 - s)
        if this:
            act.wait_ge(d.shifted, T + 1)
            act.activation(k.prob[:, s, :, :], k.logit[:, s, :, :], ACT.Exp, scale=scale).then_inc(d.exp, 1)
        if after:
            values(T + 1, 1 - s, before)
        if before:
            act.wait_ge(d.o_turned, T)
            act.wait_ge(d.y_psum, T - 1)
            act.activation(k.s_oT[:, :], k.w0[:, 512:512 + P], ACT.Identity,
                           bias=k.s_cols[:, n, 2:3]).then_inc(d.oT_ready, 1)

    turned_x(first, 0)
    front(first, 0)
    values(first, 0, False)
    short_steps(act, first, step)


def small_vector(dve, k, n, before=None):
    d, first = k.d, PHANTOM + TILES * n

    def stats(T, s, t):
        stats_vector(dve, k, k.norm, T + TILES, s, tile(k.x, t))

    def normalise(T, s, t):
        dve.wait_ge(d.xT_psum, T - 1)
        normalise_vector(dve, k, k.norm, T + TILES, s, tile(k.x, t), k.normed[:, s, :]).then_inc(k.norm.normed, 1)

    def keys(T, s):
        dve.wait_ge(d.k_psum, T + 1)
        dve.scalar_tensor_tensor(out=k.s_k8[:, s, :, :], in0=k.w0[:, None, 512:512 + P].broadcast_to([P, 8, P]),
                                 scalar=k.s_cols[:, n, 1:2], in1=k.member[:, :, None].broadcast_to([P, 8, P]),
                                 op0=ALU.add, op1=ALU.mult).then_inc(d.k8_ready, 1)

    def step(T, s, t, has):
        after2, after, this, before, before2 = has
        if this:
            logits = k.w1[:, :].rearrange("p (h m) -> p h m", m=SEQ)
            dve.wait_ge(d.s_psum, T + 1)
            dve.tensor_reduce(k.top[:, s, :], logits, AX.X, ALU.max).then_inc(d.top, 1)
            dve.wait_ge(d.top, T + 1)
            dve.tensor_tensor(k.logit[:, s, :, :], logits, k.top[:, s, :, None].broadcast_to([P, HEADS, SEQ]),
                              ALU.subtract).then_inc(d.shifted, 1)
        if before:
            dve.wait_ge(d.exp, T)
            dve.tensor_reduce(k.den[:, 1 - s, :], k.prob[:, 1 - s, :, :], AX.X, ALU.add).then_inc(d.den, 1)
            dve.wait_ge(d.den, T)
            dve.reciprocal(k.rden[:, 1 - s, :], k.den[:, 1 - s, :]).then_inc(d.rden, 1)
        if after:
            keys(T + 1, 1 - s)
        if before2:
            dve.wait_ge(d.y_psum, T - 1)
            dve.tensor_tensor(tile(k.x, t - 2), tile(k.x, t - 2), k.py[:, 0:P], ALU.add).then_inc(d.updated, 1)
        if after2:
            stats(T + 2, s, t + 2)
        if before:
            dve.wait_ge(d.o_psum, T)
            dve.wait_ge(d.rden, T)
            dve.wait_ge(d.o_turned, T - 1)
            dve.tensor_tensor(k.s_rows[:, :].rearrange("p (h d) -> p h d", d=8),
                              k.w0[:, 0:P].rearrange("p (h d) -> p h d", d=8),
                              k.rden[:, 1 - s, :, None].broadcast_to([P, HEADS, 8]), ALU.mult).then_inc(d.rows, 1)
        if before2:
            wait_apart(dve, k, d.updated, T - 1)
            stats_vector(dve, k, k.fresh, T + (TILES - 2), s, tile(k.x, t - 2))
        if after2:
            normalise(T + 2, s, t + 2)
        if before2:
            normalise_vector(dve, k, k.fresh, T + (TILES - 2), s, tile(k.x, t - 2),
                             tile(k.y, t - 2)).then_inc(k.fresh.normed, 1)

    if before:
        before(slice(0, 2))
    for i in range(2):
        stats(first + i, i, i)
        normalise(first + i, i, i)
    if before:
        before(slice(2, TILES))
    keys(first, 0)
    short_steps(dve, first, step)


def small_gpsimd(pool, k, n):
    first = PHANTOM + TILES * n

    def step(T, s, t, has):
        if has[0]:
            rstd_gpsimd(pool, k, k.norm, T + (TILES + 2), s)
        if has[4]:
            rstd_gpsimd(pool, k, k.fresh, T + (TILES - 2), s)

    rstd_gpsimd(pool, k, k.norm, first + TILES, 0)
    rstd_gpsimd(pool, k, k.norm, first + TILES + 1, 1)
    short_steps(pool, first, step)



def quantise_largest(dve, k):
    q = k.quant
    w = k.s_w[:, 2, :, :]
    dve.tensor_reduce(k.wmax[:, :], w, AX.X, ALU.max, apply_absolute_value=True).then_inc(q.wmax, 1)


def quantise_spread(dve, k):
    q = k.quant
    dve.wait_ge(q.turned, 1)
    link(dve, k, dve.tensor_reduce(k.wmaxT[:, :], k.pt[0:4, 0:P], AX.X, ALU.max))
    dve.tensor_scalar(k.wdiag[:, :], k.ident[0:4, 0:4], k.wmaxT[:, 0:1], None, ALU.mult).then_inc(q.diag, 1)


def quantise_weights(dve, k):
    q, w = k.quant, k.s_w[:, 2, :, :]
    dve.wait_ge(q.spread, 1)
    link(dve, k, dve.tensor_scalar(k.wstep[:, :], k.pt[:, P:P + 4], 1.0 / 127.0, None, ALU.mult))
    link(dve, k, dve.reciprocal(k.wrstep[:, :], k.wstep[:, :]))
    wide = (lambda c: c[:, :, None].broadcast_to([P, 4, P]))
    link(dve, k, dve.tensor_tensor(w, w, wide(k.wrstep), ALU.mult))
    link(dve, k, dve.tensor_scalar(w, w, 12582912.0, 12582912.0, ALU.add, ALU.subtract))
    link(dve, k, dve.tensor_scalar(w, w, -128.0, 127.0, ALU.max, ALU.min))
    dve.tensor_tensor(w, w, wide(k.wstep), ALU.mult).then_inc(q.done, 1)


def quantise_tensor(pe, k, n):
    if n == 0:
        pe.wait_ge(k.quant.wmax, 1)
        pe.transpose(k.pt[0:4, 0:P], k.wmax[:, :], k.ident[:, :]).then_inc(k.quant.turned, 1)
    else:
        pe.wait_ge(k.quant.diag, 1)
        pe.matmul(k.pt[:, P:P + 4], k.ones4[:, :], k.wdiag[:, :], start=True, stop=True).then_inc(k.quant.spread, 1)



def fp8_weight_vector(dve, k):
    integer = mybir.dt.int32
    link(dve, k, dve.tensor_copy(k.f_int[:, :], k.f_bytes[:, :]))
    link(dve, k, dve.tensor_scalar(k.f_mag[:, :], k.f_int[:, :], 127, None, ALU.bitwise_and))
    link(dve, k, dve.tensor_scalar(k.f_low[:, :], k.f_mag[:, :], 2.0 ** -9, 2.0 ** -6, ALU.mult, ALU.min))
    link(dve, k, dve.tensor_scalar(k.f_val[:, :].bitcast(integer), k.f_mag[:, :], 20, None, ALU.logical_shift_left))
    link(dve, k, dve.scalar_tensor_tensor(out=k.f_val[:, :], in0=k.f_val[:, :], scalar=2.0 ** 120,
                                          in1=k.f_low[:, :], op0=ALU.mult, op1=ALU.max))
    link(dve, k, dve.tensor_scalar(k.f_low[:, :], k.f_int[:, :], 128.0, -2.0, ALU.is_ge, ALU.mult))
    dve.scalar_tensor_tensor(out=k.f_w[:, :], in0=k.f_low[:, :], scalar=1.0, in1=k.f_val[:, :],
                             op0=ALU.add, op1=ALU.mult).then_inc(k.f.weight, 1)


def fp8_vector(dve, k):
    f = k.f
    y, words = k.y[:, :, :], k.logit[:, :, :, :].rearrange("p a h n -> p (a h n)").rearrange("p (t n) -> p t n", n=P)
    wide = (lambda c: c[:, :, None].broadcast_to([P, TILES, P]))
    dve.wait_ge(k.fresh.normed, PHANTOM + 2 * TILES)
    link(dve, k, dve.tensor_reduce(k.f_scale[:, :], y, AX.X, ALU.max, apply_absolute_value=True))
    link(dve, k, dve.tensor_scalar(k.f_scale[:, :], k.f_scale[:, :], 1e-12, 1.0 / 448.0, ALU.max, ALU.mult))
    link(dve, k, dve.reciprocal(k.f_rscale[:, :], k.f_scale[:, :]))
    link(dve, k, dve.tensor_tensor(y, y, wide(k.f_rscale), ALU.mult))
    link(dve, k, dve.tensor_scalar(words.bitcast(mybir.dt.int32), y.bitcast(mybir.dt.int32), 0x7F800000, None,
                                   ALU.bitwise_and))
    link(dve, k, dve.tensor_scalar(words, words, 2.0 ** -6, 1.5 * 2.0 ** 20, ALU.max, ALU.mult))
    link(dve, k, dve.tensor_tensor(y, y, words, ALU.add))
    dve.tensor_tensor(k.f_q[:, :, :], y, words, ALU.subtract).then_inc(f.quantised, 1)
    link(dve, k, dve.tensor_tensor(k.x[:, :, :], k.x[:, :, :], k.f_bias[:, None, :].broadcast_to([P, TILES, P]),
                                   ALU.add))
    link(dve, k, dve.tensor_scalar(k.f_scale[:, :], k.f_scale[:, :], k.f_ws[:, 0:1], None, ALU.mult))


def fp8_add_vector(dve, k, tiles):
    for t in range(TILES)[tiles]:
        w = k.w1 if t < 8 else k.w2
        if t % 8 == 0:
            dve.wait_ge(k.f.product, t // 8 + 1)
        last = dve.scalar_tensor_tensor(out=k.x[:, t, :], in0=w[:, (t % 8) * P:(t % 8 + 1) * P],
                                        scalar=k.f_scale[:, t:t + 1], in1=k.x[:, t, :], op0=ALU.mult, op1=ALU.add)
    if t < TILES - 1:
        link(dve, k, last)
    else:
        last.then_inc(k.f.done, 1)
        dve.wait_ge(k.f.done, 1)


def fp8_tensor(pe, k):
    f, turned = k.f, k.w0[:, :].bitcast(BF16)
    pe.wait_ge(f.quantised, 1)
    pe.wait_ge(f.weight, 1)
    for t in range(TILES):
        mm = pe.transpose(turned[:, t * P:(t + 1) * P], k.f_q[:, t, :], k.ident16[:, :])
        if t % 8 == 7:
            mm.then_inc(f.turned, 1)
    for t in range(TILES):
        if t % 8 == 0:
            pe.wait_ge(f.qT, t // 8 + 1)
        w = k.w1 if t < 8 else k.w2
        mm = pe.matmul(w[:, (t % 8) * P:(t % 8 + 1) * P], k.f_qT[:, t, :], k.f_w[:, :], start=True, stop=True)
        if t % 8 == 7:
            mm.then_inc(f.product, 1)


def fp8_scalar(act, k):
    f, turned = k.f, k.w0[:, :].bitcast(BF16)
    for c in range(2):
        act.wait_ge(f.turned, c + 1)
        act.copy(k.f_qT[:, 8 * c:8 * c + 8, :], turned[:, 1024 * c:1024 * c + 1024]).then_inc(f.qT, 1)



def experts_prelude_tensor(pe, k, e, similar):
    def turn(q):
        for j in range(4):
            mm = pe.transpose(k.pt[:, j * P:(j + 1) * P], k.y[:, 4 * q + j, :], k.ident[:, :])
        mm.then_inc(e.turned, 1)

    pe.wait_ge(k.fresh.normed, PHANTOM + (4 if similar else 3) * TILES)
    turn(0)
    for q in range(QUADS):
        pe.wait_ge(e.xnT, q + 1)
        if q + 1 < QUADS:
            turn(q + 1)
        if similar:
            w = (k.w0, k.w1)[q // 2]
            pe.matmul(w[:, 512 * (q % 2):512 * (q % 2) + 512], k.m_wp[:, :], k.m_xT[:, q, :],
                      start=True, stop=True).then_inc(e.raw, 1)
        else:
            for j in range(4):
                t = 4 * q + j
                mm = pe.matmul(k.py[:, 8 * t:8 * t + 8], k.m_xT[:, q, j * P:(j + 1) * P], k.m_wr[:, :],
                               start=True, stop=True)
    if similar:
        pe.wait_ge(e.sim_scaled, 1)
        pe.transpose(k.pt[:, 0:8], k.m_sim[:, :], k.ident[0:8, 0:8]).then_inc(e.sim_turned, 1)
        pe.wait_ge(e.sim_T, 1)
        for t in range(TILES):
            if t % 4 == 0:
                pe.wait_ge(e.projT, t // 4 + 1)
                pe.wait_ge(e.squares, t // 4 + 1)
            pe.matmul(k.py[:, 8 * t:8 * t + 8], k.m_projT[:, t * P:(t + 1) * P], k.m_wr[:, :], start=True, stop=True)
            mm = pe.matmul(k.py[:, P + t:P + t + 1], k.m_sq[:, t * P:(t + 1) * P], k.onescol[:, :],
                           start=True, stop=True)
    mm.then_inc(e.logits, 1)


def experts_tensor(pe, k, e, ne):
    bank = (lambda i: k.w2[:, 512 * (i % 2):512 * (i % 2) + 512])

    def quad(q):
        G = (lambda i: q * ne + (e.first + i))

        def hidden(i):
            for c in range(4):
                w = (k.w0, k.w1)[c // 2]
                pe.wait_ge(e.hid_ready, 4 * G(i) + (c - 3))
                pe.matmul(w[:, 512 * (c % 2):512 * (c % 2) + 512], k.m_fc[:, i, c * P:(c + 1) * P],
                          k.m_xT[:, bass.ds(q, 1), :].rearrange("p a n -> p (a n)"),
                          start=True, stop=True).then_inc(e.hid_psum, 1)

        def output(i):
            pe.wait_ge(e.hid_ready, 4 * G(i) + 4)
            pe.wait_ge(e.scaled, slot_before(G(i), i, ne))
            for j in range(4):
                for c in range(4):
                    mm = pe.matmul(bank(i)[:, j * P:(j + 1) * P], k.m_hid[i % 2][:, c, j * P:(j + 1) * P],
                                   k.m_proj[:, i, c, :], start=(c == 0), stop=(c == 3))
            mm.then_inc(e.out_psum, 1)

        for i in range(ne):
            hidden(i)
            if i:
                output(i - 1)
        output(ne - 1)

    with pe.Fori(0, QUADS) as q:
        quad(q)


def slot_before(G, i, ne):
    return G if i == 0 and ne % 2 else G - 1


def experts_bias_tensor(pe, k, e, ne):
    pe.wait_ge(e.gates, 1)
    for t in range(TILES):
        w = k.w0 if t < 8 else k.w1
        mm = pe.transpose(w[0:ne, (t % 8) * P:(t % 8 + 1) * P], k.m_gate[:, t, 0:ne], k.ident[:, :])
        if t % 8 == 7:
            mm.then_inc(e.gate_turned, 1)
    for t in range(TILES):
        if t % 8 == 0:
            pe.wait_ge(e.gateT, t // 8 + 1)
            if t == 0:
                pe.wait_ge(e.scaled, e.first + ne * QUADS)
        w = k.w2 if t < 8 else k.w0
        mm = pe.matmul(w[:, (t % 8) * P:(t % 8 + 1) * P], k.m_gateT[0:ne, t * P:(t + 1) * P], k.m_brow[0:ne, :],
                       start=True, stop=True)
        if t % 8 == 7:
            mm.then_inc(e.bias_psum, 1)


def experts_scalar(act, k, e, ne, similar, gelu):
    for q in range(QUADS):
        act.wait_ge(e.turned, q + 1)
        act.copy(k.m_xT[:, q, :], k.pt[:, :]).then_inc(e.xnT, 1)
        if similar:
            w = (k.w0, k.w1)[q // 2][:, 512 * (q % 2):512 * (q % 2) + 512]
            act.wait_ge(e.raw, q + 1)
            act.copy(k.m_projT[:, 512 * q:512 * q + 512], w).then_inc(e.projT, 1)
            act.activation(k.m_sq[:, 512 * q:512 * q + 512], w, ACT.Square).then_inc(e.squares, 1)
    if similar:
        act.wait_ge(e.sim_turned, 1)
        act.copy(k.m_wr[:, :], k.pt[:, 0:8]).then_inc(e.sim_T, 1)
    act.wait_ge(e.below, 1)
    act.activation(k.m_exp[:, :, :], k.m_exp[:, :, :], ACT.Exp).then_inc(e.exp, 1)

    with act.Fori(0, QUADS) as q:
        for i in range(ne):
            G = q * ne + (e.first + i)
            for c in range(4):
                w = (k.w0, k.w1)[c // 2]
                act.wait_ge(e.hid_psum, 4 * G + (c + 1))
                if c == 0:
                    act.wait_ge(e.out_psum, slot_before(G, i, ne))
                act.activation(k.m_hid[i % 2][:, c, :], w[:, 512 * (c % 2):512 * (c % 2) + 512], gelu,
                               bias=k.m_bfc[:, i, c:c + 1]).then_inc(e.hid_ready, 1)
    for c in range(2):
        act.wait_ge(e.gate_turned, c + 1)
        act.copy(k.m_gateT[0:ne, 1024 * c:1024 * c + 1024], (k.w0, k.w1)[c][0:ne, :]).then_inc(e.gateT, 1)


def similar_vector(dve, k, e):
    dve.wait_ge(e.loaded, 16 * EXPERT3_LOADS)
    link(dve, k, dve.tensor_tensor(k.m_simsq[:, :], k.m_sim[:, :], k.m_sim[:, :], ALU.mult))
    dve.reciprocal(k.m_rtemp[:, :], k.m_temp[:, :]).then_inc(e.cooled, 1)
    dve.tensor_reduce(k.m_simn[:, :], k.m_simsq[:, :], AX.X, ALU.add).then_inc(e.sim_norm2, 1)
    dve.wait_ge(e.sim_rnorm, 1)
    dve.tensor_scalar(k.m_sim[:, :], k.m_sim[:, :], k.m_simn[:, 0:1], None, ALU.mult).then_inc(e.sim_scaled, 1)


def gates_vector(dve, k, e, similar):
    lg, wide = k.m_logit[:, :, :], [P, TILES, 8]
    dve.wait_ge(e.logits, 1)
    raw = k.py[:, 0:P].rearrange("p (t e) -> p t e", e=8)
    if similar:
        dve.tensor_copy(k.m_norm2[:, :], k.py[:, P:P + TILES]).then_inc(e.norm2, 1)
        dve.wait_ge(e.rnorm, 1)
        link(dve, k, dve.tensor_tensor(lg, raw, k.m_norm2[:, :, None].broadcast_to(wide), ALU.mult))
        dve.wait_ge(e.cooled, 1)
        link(dve, k, dve.tensor_scalar(lg, lg, k.m_rtemp[:, 0:1], None, ALU.mult))
    else:
        link(dve, k, dve.tensor_copy(lg, raw))
    link(dve, k, dve.tensor_reduce(k.m_top[:, :], lg, AX.X, ALU.max))
    dve.tensor_tensor(k.m_exp[:, :, :], lg, k.m_top[:, :, None].broadcast_to(wide), ALU.subtract).then_inc(e.below, 1)
    pairs = [P, TILES, 8, 8]
    split = (lambda b: b.rearrange("p t (e j) -> p t e j", e=8))
    link(dve, k, dve.tensor_tensor(split(k.m_greater), lg[:, :, None, :].broadcast_to(pairs), lg[:, :, :, None].broadcast_to(pairs),
                                   ALU.is_gt))
    link(dve, k, dve.tensor_tensor(split(k.m_equal), lg[:, :, None, :].broadcast_to(pairs), lg[:, :, :, None].broadcast_to(pairs),
                                   ALU.is_equal))
    link(dve, k, dve.tensor_tensor(k.m_equal, k.m_equal, k.m_tri[:, None, :].broadcast_to([P, TILES, SEQ]),
                                   ALU.mult))
    link(dve, k, dve.tensor_tensor(k.m_equal, k.m_equal, k.m_greater, ALU.add))
    link(dve, k, dve.tensor_reduce(k.m_rank[:, :, :], split(k.m_equal), AX.X, ALU.add))
    dve.wait_ge(e.exp, 1)
    link(dve, k, dve.scalar_tensor_tensor(out=k.m_exp[:, :, :], in0=k.m_rank[:, :, :], scalar=2.0, in1=k.m_exp[:, :, :],
                                          op0=ALU.is_lt, op1=ALU.mult))
    link(dve, k, dve.tensor_reduce(k.m_top[:, :], k.m_exp[:, :, :], AX.X, ALU.add))
    link(dve, k, dve.reciprocal(k.m_top[:, :], k.m_top[:, :]))
    dve.tensor_tensor(k.m_gate[:, :, 0:8], k.m_exp[:, :, :], k.m_top[:, :, None].broadcast_to(wide),
                      ALU.mult).then_inc(e.gates, 1)
    dve.wait_ge(e.gates, 1)


def experts_vector(dve, k, e, ne, similar):
    if similar:
        similar_vector(dve, k, e)
    gates_vector(dve, k, e, similar)
    with dve.Fori(0, QUADS) as q:
        for i in range(ne):
            G = q * ne + (e.first + i)
            bank = k.w2[:, 512 * (i % 2):512 * (i % 2) + 512].rearrange("p (j n) -> p j n", j=4)
            dve.wait_ge(e.out_psum, G + 1)
            dve.wait_ge(e.added, slot_before(G, i, ne))
            dve.tensor_tensor(k.m_scaled[:, i % 2, :, :], bank,
                              k.m_gate[:, bass.ds(q * 4, 4), i:i + 1].broadcast_to([P, 4, P]),
                              ALU.mult).then_inc(e.scaled, 1)
    dve.wait_ge(e.added, e.first + ne * QUADS)
    for c in range(2):
        dve.wait_ge(e.bias_psum, c + 1)
        rows = k.x[:, 8 * c:8 * c + 8, :].rearrange("p t n -> p (t n)")
        dve.tensor_tensor(rows, rows, (k.w2, k.w0)[c][:, :], ALU.add).then_inc(e.done, 1)
    dve.wait_ge(e.done, 2)


def experts_gpsimd(pool, k, e, ne, similar):
    if similar:
        pool.wait_ge(e.sim_norm2, 1)
        pool.tensor_scalar(k.m_simn[:, :], k.m_simn[:, :], 1e-24, None, ALU.max).then_inc(e.sim_floor, 1)
        pool.wait_ge(e.sim_floor, 1)
        pool.tensor_tensor(k.m_simn[:, :], k.m_simn[:, :], k.power[0:8, 0:1], ALU.pow).then_inc(e.sim_rnorm, 1)
        pool.wait_ge(e.norm2, 1)
        pool.tensor_scalar(k.m_norm2[:, :], k.m_norm2[:, :], 1e-24, None, ALU.max).then_inc(e.floor, 1)
        pool.wait_ge(e.floor, 1)
        pool.tensor_tensor(k.m_norm2[:, :], k.m_norm2[:, :], k.power[:, :], ALU.pow).then_inc(e.rnorm, 1)
    with pool.Fori(0, QUADS) as q:
        for i in range(ne):
            G = q * ne + (e.first + i)
            rows = k.x[:, bass.ds(q * 4, 4), :]
            wait_apart(pool, k, e.scaled, G + 1)
            pool.wait_ge(e.added, G)
            pool.tensor_tensor(rows, rows, k.m_scaled[:, i % 2, :, :], ALU.add).then_inc(e.added, 1)



def urgent_loads(k, a):
    x = a["x"].rearrange("(t p) d -> p t d", p=P)
    return [
        (k.a_ly[:, :], a["a_ly"]), (k.a_lo[:, :], a["a_lo"]), (k.a_lx[:, :], a["a_lx"]), (k.a_tx[:, :, :], a["a_tx"]),
        (k.a_mask[0:SEQ, :], a["a_mask"]), (k.a_mask[SEQ:P, :], a["a_mask"]), (k.x[:, 2:TILES, :], x[:, 2:TILES, :]),
        (k.a_to0[:, :], a["a_to0"]), (k.a_ty[:, :, :], a["a_ty"]), (k.a_to1[:, :], a["a_to1"]),
    ]


def later_loads(k, a):
    return [
        (k.f_bytes[:, :], a["f_w"]), (k.s_w[:, :, :, :], a["s_w"]),
        (k.band[:, :], a["band"]), (k.rope[:, :], a["rope"]), (k.shift[:, :], a["shift"]),
        (k.s_cols[:, :, :], a["s_cols"]), (k.s_bo[:, :, :], a["s_bo"]),
        (k.member[:, :], a["member"]), (k.m_tri[:, :], a["m_tri"]),
        (k.f_ws[:, :], a["f_ws"].partition_broadcast(P)),
        (k.f_bias[:, :], a["f_bias"].partition_broadcast(P)),
    ]


N_URGENT, N_LATER = 10, 11

B_LOADS, C_LOADS = 3, 3


def load_local(sp, k, a, d):
    row = (lambda x: x[d]) if isinstance(d, int) else (lambda x: x[bass.ds(d, 1)].rearrange("a p n -> p (a n)"))
    sp.dma_start(k.b_wqkv[:, :], row(a["b_wqkv"])).then_inc(k.b_loaded, 16)
    sp.dma_start(k.b_wo[:, :, :].rearrange("p h n -> p (h n)"), row(a["b_wo"])).then_inc(k.b_loaded, 16)
    sp.dma_start(k.b_scales[:, :], row(a["b_scales"]).partition_broadcast(P)).then_inc(k.b_loaded, 16)


def load_gated(sp, k, a, d):
    row = (lambda x: x[d]) if isinstance(d, int) else (lambda x: x[bass.ds(d, 1)].rearrange("a p n -> p (a n)"))
    sp.dma_start(k.c_w1[:, :], row(a["c_w1"])).then_inc(k.c_loaded, 16)
    sp.dma_start(k.c_w2[:, :, :].rearrange("p c n -> p (c n)"), row(a["c_w2"])).then_inc(k.c_loaded, 16)
    sp.dma_start(k.c_cols[:, :], row(a["c_cols"])).then_inc(k.c_loaded, 16)


def layers(eng, run):
    with eng.Fori(0, DEPTH) as d:
        run(d * TILES + (PHANTOM + TILES), d * QUADS + PHANTOM)


def small_ctx_first(sp, k, a, n):
    before = (k.v_psum, PHANTOM + TILES) if n == 0 else (k.d.v_psum, PHANTOM + TILES * n)
    for s in range(2):
        sp.wait_ge(*before)
        sp.dma_start(k.ctxT[:, s, :], a["ctxT"][s, :, :]).then_inc(k.ctx_loaded[s], 16)


def small_ctx(sp, k, a, n):
    with sp.Fori(2, TILES - 1, 2) as t:
        for s in range(2):
            sp.wait_ge(k.d.v_psum, t + s + (PHANTOM + TILES * n - 1))
            sp.dma_start(k.ctxT[:, s, :], a["ctxT"][bass.ds(t + s, 1), :, :].rearrange("a p n -> p (a n)")
                         ).then_inc(k.ctx_loaded[s], 16)


EXPERT2_LOADS, EXPERT3_LOADS = 5, 7


def load_experts(sp, k, a, n, e, ne):
    pairs = [(k.m_fc[:, 0:ne, :], a[f"m{n}_fc"]), (k.m_proj[:, 0:ne, :, :], a[f"m{n}_proj"]),
             (k.m_bfc[:, 0:ne, :], a[f"m{n}_bfc"]), (k.m_brow[0:ne, :], a[f"m{n}_brow"])]
    if n == 2:
        pairs += [(k.m_wr[:, :], a["m2_wr"])]
    else:
        pairs += [(k.m_wp[:, :], a["m3_wp"]), (k.m_sim[:, :], a["m3_sim"]),
                  (k.m_temp[:, :], a["m3_temp"].partition_broadcast(P))]
    for dst, src in pairs:
        sp.dma_start(dst, src).then_inc(e.loaded, 16)


def sync_program(nc, sp, k, a, out):
    first = PHANTOM
    sp.dma_start(k.x[:, 0:2, :], a["x"][0:2 * P, :].rearrange("(t p) d -> p t d", p=P)).then_inc(k.x_head, 16)
    ctx = a["ctxT"]
    for i, (dst, src) in enumerate(urgent_loads(k, a)):
        sp.dma_start(dst, src).then_inc(k.loaded, 16)
        if i < 2:
            sp.dma_start(k.ctxT[:, i, :], ctx[i, :, :]).then_inc(k.ctx_loaded[i], 16)
    for dst, src in later_loads(k, a):
        sp.dma_start(dst, src).then_inc(k.loaded_later, 16)
    load_local(sp, k, a, 0)
    load_gated(sp, k, a, 0)
    with sp.Fori(2, TILES - 1, 2) as t:
        for s in range(2):
            sp.wait_ge(k.v_psum, t + s + first - 1)
            sp.dma_start(k.ctxT[:, s, :], ctx[bass.ds(t + s, 1), :, :].rearrange("a p n -> p (a n)")
                         ).then_inc(k.ctx_loaded[s], 16)
    sp.wait_ge(k.updated, PHANTOM + TILES)
    load_experts(sp, k, a, 2, k.e[0], 9)
    small_ctx_first(sp, k, a, 0)
    with sp.Fori(1, DEPTH) as d:
        sp.wait_ge(k.updated, d * TILES + (PHANTOM + TILES))
        load_local(sp, k, a, d)
        sp.wait_ge(k.y_done, d * QUADS + PHANTOM)
        load_gated(sp, k, a, d)
    for n in range(2):
        small_ctx(sp, k, a, n)
        small_ctx_first(sp, k, a, n + 1)
    sp.wait_ge(k.e[0].done, 2)
    load_experts(sp, k, a, 3, k.e[1], 8)
    small_ctx(sp, k, a, 2)
    sp.wait_ge(k.e[1].done, 2)
    sp.dma_start(out.rearrange("(t p) d -> p t d", p=P), k.x[:, :, :]).then_inc(k.stored, 16)
    sp.wait_ge(k.stored, 16)


def tensor_program(nc, pe, k):
    pe.wait_ge(k.consts, 5)
    cross0_tensor(pe, k, PHANTOM)

    def run(first, qfirst):
        quad = GatedTensor(pe, k, first, qfirst)
        local_tensor(pe, k, first, quad)
        quad.rest()
    layers(pe, run)
    pe.wait_ge(k.y_done, PHANTOM + DEPTH * QUADS)
    small_tensor(pe, k, 0)
    fp8_tensor(pe, k)
    small_tensor(pe, k, 1, k.f.done)
    experts2, experts3 = k.e
    pe.wait_ge(experts2.loaded, 16 * EXPERT2_LOADS)
    pe.wait_ge(k.d.updated, PHANTOM + 2 * TILES)
    experts_prelude_tensor(pe, k, experts2, False)
    experts_tensor(pe, k, experts2, 9)
    experts_bias_tensor(pe, k, experts2, 9)
    pe.wait_ge(experts2.done, 2)
    pe.wait_ge(k.quant.done, 1)
    small_tensor(pe, k, 2)
    pe.wait_ge(experts3.loaded, 16 * EXPERT3_LOADS)
    pe.wait_ge(k.d.updated, PHANTOM + 3 * TILES)
    experts_prelude_tensor(pe, k, experts3, True)
    experts_tensor(pe, k, experts3, 8)
    experts_bias_tensor(pe, k, experts3, 8)


def scalar_program(nc, act, k):
    act.wait_ge(k.consts, 5)
    cross0_scalar(act, k, PHANTOM)

    def run(first, qfirst):
        quad = GatedScalar(act, k, first, qfirst)
        local_scalar(act, k, first, qfirst, quad)
        quad.rest()
    layers(act, run)
    small_scalar(act, k, 0, 8 ** -0.5)
    fp8_scalar(act, k)
    small_scalar(act, k, 1, 1.0)
    experts_scalar(act, k, k.e[0], 9, False, ACT.Gelu_apprx_tanh)
    small_scalar(act, k, 2, 8 ** -0.5)
    experts_scalar(act, k, k.e[1], 8, True, ACT.Gelu)


def vector_program(nc, dve, k):
    dve.memset(k.ones[:, :], 1.0).then_inc(k.consts, 1)
    dve.memset(k.sT[:, :, :], 0.0).then_inc(k.consts, 1)
    dve.memset(k.s_v[:, :, :, :, :, :], 0.0)
    dve.memset(k.hid[64:P, 2, :], 1.0)
    dve.memset(k.m_gate[:, :, 8:9], 1.0)
    dve.memset(k.onescol[:, :], 1.0)
    dve.memset(k.ones4[:, :], 1.0).then_inc(k.consts, 1)
    dve.wait_ge(k.x_head, 16)
    cross0_vector(dve, k, PHANTOM)
    dve.wait_ge(k.updated, PHANTOM + TILES)

    def run(first, qfirst):
        quad = GatedVector(dve, k, first, qfirst)
        local_vector(dve, k, first, quad)
        quad.rest()
    layers(dve, run)
    dve.wait_ge(k.y_done, PHANTOM + DEPTH * QUADS)

    def add_y(tiles):
        link(dve, k, dve.tensor_tensor(k.x[:, tiles, :], k.x[:, tiles, :], k.y[:, tiles, :], ALU.add))
    small_vector(dve, k, 0, add_y)
    dve.wait_ge(k.d.updated, PHANTOM + TILES)
    fp8_vector(dve, k)
    small_vector(dve, k, 1, lambda tiles: fp8_add_vector(dve, k, tiles))
    dve.wait_ge(k.d.updated, PHANTOM + 2 * TILES)
    experts_vector(dve, k, k.e[0], 9, False)
    small_vector(dve, k, 2)
    dve.wait_ge(k.d.updated, PHANTOM + 3 * TILES)
    experts_vector(dve, k, k.e[1], 8, True)


def gpsimd_program(nc, pool, k):
    pool.memset(k.ident[:, :], 0.0).then_inc(k.powers, 1)
    pool.memset(k.power[:, :], -0.5).then_inc(k.powers, 1)
    pool.memset(k.eps[:, :], EPS).then_inc(k.powers, 1)
    pool.wait_ge(k.powers, 3)
    pool.affine_select(out=k.ident[:, :], in_=k.ident[:, :], compare_op=ALU.not_equal, fill=1.0, base=0,
                       pattern=[[-1, P]], channel_multiplier=1).then_inc(k.consts, 1)
    pool.wait_ge(k.consts, 4)
    pool.tensor_copy(k.ident16[:, :], k.ident[:, :]).then_inc(k.consts, 1)
    cross0_gpsimd(pool, k, PHANTOM)

    def run(first, qfirst):
        quad = GatedGpsimd(pool, k, qfirst)
        local_gpsimd(pool, k, first, quad)
        quad.rest()
    layers(pool, run)
    small_gpsimd(pool, k, 0)
    small_gpsimd(pool, k, 1)
    experts_gpsimd(pool, k, k.e[0], 9, False)
    small_gpsimd(pool, k, 2)
    experts_gpsimd(pool, k, k.e[1], 8, True)



def tables():
    f = np.float32
    half = np.arange(0, HD, 2, dtype=f)
    t = np.arange(SEQ, dtype=f)
    angle = t[:, None] * (f(1.0) / f(10000.0) ** (half / f(HD)))[None, :]
    base = (half + f(0.4 * HD)) / f(1.4 * HD)
    grow = base[None, :] ** ((t - SEQ // 2) / (WINDOW // 2))[:, None]
    cos, sin = np.cos(angle), np.sin(angle)
    rope = np.concatenate([cos * grow, cos * grow, -sin * grow, sin * grow,
                           cos / grow, cos / grow, -sin / grow, sin / grow], axis=1).astype(f)
    i, j = np.arange(SEQ)[:, None], np.arange(SEQ)[None, :]
    band = np.where((i < j) | (i > j + WINDOW), f(-1e30), f(0)).astype(f)
    shift = np.eye(P, k=1, dtype=f)
    shift[SEQ - 1, SEQ] = 0
    member = (np.arange(P)[:, None] % 64 // 8 == np.arange(8)[None, :]).astype(f)
    lower = np.tile(np.tril(np.ones((8, 8), f), -1).reshape(1, 64), (P, 1))
    return {"m_tri": lower, "member": member, "rope": np.tile(rope, (2, 1)), "band": np.tile(band, (2, 1)), "shift": shift}


def layout(i):
    n = {name: np.asarray(v) for name, v in i.items()}
    a = {}
    a["x"] = n["x"].reshape(TILES * P, P)
    a["ctxT"] = n["ctx_1024"].reshape(TILES, P, P).transpose(0, 2, 1)
    a["a_mask"] = n["mask_SxS2_ff0"].T
    a["a_ly"] = n["L0_xattn_Ly"].transpose(1, 0, 2).reshape(P, 1024)
    a["a_lx"] = n["L0_xattn_Lx"].transpose(1, 0, 2).reshape(P, 1024)
    a["a_tx"] = n["L0_xattn_Tx"].reshape(PAIRS, 2, P, HD).transpose(2, 1, 0, 3).reshape(P, 2, 512)
    a["a_ty"] = n["L0_xattn_Ty"].reshape(PAIRS, 2, P, HD).transpose(1, 3, 0, 2).reshape(P, PAIRS, P)
    a["a_lo"] = n["L0_xattn_Lo"].reshape(PAIRS, P).T
    a["a_to0"] = n["L0_xattn_To0"].reshape(PAIRS, P).T
    a["a_to1"] = n["L0_xattn_To1"].reshape(1, P)
    wqkv = n["L0_ffn_Wqkv"].reshape(DEPTH, P, 3, PAIRS, 2, HD)
    v_even_first = wqkv[:, :, 2].transpose(0, 1, 3, 2, 4).reshape(DEPTH, P, 1024)
    a["b_wqkv"] = np.concatenate([n["L0_ffn_Wqkv"][:, :, :2048], v_even_first], axis=2)
    a["b_wo"] = n["L0_ffn_Wo"].reshape(DEPTH, PAIRS, P, P).transpose(0, 2, 1, 3).reshape(DEPTH, P, 1024)
    halves = [np.roll(n[s], r, axis=1) for s in ("L0_ffn_q_scale", "L0_ffn_k_scale") for r in (0, HD // 2)]
    a["b_scales"] = np.concatenate(halves, axis=1).reshape(DEPTH, 1, 4 * HD)
    a["c_w1"] = n["L0_ffn_W1"]
    w2 = np.zeros((DEPTH, 3 * P, P), np.float32)
    w2[:, :HID], w2[:, HID] = n["L0_ffn_W2"], n["L0_ffn_b2"]
    a["c_w2"] = w2.reshape(DEPTH, 3, P, P).transpose(0, 2, 1, 3).reshape(DEPTH, P, 3 * P)
    cols = np.zeros((DEPTH, 8, P), np.float32)
    cols[:, 0], cols[:, 1] = n["L0_ffn_ln_g"], n["L0_ffn_ln_b"]
    for c, (at, m) in enumerate(CHUNKS):
        cols[:, 2 + c, :m] = n["L0_ffn_b1"][:, at:at + m]
        cols[:, 5 + c, :m] = n["L0_ffn_b1"][:, HID + at:HID + at + m]
    a["c_cols"] = cols.transpose(0, 2, 1)
    heads_apart = (lambda w: w.reshape(P, PAIRS, 2, 8).transpose(0, 2, 1, 3).reshape(P, P))
    per_stage = [[n["L1_xattn_w_q"], n["L1_xattn_w_k"], n["L1_xattn_w_v"], n["L1_xattn_w_out"]],
                 [n[f"L2_xattn_W{c}"].T for c in "qkvo"], [n[f"L3_xattn_W{c}"].T for c in "qkvo"]]
    a["s_w"] = np.stack([np.stack([wq, wk, heads_apart(wv), wo], 1) for wq, wk, wv, wo in per_stage], 1)
    zero = np.zeros(P, np.float32)
    a["s_cols"] = np.stack([np.stack(c, 1) for c in (
        [n["L1_xattn_b_q"], n["L1_xattn_b_k"], n["L1_xattn_b_v"]], [zero] * 3,
        [n["L3_xattn_bq"], n["L3_xattn_bk"], n["L3_xattn_bv"]])], 1)
    a["s_bo"] = np.stack([n["L1_xattn_b_out"], n["L2_xattn_bo"], n["L3_xattn_bo"]])[None]
    a["f_w"] = n["L1_ffn_weight"].view(np.uint8).T
    a["f_ws"] = n["L1_ffn_weight_scale"].reshape(1, 1)
    a["f_bias"] = n["L1_ffn_bias"].reshape(1, P)
    both = (lambda routed, shared: np.concatenate([routed, shared[None]]))
    layers2 = [both(n["L2_ffn_" + w], n["L2_ffn_" + w + "_s"]) for w in ("Wfc", "bfc", "Wproj", "bproj")]
    layers3 = [n["L3_ffn_" + w] for w in ("W1", "b1", "W2", "b2")]
    for m, (fc, bfc, proj, brow) in ((2, layers2), (3, layers3)):
        a[f"m{m}_fc"] = fc.transpose(1, 0, 2)
        a[f"m{m}_bfc"] = bfc.reshape(-1, 4, P).transpose(2, 0, 1)
        a[f"m{m}_proj"] = proj.reshape(-1, 4, P, P).transpose(2, 0, 1, 3)
        a[f"m{m}_brow"] = brow
    a["m2_wr"] = n["L2_ffn_Wr"]
    a["m3_wp"] = n["L3_ffn_Wp"].T
    a["m3_sim"] = n["L3_ffn_sim_matrix"]
    a["m3_temp"] = n["L3_ffn_temperature"].reshape(1, 1)
    a.update(tables())
    return {name: np.ascontiguousarray(v) for name, v in a.items()}


def kernel(**inputs):
    import concourse.bacc as bacc
    from concourse.bass_utils import run_bass_kernel_spmd

    nc = bacc.Bacc("TRN2", target_bir_lowering=False, num_devices=1)
    arrays = layout(inputs)
    dram = {name: nc.dram_tensor("in_" + name, v.shape, mybir.dt.from_np(v.dtype), kind="ExternalInput").ap()
            for name, v in arrays.items()}
    out = nc.dram_tensor("out", (TILES * P, P), F32, kind="ExternalOutput").ap()
    build(nc, dram, out)
    r = run_bass_kernel_spmd(nc, [{"in_" + name: v for name, v in arrays.items()}], core_ids=[0])
    return r.results[0]["out"].reshape(32, SEQ, P)
```
